# Optimizing a Trainium2 kernel written in Bass

```python
import numpy as np
import jax
import jax.numpy as jnp

def _softmax(x, axis=-1):
    return jax.nn.softmax(x, axis=axis)

def _gelu(x):
    return jax.nn.gelu(x, approximate=True)

def _silu(x):
    return jax.nn.silu(x)

def _sigmoid(x):
    return jax.nn.sigmoid(x)

def _layernorm(x, axis=-1, eps=1e-05):
    m = jnp.mean(x, axis=axis, keepdims=True)
    v = jnp.var(x, axis=axis, keepdims=True)
    return (x - m) / jnp.sqrt(v + eps)

def _scatter_add(tgt, idx, src, axis=0):
    return tgt.at[idx].add(src)

def _segment_sum(src, seg, n):
    return jax.ops.segment_sum(src, seg, n)
kernel_name = 'mk_gps_d2_gnn_r16_65ac3d'

def setup_inputs(seed: int=0):
    np.random.seed(seed)
    _w = jnp.asarray

    def _rec_inputs():
        import jax
        import jax.numpy as jnp
        _gk = jax.random.key(seed)
        x = -0.000364 + 1 * jax.random.normal(jax.random.fold_in(_gk, 1), (1250, 768), jnp.float32)
        _s = jax.random.randint(jax.random.fold_in(_gk, 2), (10000,), 0, 1250, jnp.int32)
        _d = jax.random.randint(jax.random.fold_in(_gk, 3), (10000,), 0, 1250, jnp.int32)
        _loop = jnp.arange(1250, dtype=jnp.int32)
        src = jnp.concatenate([_s, _d, _loop])
        dst = jnp.concatenate([_d, _s, _loop])
        _o = jnp.argsort(dst, stable=True)
        src = src[_o]
        dst = dst[_o]
        return (x, src, dst)
    x, src, dst = _rec_inputs()

    def _L0_gnn_setup():
        import jax, jax.numpy as jnp
        import numpy as np
        N = 1250
        E = 20000
        D = 768
        H = 4
        C = D // H
        NEG_SLOPE = 0.2

        def gat_layer(x, src, dst, W, a_src, a_dst, b):
            h = (x @ W).reshape(-1, H, C)
            as_ = jnp.sum(h * a_src, axis=-1)
            ad_ = jnp.sum(h * a_dst, axis=-1)
            e = jax.nn.leaky_relu(as_[src] + ad_[dst], NEG_SLOPE)
            m = jax.ops.segment_max(e, dst, num_segments=N)
            e = jnp.exp(e - m[dst])
            s = jax.ops.segment_sum(e, dst, num_segments=N)
            alpha = e / s[dst]
            msg = h[src] * alpha[:, :, None]
            out = jax.ops.segment_sum(msg, dst, num_segments=N)
            return out.reshape(-1, H * C) + b
        key = jax.random.key(seed)
        ks = jax.random.split(key, 10)
        x = jax.random.normal(ks[0], (N, D), dtype=jnp.float32)
        edge_index = jax.random.randint(ks[1], (2, E), 0, N, dtype=jnp.int64)
        sc = 0.05
        W1 = jax.random.normal(ks[2], (D, H * C), dtype=jnp.float32) * sc
        a_src1 = jax.random.normal(ks[3], (H, C), dtype=jnp.float32) * sc
        a_dst1 = jax.random.normal(ks[4], (H, C), dtype=jnp.float32) * sc
        b1 = jnp.zeros((H * C,), dtype=jnp.float32)
        W2 = jax.random.normal(ks[5], (H * C, H * C), dtype=jnp.float32) * sc
        a_src2 = jax.random.normal(ks[6], (H, C), dtype=jnp.float32) * sc
        a_dst2 = jax.random.normal(ks[7], (H, C), dtype=jnp.float32) * sc
        b2 = jnp.zeros((H * C,), dtype=jnp.float32)
        return {'x': x, 'edge_index': edge_index, 'W1': W1, 'a_src1': a_src1, 'a_dst1': a_dst1, 'b1': b1, 'W2': W2, 'a_src2': a_src2, 'a_dst2': a_dst2, 'b2': b2}
    _L0_gnn_all = _L0_gnn_setup()
    _L0_gnn_in = {k: v for k, v in _L0_gnn_all.items() if k in ('W1', 'a_src1', 'a_dst1', 'b1', 'W2', 'a_src2', 'a_dst2', 'b2')}
    del _L0_gnn_all

    def _L0_mix_setup():
        import jax, jax.numpy as jnp
        import numpy as np
        EMBED_DIM = 768
        NUM_HEADS = 8
        HEAD_DIM = EMBED_DIM // NUM_HEADS
        NUM_RF = 256
        B, N = (8, 256)
        key = jax.random.key(seed)
        ks = jax.random.split(key, 6)
        x = jax.random.normal(ks[0], (B, N, EMBED_DIM), dtype=jnp.float32)
        s_qkv = 1.0 / np.sqrt(EMBED_DIM)
        qkv_w = jax.random.uniform(ks[1], (3 * EMBED_DIM, EMBED_DIM), minval=-s_qkv, maxval=s_qkv)
        qkv_b = jax.random.uniform(ks[2], (3 * EMBED_DIM,), minval=-s_qkv, maxval=s_qkv)
        proj_w = jax.random.uniform(ks[3], (EMBED_DIM, EMBED_DIM), minval=-s_qkv, maxval=s_qkv)
        proj_b = jax.random.uniform(ks[4], (EMBED_DIM,), minval=-s_qkv, maxval=s_qkv)
        rf = jax.random.normal(ks[5], (NUM_RF, HEAD_DIM), dtype=jnp.float32)
        rf = rf / jnp.linalg.norm(rf, axis=1, keepdims=True)
        return {'x': x, 'qkv_w': qkv_w, 'qkv_b': qkv_b, 'proj_w': proj_w, 'proj_b': proj_b, 'rf': rf}
    _L0_mix_all = _L0_mix_setup()
    _L0_mix_in = {k: v for k, v in _L0_mix_all.items() if k in ('qkv_w', 'qkv_b', 'proj_w', 'proj_b', 'rf')}
    del _L0_mix_all

    def _L0_ffn_setup():
        import jax, jax.numpy as jnp
        import numpy as np
        B, L, D, E, TOP_K = (8, 1024, 768, 4, 2)
        H = 2 * D
        LN_EPS = 1e-05

        def _gelu(v):
            return jax.nn.gelu(v, approximate=False)

        def _mish(v):
            return v * jnp.tanh(jax.nn.softplus(v))
        _ACTS = [_gelu, jax.nn.silu, _mish, _gelu]
        key = jax.random.key(seed)
        ks = jax.random.split(key, 8)
        x = jax.random.normal(ks[0], (B, L, D), dtype=jnp.float32)
        router_w = jax.random.normal(ks[1], (E, D), dtype=jnp.float32) * 0.02
        router_b = jnp.zeros((E,), dtype=jnp.float32)
        w1 = jax.random.normal(ks[2], (E, D, H), dtype=jnp.float32) * (1.0 / np.sqrt(D))
        b1 = jax.random.normal(ks[3], (E, H), dtype=jnp.float32) * 0.01
        w2 = jax.random.normal(ks[4], (E, H, D), dtype=jnp.float32) * (1.0 / np.sqrt(H))
        b2 = jax.random.normal(ks[5], (E, D), dtype=jnp.float32) * 0.01
        ln_g = jnp.ones((D,), dtype=jnp.float32)
        ln_b = jnp.zeros((D,), dtype=jnp.float32)
        return {'x': x, 'router_w': router_w, 'router_b': router_b, 'w1': w1, 'b1': b1, 'w2': w2, 'b2': b2, 'ln_g': ln_g, 'ln_b': ln_b}
    _L0_ffn_all = _L0_ffn_setup()
    _L0_ffn_in = {k: v for k, v in _L0_ffn_all.items() if k in ('router_w', 'router_b', 'w1', 'b1', 'w2', 'b2', 'ln_g', 'ln_b')}
    del _L0_ffn_all

    def _L1_gnn_setup():
        import jax, jax.numpy as jnp
        import numpy as np
        NEG_SLOPE = 0.2

        def _gat_layer(x, W, a_src, a_dst, b, src, dst, n_nodes):
            h = x @ W
            e_src = h @ a_src
            e_dst = h @ a_dst
            e = jax.nn.leaky_relu(e_src[src] + e_dst[dst], NEG_SLOPE)
            m = jax.ops.segment_max(e, dst, num_segments=n_nodes)
            w = jnp.exp(e - m[dst])
            z = jax.ops.segment_sum(w, dst, num_segments=n_nodes)
            alpha = w / z[dst]
            out = jax.ops.segment_sum(h[src] * alpha[:, None], dst, num_segments=n_nodes)
            return out + b
        key = jax.random.key(seed)
        ks = jax.random.split(key, 10)
        N, E, D = (625, 6250, 768)
        scale = 1.0 / np.sqrt(D)
        x = jax.random.normal(ks[0], (N, D), dtype=jnp.float32)
        edge_index = jax.random.randint(ks[1], (2, E), 0, N, dtype=jnp.int32)
        params = {}
        for i, nm in enumerate(['1', '2']):
            params[f'W{nm}'] = jax.random.normal(ks[2 + 4 * i], (D, D), jnp.float32) * scale
            params[f'att_src{nm}'] = jax.random.normal(ks[3 + 4 * i], (D,), jnp.float32) * scale
            params[f'att_dst{nm}'] = jax.random.normal(ks[4 + 4 * i], (D,), jnp.float32) * scale
            params[f'b{nm}'] = jnp.zeros((D,), jnp.float32)
        return {'x': x, 'edge_index': edge_index, **params}
    _L1_gnn_all = _L1_gnn_setup()
    _L1_gnn_in = {k: v for k, v in _L1_gnn_all.items() if k in ('W1', 'att_src1', 'att_dst1', 'b1', 'W2', 'att_src2', 'att_dst2', 'b2')}
    del _L1_gnn_all

    def _L1_mix_setup():
        import jax, jax.numpy as jnp
        import numpy as np
        FEATS = 768
        HEAD = 12

        def _phi(t):
            return jax.nn.elu(t) + 1.0
        key = jax.random.key(seed)
        ks = jax.random.split(key, 9)
        f = FEATS
        s = 1.0 / np.sqrt(f)
        x = jax.random.normal(ks[0], (4, 256, f), dtype=jnp.float32)
        Wq = jax.random.normal(ks[1], (f, f), dtype=jnp.float32) * s
        bq = jax.random.normal(ks[2], (f,), dtype=jnp.float32) * 0.01
        Wk = jax.random.normal(ks[3], (f, f), dtype=jnp.float32) * s
        bk = jax.random.normal(ks[4], (f,), dtype=jnp.float32) * 0.01
        Wv = jax.random.normal(ks[5], (f, f), dtype=jnp.float32) * s
        bv = jax.random.normal(ks[6], (f,), dtype=jnp.float32) * 0.01
        Wo = jax.random.normal(ks[7], (f, f), dtype=jnp.float32) * s
        bo = jax.random.normal(ks[8], (f,), dtype=jnp.float32) * 0.01
        return {'x': x, 'Wq': Wq, 'bq': bq, 'Wk': Wk, 'bk': bk, 'Wv': Wv, 'bv': bv, 'Wo': Wo, 'bo': bo}
    _L1_mix_all = _L1_mix_setup()
    _L1_mix_in = {k: v for k, v in _L1_mix_all.items() if k in ('Wq', 'bq', 'Wk', 'bk', 'Wv', 'bv', 'Wo', 'bo')}
    del _L1_mix_all

    def _L1_ffn_setup():
        import jax, jax.numpy as jnp
        import numpy as np
        DECAY = 0.9
        EPS = 0.01
        TOP_K = 2
        key = jax.random.key(seed)
        k1, k2, k3, k4 = jax.random.split(key, 4)
        B, S, H, I, E = (4, 128, 768, 128, 8)
        return {'hidden_states': jax.random.normal(k1, (B, S, H), jnp.float32), 'router_w': jax.random.normal(k2, (E, H), jnp.float32) * 0.02, 'w1': jax.random.normal(k3, (E, I, H), jnp.float32) * 0.02, 'w2': jax.random.normal(k4, (E, H, I), jnp.float32) * 0.02}
    _L1_ffn_all = _L1_ffn_setup()
    _L1_ffn_in = {k: v for k, v in _L1_ffn_all.items() if k in ('router_w', 'w1', 'w2')}
    del _L1_ffn_all
    return {'x': x, 'src': src, 'dst': dst, 'L0_gnn_W1': _L0_gnn_in['W1'], 'L0_gnn_a_src1': _L0_gnn_in['a_src1'], 'L0_gnn_a_dst1': _L0_gnn_in['a_dst1'], 'L0_gnn_b1': _L0_gnn_in['b1'], 'L0_gnn_W2': _L0_gnn_in['W2'], 'L0_gnn_a_src2': _L0_gnn_in['a_src2'], 'L0_gnn_a_dst2': _L0_gnn_in['a_dst2'], 'L0_gnn_b2': _L0_gnn_in['b2'], 'L0_mix_qkv_w': _L0_mix_in['qkv_w'], 'L0_mix_qkv_b': _L0_mix_in['qkv_b'], 'L0_mix_proj_w': _L0_mix_in['proj_w'], 'L0_mix_proj_b': _L0_mix_in['proj_b'], 'L0_mix_rf': _L0_mix_in['rf'], 'L0_ffn_router_w': _L0_ffn_in['router_w'], 'L0_ffn_router_b': _L0_ffn_in['router_b'], 'L0_ffn_w1': _L0_ffn_in['w1'], 'L0_ffn_b1': _L0_ffn_in['b1'], 'L0_ffn_w2': _L0_ffn_in['w2'], 'L0_ffn_b2': _L0_ffn_in['b2'], 'L0_ffn_ln_g': _L0_ffn_in['ln_g'], 'L0_ffn_ln_b': _L0_ffn_in['ln_b'], 'L1_gnn_W1': _L1_gnn_in['W1'], 'L1_gnn_att_src1': _L1_gnn_in['att_src1'], 'L1_gnn_att_dst1': _L1_gnn_in['att_dst1'], 'L1_gnn_b1': _L1_gnn_in['b1'], 'L1_gnn_W2': _L1_gnn_in['W2'], 'L1_gnn_att_src2': _L1_gnn_in['att_src2'], 'L1_gnn_att_dst2': _L1_gnn_in['att_dst2'], 'L1_gnn_b2': _L1_gnn_in['b2'], 'L1_mix_Wq': _L1_mix_in['Wq'], 'L1_mix_bq': _L1_mix_in['bq'], 'L1_mix_Wk': _L1_mix_in['Wk'], 'L1_mix_bk': _L1_mix_in['bk'], 'L1_mix_Wv': _L1_mix_in['Wv'], 'L1_mix_bv': _L1_mix_in['bv'], 'L1_mix_Wo': _L1_mix_in['Wo'], 'L1_mix_bo': _L1_mix_in['bo'], 'L1_ffn_router_w': _L1_ffn_in['router_w'], 'L1_ffn_w1': _L1_ffn_in['w1'], 'L1_ffn_w2': _L1_ffn_in['w2']}

def reference(x, src, dst, L0_gnn_W1, L0_gnn_a_src1, L0_gnn_a_dst1, L0_gnn_b1, L0_gnn_W2, L0_gnn_a_src2, L0_gnn_a_dst2, L0_gnn_b2, L0_mix_qkv_w, L0_mix_qkv_b, L0_mix_proj_w, L0_mix_proj_b, L0_mix_rf, L0_ffn_router_w, L0_ffn_router_b, L0_ffn_w1, L0_ffn_b1, L0_ffn_w2, L0_ffn_b2, L0_ffn_ln_g, L0_ffn_ln_b, L1_gnn_W1, L1_gnn_att_src1, L1_gnn_att_dst1, L1_gnn_b1, L1_gnn_W2, L1_gnn_att_src2, L1_gnn_att_dst2, L1_gnn_b2, L1_mix_Wq, L1_mix_bq, L1_mix_Wk, L1_mix_bk, L1_mix_Wv, L1_mix_bv, L1_mix_Wo, L1_mix_bo, L1_ffn_router_w, L1_ffn_w1, L1_ffn_w2):
    import jax
    import jax.numpy as jnp

    def _L0_gnn_ref(x, edge_index, W1, a_src1, a_dst1, b1, W2, a_src2, a_dst2, b2):
        import jax, jax.numpy as jnp
        import numpy as np
        N = 1250
        E = 20000
        D = 768
        H = 4
        C = D // H
        NEG_SLOPE = 0.2

        def gat_layer(x, src, dst, W, a_src, a_dst, b):
            h = (x @ W).reshape(-1, H, C)
            as_ = jnp.sum(h * a_src, axis=-1)
            ad_ = jnp.sum(h * a_dst, axis=-1)
            e = jax.nn.leaky_relu(as_[src] + ad_[dst], NEG_SLOPE)
            m = jax.ops.segment_max(e, dst, num_segments=N)
            e = jnp.exp(e - m[dst])
            s = jax.ops.segment_sum(e, dst, num_segments=N)
            alpha = e / s[dst]
            msg = h[src] * alpha[:, :, None]
            out = jax.ops.segment_sum(msg, dst, num_segments=N)
            return out.reshape(-1, H * C) + b
        loop = jnp.arange(N, dtype=edge_index.dtype)
        src = jnp.concatenate([edge_index[0], loop])
        dst = jnp.concatenate([edge_index[1], loop])
        h = gat_layer(x, src, dst, W1, a_src1, a_dst1, b1)
        h = jax.nn.relu(h)
        out = gat_layer(h, src, dst, W2, a_src2, a_dst2, b2)
        return out

    def _L0_mix_ref(x, qkv_w, qkv_b, proj_w, proj_b, rf):
        import jax, jax.numpy as jnp
        import numpy as np
        EMBED_DIM = 768
        NUM_HEADS = 8
        HEAD_DIM = EMBED_DIM // NUM_HEADS
        NUM_RF = 256
        B, N = (8, 256)
        Bn, Nn, C = x.shape
        H, D = (NUM_HEADS, HEAD_DIM)
        qkv = x @ qkv_w.T + qkv_b
        qkv = qkv.reshape(Bn, Nn, 3, H, D).transpose(2, 0, 3, 1, 4)
        q, k, v = (qkv[0], qkv[1], qkv[2])
        scale = D ** (-0.5)
        q = q * scale
        k = k * scale
        q_norm = jnp.sum(q * q, axis=-1, keepdims=True) * 0.5
        k_norm = jnp.sum(k * k, axis=-1, keepdims=True) * 0.5
        phi_q = jnp.exp(jnp.einsum('bhnd,md->bhnm', q, rf) - q_norm)
        phi_k = jnp.exp(jnp.einsum('bhnd,md->bhnm', k, rf) - k_norm)
        kv = jnp.einsum('bhnm,bhnd->bhmd', phi_k, v)
        numerator = jnp.einsum('bhnm,bhmd->bhnd', phi_q, kv)
        k_sum = jnp.sum(phi_k, axis=2)
        denominator = jnp.einsum('bhnm,bhm->bhn', phi_q, k_sum)[..., None]
        attn = numerator / jnp.maximum(denominator, 1e-06)
        out = attn.transpose(0, 2, 1, 3).reshape(Bn, Nn, C)
        return out @ proj_w.T + proj_b

    def _L0_ffn_ref(x, router_w, router_b, w1, b1, w2, b2, ln_g, ln_b):
        import jax, jax.numpy as jnp
        import numpy as np
        B, L, D, E, TOP_K = (8, 1024, 768, 4, 2)
        H = 2 * D
        LN_EPS = 1e-05

        def _gelu(v):
            return jax.nn.gelu(v, approximate=False)

        def _mish(v):
            return v * jnp.tanh(jax.nn.softplus(v))
        _ACTS = [_gelu, jax.nn.silu, _mish, _gelu]
        b, l, d = x.shape
        e = router_w.shape[0]
        pooled = x.mean(axis=1)
        logits = pooled @ router_w.T + router_b
        top_v, top_i = jax.lax.top_k(logits, TOP_K)
        gates_k = jax.nn.softmax(top_v, axis=-1)
        gate = jnp.zeros((b, e), x.dtype).at[jnp.arange(b)[:, None], top_i].add(gates_k)
        h = jnp.einsum('bld,edh->belh', x, w1) + b1[None, :, None, :]
        h = jnp.stack([_ACTS[i](h[:, i]) for i in range(e)], axis=1)
        out = jnp.einsum('belh,ehd->beld', h, w2) + b2[None, :, None, :]
        y = jnp.einsum('be,beld->bld', gate, out) + x
        mu = y.mean(axis=-1, keepdims=True)
        var = ((y - mu) ** 2).mean(axis=-1, keepdims=True)
        return (y - mu) * jax.lax.rsqrt(var + LN_EPS) * ln_g + ln_b

    def _L1_gnn_ref(x, edge_index, W1, att_src1, att_dst1, b1, W2, att_src2, att_dst2, b2):
        import jax, jax.numpy as jnp
        import numpy as np
        NEG_SLOPE = 0.2

        def _gat_layer(x, W, a_src, a_dst, b, src, dst, n_nodes):
            h = x @ W
            e_src = h @ a_src
            e_dst = h @ a_dst
            e = jax.nn.leaky_relu(e_src[src] + e_dst[dst], NEG_SLOPE)
            m = jax.ops.segment_max(e, dst, num_segments=n_nodes)
            w = jnp.exp(e - m[dst])
            z = jax.ops.segment_sum(w, dst, num_segments=n_nodes)
            alpha = w / z[dst]
            out = jax.ops.segment_sum(h[src] * alpha[:, None], dst, num_segments=n_nodes)
            return out + b
        n_nodes = x.shape[0]
        loops = jnp.arange(n_nodes, dtype=edge_index.dtype)
        src = jnp.concatenate([edge_index[0], loops])
        dst = jnp.concatenate([edge_index[1], loops])
        h = _gat_layer(x, W1, att_src1, att_dst1, b1, src, dst, n_nodes)
        h = jax.nn.relu(h)
        out = _gat_layer(h, W2, att_src2, att_dst2, b2, src, dst, n_nodes)
        return out

    def _L1_mix_ref(x, Wq, bq, Wk, bk, Wv, bv, Wo, bo):
        import jax, jax.numpy as jnp
        import numpy as np
        FEATS = 768
        HEAD = 12

        def _phi(t):
            return jax.nn.elu(t) + 1.0
        b, n, f = x.shape
        h = HEAD
        d = f // h

        def heads(t):
            return t.reshape(b, n, h, d).transpose(0, 2, 1, 3)
        q = _phi(heads(x @ Wq + bq))
        k = _phi(heads(x @ Wk + bk))
        v = heads(x @ Wv + bv)
        kv = jnp.einsum('bhnd,bhne->bhde', k, v)
        ksum = k.sum(axis=2)
        z = 1.0 / jnp.einsum('bhld,bhd->bhl', q, ksum)
        num = jnp.einsum('bhld,bhde->bhle', q, kv)
        normed = num * z[..., None]
        out = normed.transpose(0, 2, 1, 3).reshape(b, n, f)
        return out @ Wo + bo

    def _L1_ffn_ref(hidden_states, router_w, w1, w2):
        import jax, jax.numpy as jnp
        import numpy as np
        DECAY = 0.9
        EPS = 0.01
        TOP_K = 2
        B, S, H = hidden_states.shape
        E = router_w.shape[0]
        flat = hidden_states.reshape(B * S, H)
        logits = flat @ router_w.T
        probs = jax.nn.softmax(logits, axis=-1)
        topk_probs, topk_idx = jax.lax.top_k(probs, TOP_K)
        importance = jax.lax.stop_gradient(probs).sum(axis=0)
        running = jnp.ones((E,), dtype=flat.dtype)
        blended = running + (1.0 - DECAY) * (importance - running)
        running = blended + EPS
        balance = running[topk_idx]
        balanced = topk_probs / balance
        balanced = balanced / balanced.sum(axis=-1, keepdims=True)
        h = jnp.einsum('th,eih->tei', flat, w1)
        h = jax.nn.silu(h)
        outs = jnp.einsum('tei,ehi->teh', h, w2)
        sel = jnp.take_along_axis(outs, topk_idx[:, :, None], axis=1)
        combined = (sel * balanced[..., None]).sum(axis=1)
        return combined.reshape(B, S, H)
    edge_index = jnp.stack([src, dst])
    xn = _layernorm(x, axis=-1)
    x = x + _L0_gnn_ref(xn, edge_index, L0_gnn_W1, L0_gnn_a_src1, L0_gnn_a_dst1, L0_gnn_b1, L0_gnn_W2, L0_gnn_a_src2, L0_gnn_a_dst2, L0_gnn_b2) + _L0_mix_ref(xn[None], L0_mix_qkv_w, L0_mix_qkv_b, L0_mix_proj_w, L0_mix_proj_b, L0_mix_rf)[0]
    x = x + _L0_ffn_ref(_layernorm(x, axis=-1)[None], L0_ffn_router_w, L0_ffn_router_b, L0_ffn_w1, L0_ffn_b1, L0_ffn_w2, L0_ffn_b2, L0_ffn_ln_g, L0_ffn_ln_b)[0]
    xn = _layernorm(x, axis=-1)
    x = x + _L1_gnn_ref(xn, edge_index, L1_gnn_W1, L1_gnn_att_src1, L1_gnn_att_dst1, L1_gnn_b1, L1_gnn_W2, L1_gnn_att_src2, L1_gnn_att_dst2, L1_gnn_b2) + _L1_mix_ref(xn[None], L1_mix_Wq, L1_mix_bq, L1_mix_Wk, L1_mix_bk, L1_mix_Wv, L1_mix_bv, L1_mix_Wo, L1_mix_bo)[0]
    x = x + _L1_ffn_ref(_layernorm(x, axis=-1)[None], L1_ffn_router_w, L1_ffn_w1, L1_ffn_w2)[0]
    return x

_drawn_inputs = setup_inputs


def setup_inputs(seed=0):
    import zlib

    import numpy as np

    out = dict(_drawn_inputs(seed))
    spreads = {'L0_gnn_b1': (0.0, 0.1),
     'L0_gnn_b2': (0.0, 0.1),
     'L0_ffn_router_b': (0.0, 0.8),
     'L0_ffn_ln_g': (1.0, 0.2),
     'L0_ffn_ln_b': (0.0, 0.1),
     'L1_gnn_b1': (0.0, 0.269),
     'L1_gnn_b2': (0.0, 0.1)}
    factors = {'L0_gnn_a_dst1': 2.714,
     'L0_gnn_a_src2': 3.235,
     'L0_gnn_a_dst2': 24.373,
     'L0_mix_qkv_w': 5.351,
     'L0_mix_qkv_b': 4.422,
     'L0_mix_proj_w': 3.357,
     'L0_mix_rf': 8.0,
     'L0_ffn_b1': 24.844,
     'L0_ffn_b2': 8.0,
     'L1_gnn_att_dst1': 137.658,
     'L1_gnn_att_src2': 54.425,
     'L1_gnn_att_dst2': 200.0,
     'L1_mix_Wq': 200.0,
     'L1_mix_bq': 200.0,
     'L1_mix_Wk': 200.0,
     'L1_mix_bk': 200.0,
     'L1_mix_bv': 8.0,
     'L1_mix_bo': 8.0,
     'L0_mix_proj_b': 2.885,
     'L0_ffn_router_w': 7.305,
     'L1_ffn_router_w': 2.966,
     'L1_ffn_w1': 2.676,
     'L1_gnn_att_src1': 3.031}
    for name, (base, spread) in spreads.items():
        noise = np.random.default_rng([zlib.crc32(name.encode()), seed]).standard_normal(out[name].shape)
        drawn = base * np.exp(spread * noise) if base else spread * noise
        out[name] = jnp.asarray(drawn.astype(out[name].dtype))
    for name, factor in factors.items():
        out[name] = (out[name] * factor).astype(out[name].dtype)
    return out
```

```python
import concourse.bass as bass
from concourse import mybir
from contextlib import ExitStack

F32 = mybir.dt.float32
BF16 = mybir.dt.bfloat16
U16 = mybir.dt.uint16
I32 = mybir.dt.int32
U32 = mybir.dt.uint32
ALU = mybir.AluOpType
ACT = mybir.ActivationFunctionType
AX = mybir.AxisListType.X

N, D = 1250, 768
T, NT = 125, 10
KD = D // 128
E = 21250
EC = E // T
KEYG = 4
NKEY = (EC + KEYG - 1) // KEYG
CH = [(0, 500), (500, 500), (1000, 250)]
TG = [(0, 4), (4, 4), (8, 2)]
HALF = D // 2
CNT = N * N + T
NEG_BIG = -1.0e30
LN_EPS = 1e-5
SLOPE = 0.2
H0, C0 = 4, 192
MH, MD, RF = 8, 96, 256
HID, HM = 1536, 12
E1, I1 = 8, 128
VBANKS, ABANKS = 5, 3


def front(layer):
    seq = [("asrow", 0)]
    if layer < 2:
        seq.append(("asrow", 1))
    for t in range(NT):
        seq.append(("h", t))
        if layer < 2:
            seq += {2: [("asrow", 2)], 4: [("asrow", 3)]}.get(t, [])
        if layer == 1:
            seq += {7: [("rows", 0), ("step", 0)], 8: [("step", 1)], 9: [("step", 2)]}.get(t, [])
        if layer > 1:
            seq += {3: [("rows", 0)], 5: [("step", 0)], 7: [("step", 1)]}.get(t, [])
    if layer == 0:
        seq.append(("rows", 0))
    return seq


def plan():
    V, A = [], []

    def turned(stage):
        A.extend(("tr", stage, g, k) for g in range(3) for k in range(KD))

    def gat(layer):
        heads = H0 if layer < 2 else 1
        V.append(("sc", layer))

        def rows(h):
            A.extend(("p", layer, h, i, q) for i in range(2) for q in range(3))

        for what, i in front(layer):
            if what == "h":
                A.extend(("h", layer, i, half) for half in range(2))
            elif what == "asrow":
                A.extend(("asrow", layer, i, q) for q in range(3))
            elif what == "rows":
                rows(i)
        if heads > 1:
            for h in range(heads - 1):
                rows(h + 1)
            V.extend(("acc", layer, h, b) for h in range(heads) for b in range(5))
        else:
            V.extend(("acc", layer, g, i) for g in range(5) for i in range(4))

    turned("ln0")
    keys = [("key", i) for i in range(NKEY)]
    for t in range(NT):
        for half in range(2):
            V.append(("v", t, half))
            for _ in range(2):
                if keys:
                    V.append(keys.pop(0))
    V.extend(keys)

    def qk(h):
        V.extend((x, h, c) for x in "qk" for c in range(3))

    qk(0)
    for h in range(MH):
        A.append(("kn", h))
        A.extend(("pk", h, i) for i in range(5))
        A.extend(("pq", h, m, c) for m in range(2) for c in range(3))
        V.append(("kv", h))
        if h + 1 < MH:
            qk(h + 1)
        V.extend(("num", h, i) for i in range(2))
    turned("mix0")
    for t in range(NT):
        V.extend(("proj", t, half) for half in range(2))
        V.extend(("mask", t, g) for g in range(3))
    gat(0)
    turned("gat0")
    gat(1)
    turned("lnf")
    V.append(("logits",))
    for u in range(11):
        if u < 10:
            A.extend(("f1", u, i) for i in range(6))
        if u > 0:
            V.extend(("f2", u - 1, i) for i in range(4))
    turned("ln1")
    A.extend(("q1", m, c) for m in range(KD) for c in range(3))
    V.extend(("k1", t, half) for t in range(NT) for half in range(2))
    V.extend(("v1", t, half) for t in range(NT) for half in range(2))
    V.extend(("kv1", i) for i in range(2))
    V.extend(("n1", t, i) for t in range(NT) for i in range(2))
    turned("mix1")
    V.extend(("proj1", t, half) for t in range(NT) for half in range(2))
    gat(2)
    turned("gat1")
    gat(3)
    turned("lng")
    V.append(("router",))
    A.extend(("g1", 0, i) for i in range(4))
    V.append(("imp",))
    for c in range(6):
        if 0 < c < 5:
            A.extend(("g1", c, i) for i in range(4))
        if c < 5:
            V.extend(("gb", c, i) for i in range(4))
        if c > 0:
            V.extend(("g2", c - 1, i) for i in range(4))
    return V, A


def gps_kernel(nc, w, out):
    V_LIST, A_LIST = plan()
    V_AT = {name: i for i, name in enumerate(V_LIST)}
    A_AT = {name: i for i, name in enumerate(A_LIST)}

    counts = [nc.dram_tensor(f"count_matrix{i}", [CNT, 1], F32).ap() for i in range(2)]
    ct_dram = nc.dram_tensor("ct_saved", [T, NT * N], U16).ap()
    neg_dram = nc.dram_tensor("neg_saved", [T, NT * N], BF16).ap()
    res = [nc.dram_tensor(f"residual{i}", [N, D], F32).ap() for i in range(5)]
    XMID0, X1, X2, XMID1, X3 = range(5)

    ctx = ExitStack()
    with ctx:
        def sem(name):
            return ctx.enter_context(nc.semaphore(name))

        ARENA = 53200
        arena = ctx.enter_context(nc.sbuf_tensor("arena", [128, ARENA], F32))
        psum = ctx.enter_context(nc.psum_tensor("psum", [128, 8, 512], F32))
        BANKS_V = [psum[:, i, :] for i in range(VBANKS)]
        BANKS_A = [psum[:, VBANKS + i, :] for i in range(ABANKS)]

        def mem(at, *shape):
            n = 1
            for s in shape:
                n *= s
            assert at + n <= ARENA, (at, shape)
            v = arena[:, at:at + n]
            if len(shape) == 1:
                return v
            names = "abcd"[:len(shape)]
            return v.rearrange(f"p ({' '.join(names)}) -> p {' '.join(names)}",
                               **{k: s for k, s in zip(names[1:], shape[1:])})

        XT_AT, B_AT, C_AT, D_AT = 0, 7500, 15260, 22940
        W_AT = D_AT + 6250
        F_AT = W_AT + 4608
        ROW_AT = ARENA - 6 * D
        K_AT = ROW_AT - 810
        XT = mem(XT_AT, KD, N)
        Y = mem(C_AT, NT, D)
        NEG = arena[:, C_AT:C_AT + 6250].bitcast(BF16).rearrange("p (a b) -> p a b", a=NT)
        CT = arena[:, D_AT:D_AT + 6250].bitcast(U16).rearrange("p (a b) -> p a b", a=NT)
        W = mem(W_AT, KD, D)
        ROW = [mem(ROW_AT + i * D, D) for i in range(6)]
        used = [K_AT]

        def small(*shape):
            n = 1
            for s in shape:
                n *= s
            at = used[0]
            used[0] += n
            assert used[0] <= ROW_AT
            return mem(at, *shape) if shape else None

        IDENT = small(128)
        ONES = small(1)
        STATS = small(2, 2, 6)
        MV = small(NT, 2)
        STD = small(NT)
        RSTD = small(NT)
        VAR = small(NT)
        ASC, ADC, AS2, MX, EM, P1C, P2C = (small(H0, NT) for _ in range(7))
        RS = small(12)
        RS2 = small(12)
        POOLC = small(KD)
        LG = small(4)
        RB = small(4)
        CMP, CMP2 = small(4, 4), small(4, 4)
        LT4 = small(4, 4)
        IOTA4 = small(4)
        RANK = small(4)
        SEL = small(2, 4)
        TMP4 = small(2, 4)
        IDXF = small(2)
        LV = small(2)
        IDXI = small(2).bitcast(I32)
        GATE = small(2)
        CO = small(16)
        IS = small(2, 4)
        B1C = small(2, HM)
        RW0 = small(KD, 4)
        RZ2 = small(2, 3, 2)
        WA = small(KD, 2, H0)
        BC = [small(KD) for _ in range(2)]

        V0 = mem(B_AT, NT, MH, MD + 1)
        AT = mem(B_AT, KD, N)
        QK_AT = F_AT
        QKW = [mem(QK_AT + i * 1152, 2, KD, MD) for i in range(2)]
        QT, KT, Q2, K2 = (mem(QK_AT + 2304 + i * N, N) for i in range(4))
        PQ = mem(QK_AT + 7304, 2, N)
        PK = mem(QK_AT + 9804, NT, RF)
        assert QK_AT + 12364 <= K_AT
        d = [D_AT]

        def in_d(*shape):
            n = 1
            for s in shape:
                n *= s
            at = d[0]
            d[0] += n
            assert d[0] <= W_AT
            return mem(at, *shape)

        RFT = in_d(RF)
        KV0 = in_d(2, MD + 1)
        QKB = in_d(2, MH)
        KN = in_d(NT)
        HALVES = in_d(128)
        SRCI, DSTI = in_d(EC).bitcast(I32), in_d(EC).bitcast(I32)
        SRCF, DSTF, KEY, SEEN, COUNT, FIRSTF, IDXE = (in_d(EC) for _ in range(7))
        IDX_I = in_d(EC).bitcast(I32)
        TRASHI, TRASH = in_d(1).bitcast(I32), in_d(1)
        LOWER = in_d(T)
        EQ = [in_d(T) for _ in range(2)]
        EQL = [in_d(T) for _ in range(2)]
        SLOT_M = [mem(F_AT + 5000 + i * D, D) for i in range(2)]
        WG0 = mem(F_AT + 7500, KD, D)
        ZERO = in_d(N)

        HN4 = mem(B_AT, NT, H0, C0 + 1)
        HN1 = mem(B_AT, NT, D + 1)
        ET4 = [mem(F_AT + i * N, N) for i in range(4)]
        ET1 = [mem(F_AT + i * 2500, NT, 250) for i in range(2)]
        E2_AT = F_AT + 5000
        E24 = [mem(E2_AT + i * N, N) for i in range(2)]
        E21 = mem(E2_AT, NT, 250)
        PROW = [[mem(F_AT + 7500 + (2 * s + i) * N, N) for i in range(2)] for s in range(2)]
        ASROW = [mem(F_AT + 12500, N), mem(F_AT + 3750, N)]
        WA_PART = [[mem(F_AT + at + i * n, n) for i in range(2)]
                   for at, n in ((12500, C0), (12500, C0), (9216, D), (10000, D))]
        assert F_AT + 13750 <= K_AT
        SLOT_G = [mem(E2_AT + i * D, D) for i in range(2)]
        CS = [[mem(F_AT + (2 * s + i) * N, N) for i in range(2)] for s in range(2)]

        W1 = mem(D_AT, KD, HID)
        W2 = mem(D_AT + KD * HID, HM, D)
        HB_AT = D_AT + KD * HID + HM * D
        HB = [mem(HB_AT + i * 3000, HM, 250) for i in range(2)]
        assert HB_AT + 6000 <= K_AT
        EB = mem(B_AT, HM, 250)
        TB = mem(B_AT + 3000, HM, 250)
        SLOT_F = [mem(B_AT + i * D, D) for i in range(2)]
        NORM_F = [mem(B_AT + (2 + i) * D, D) for i in range(2)]

        QT1 = mem(D_AT, KD, N)
        K1 = mem(C_AT, NT, D)
        V1 = mem(B_AT, NT, KD, 129)
        WF = [mem(F_AT + i * KD * D, KD, D) for i in range(2)]
        TE = [mem(F_AT + 9216 + i * 500, 500) for i in range(2)]
        TR = [mem(F_AT + 10216 + i * 500, 500) for i in range(2)]
        KVB = mem(F_AT + 11216, KD, 130)
        BQ1 = mem(F_AT + 12002, KD)
        NBQ1 = mem(F_AT + 12008, KD)
        SLOT_1 = [mem(F_AT + 12014 + i * D, D) for i in range(2)]
        assert F_AT + 12014 + 2 * D <= K_AT

        GW1 = mem(D_AT, KD, E1 * I1)
        GW2 = mem(D_AT + KD * E1 * I1, E1, D)
        G_AT = D_AT + KD * E1 * I1 + E1 * D
        GA = [mem(G_AT + i * 2000, E1, 250) for i in range(2)]
        SLOT_2 = [mem(G_AT + 4000 + i * D, D) for i in range(2)]
        RWT = mem(G_AT + 5600, KD, E1)
        PR = mem(G_AT + 5700, NT, E1)
        PE_ = mem(G_AT + 5800, NT, E1)
        MASK1 = mem(G_AT + 5900, NT, E1)
        GG = mem(G_AT + 6000, NT, E1)
        RUN = mem(G_AT + 6100, E1)
        RMX = mem(G_AT + 6110, NT)
        LT8 = mem(G_AT + 6130, E1, E1)
        CM8 = mem(G_AT + 6200, NT, E1, E1)
        CM8B = mem(G_AT + 6200 + 640, NT, E1, E1)
        assert G_AT + 7480 <= K_AT

        v_filled, a_filled = sem("v_filled"), sem("a_filled")
        v_drained, a_drained = sem("v_drained"), sem("a_drained")
        x_loaded, edges_loaded = [sem(f"x_loaded{i}") for i in range(5)], sem("edges_loaded")
        consts_made, zeros_made, zeros_written = sem("consts_made"), sem("zeros_made"), sem("zeros_written")
        stats_made, std_made, tile_normed = sem("stats_made"), sem("std_made"), sem("tile_normed")
        keys_made, index_made = sem("keys_made"), sem("index_made")
        added = [sem("edges_added0"), sem("edges_added1")]
        wv_loaded, qkw_loaded, wp_loaded = sem("wv_loaded"), [sem("qkw_loaded0"), sem("qkw_loaded1")], sem("wp_loaded")
        m0_small = sem("mix0_constants_loaded")
        squares_made, v_ones = sem("squares_made"), sem("v_ones_made")
        slot_loaded = [sem("residual_loaded0"), sem("residual_loaded1")]
        slot_stored = [sem("residual_stored0"), sem("residual_stored1")]
        slot_done = sem("residual_done")
        count_loaded = [sem("counts_loaded0"), sem("counts_loaded1")]
        count_summed = sem("counts_summed")
        mask_saved = sem("mask_saved")
        max_done = sem("maxima_made")
        b1_loaded, lt8_made = sem("b1_loaded"), sem("lt8_made")
        neg_loaded, ct_loaded = [sem(f"neg_loaded{i}") for i in range(5)], sem("ct_loaded")
        wa_made = sem("score_weights_made")
        gw_loaded = [sem(f"gat_weight_loaded{i}") for i in range(4)]
        grow_loaded = [sem(f"gat_rows_loaded{i}") for i in range(4)]
        as_made, p_made, h_ones = sem("source_scores_made"), sem("target_scores_made"), sem("h_ones_made")
        gatb_loaded = sem("gat1_bias_loaded")
        row_made, score_made = sem("slope_rows_made"), sem("scores_made")
        exp_made, et_made, et_used = sem("exp_made"), sem("weights_made"), sem("weights_used")
        y_stored = sem("tiles_stored")
        pooled, routed, gate_exp = sem("pooled"), sem("experts_chosen"), sem("gate_exp")
        idx_made = sem("expert_index_made")
        rw_loaded = sem("router_loaded")
        f1_loaded, f2_loaded = [sem("w1_loaded0"), sem("w1_loaded1")], [sem("w2_loaded0"), sem("w2_loaded1")]
        frow_loaded = sem("ffn_rows_loaded")
        clamped, expd, t_made, gelu_made, act_made = (sem("hidden_clamped"), sem("hidden_exp"), sem("hidden_exp_used"),
                                                      sem("gelu_made"), sem("hidden_made"))
        m1w = [sem(f"mix1_weight_loaded{i}") for i in range(4)]
        m1_small = sem("mix1_constants_loaded")
        te_made, te_used, kvb_zero = sem("phi_parts_made"), sem("phi_made"), sem("kv1_cleared")
        gw1_loaded, gw2_loaded, grw_loaded = sem("gw1_loaded"), sem("gw2_loaded"), sem("grouter_loaded")
        rl_made, re_made, rp_made, gates_made, ga_made = (sem("router_centred"), sem("router_exp"), sem("router_probs"),
                                                          sem("gates_made"), sem("gated_hidden"))
        dve_step, act_step, pool_step = sem("dve_step"), sem("act_step"), sem("pool_step")

        block = ctx.enter_context(nc.Block())

        NCONST = 15

        @block.tensor
        def _(pe):
            count = {"V": 0, "A": 0}

            def fill(ring, name):
                at, banks, drained = (V_AT, BANKS_V, v_drained) if ring == "V" else (A_AT, BANKS_A, a_drained)
                i = at[name]
                assert i == count[ring], (name, i, count[ring])
                count[ring] += 1
                if i >= len(banks):
                    pe.wait_ge(drained, i - len(banks) + 1)
                return banks[i % len(banks)]

            def mm(o, lhsT, rhs, start, stop, share=False):
                return pe.matmul(o, lhsT, rhs, start=start, stop=stop, skip_group_check=share)

            def turn(stage, source, ready):
                for g, (t0, n) in enumerate(TG):
                    for k in range(KD):
                        ready(t0 + n - 1)
                        b = fill("A", ("tr", stage, g, k))
                        for i in range(n):
                            last = pe.transpose(b[:, i * T:(i + 1) * T], source[0:T, t0 + i, k * 128:(k + 1) * 128],
                                                IDENT[0:T, 0:T])
                        last.then_inc(a_filled, 1)

            def turned(stage):
                pe.wait_ge(a_drained, A_AT[("tr", stage, 2, KD - 1)] + 1)

            def natural_product(ring, name, weight, n, xt, blocks=KD, n0=0, tile=0):
                b = fill(ring, name)
                for k in range(blocks):
                    last = mm(b[0:T, 0:n], xt[:, k, tile * T:(tile + 1) * T], weight[:, k, n0:n0 + n],
                              k == 0, k == blocks - 1)
                last.then_inc(v_filled if ring == "V" else a_filled, 1)

            pe.wait_ge(consts_made, NCONST)
            turn("ln0", Y, lambda t: pe.wait_ge(tile_normed, t + 1))

            keys = list(range(NKEY))

            def key_rows():
                i = keys.pop(0)
                pe.wait_ge(keys_made, 1)
                b = fill("V", ("key", i))
                for j in range(min(KEYG, EC - i * KEYG)):
                    c = i * KEYG + j
                    last = pe.transpose(b[0:T, j * T:(j + 1) * T], KEY[0:T, c:c + 1].to_broadcast([T, T]),
                                        IDENT[0:T, 0:T])
                last.then_inc(v_filled, 1)

            turned("ln0")
            pe.wait_ge(wv_loaded, 16)
            for t in range(NT):
                for half in range(2):
                    natural_product("V", ("v", t, half), W, HALF, XT, n0=half * HALF, tile=t)
                    for _ in range(2):
                        if keys:
                            key_rows()
            while keys:
                key_rows()

            def qk(h):
                pe.wait_ge(qkw_loaded[h % 2], 16 * (h // 2 + 1))
                for i, x in enumerate("qk"):
                    for c, (n0, n) in enumerate(CH):
                        b = fill("V", (x, h, c))
                        for k in range(KD):
                            last = mm(b[0:MD, 0:n], QKW[h % 2][:, i, k, :], XT[:, k, n0:n0 + n], k == 0, k == KD - 1)
                        last.then_inc(v_filled, 1)

            qk(0)
            pe.wait_ge(m0_small, 64)
            for h in range(MH):
                pe.wait_ge(squares_made, 6 * h + 6)
                b = fill("A", ("kn", h))
                for t in range(NT):
                    last = mm(b[0:T, t:t + 1], K2[0:MD, t * T:(t + 1) * T], HALVES[0:MD, 0:1], True, True)
                last.then_inc(a_filled, 1)
                pe.wait_ge(v_drained, V_AT[("k", h, 2)] + 1)
                for i in range(5):
                    b = fill("A", ("pk", h, i))
                    for j in range(2):
                        t = 2 * i + j
                        last = mm(b[0:T, j * RF:(j + 1) * RF], KT[0:MD, t * T:(t + 1) * T], RFT[0:MD, :], True, True)
                    last.then_inc(a_filled, 1)
                for m in range(2):
                    for c, (n0, n) in enumerate(CH):
                        b = fill("A", ("pq", h, m, c))
                        mm(b[:, 0:n], RFT[0:MD, m * 128:(m + 1) * 128], QT[0:MD, n0:n0 + n], True, False)
                        mm(b[:, 0:n], HALVES[0:MD, :], Q2[0:MD, n0:n0 + n], False, True).then_inc(a_filled, 1)
                pe.wait_ge(a_drained, A_AT[("pk", h, 4)] + 1)
                pe.wait_ge(v_ones, 1)
                pe.wait_ge(v_drained, V_AT[("v", NT - 1, 1)] + 1)
                b = fill("V", ("kv", h))
                for m in range(2):
                    for t in range(NT):
                        last = mm(b[:, m * 97:(m + 1) * 97], PK[0:T, t, m * 128:(m + 1) * 128], V0[0:T, t, h, :],
                                  t == 0, t == NT - 1)
                last.then_inc(v_filled, 1)
                if h + 1 < MH:
                    qk(h + 1)
                pe.wait_ge(a_drained, A_AT[("pq", h, 1, 2)] + 1)
                pe.wait_ge(v_drained, V_AT[("kv", h)] + 1)
                for i in range(2):
                    b = fill("V", ("num", h, i))
                    for j in range(5):
                        t = 5 * i + j
                        for m in range(2):
                            last = mm(b[0:T, j * 97:(j + 1) * 97], PQ[:, m, t * T:(t + 1) * T], KV0[:, m, :],
                                      m == 0, m == 1)
                    last.then_inc(v_filled, 1)
            pe.wait_ge(v_drained, V_AT[("num", MH - 1, 1)] + 1)
            turn("mix0", Y, lambda t: None)
            turned("mix0")
            pe.wait_ge(wp_loaded, 16)
            for j in range(NT):
                for half in range(2):
                    natural_product("V", ("proj", j, half), W, HALF, AT, n0=half * HALF, tile=j)
                pe.wait_ge(count_summed, j + 1)
                for g, (t0, n) in enumerate(TG):
                    b = fill("V", ("mask", j, g))
                    for i in range(n):
                        last = pe.transpose(b[0:T, i * T:(i + 1) * T], CS[j % 2][0][0:T, (t0 + i) * T:(t0 + i + 1) * T],
                                            IDENT[0:T, 0:T])
                    last.then_inc(v_filled, 1)

            def column_rows(name, col):
                for q, (t0, n) in enumerate(TG):
                    b = fill("A", name + (q,))
                    for i in range(n):
                        last = pe.transpose(b[:, i * T:(i + 1) * T], col[0:T, t0 + i:t0 + i + 1].to_broadcast([T, 128]),
                                            IDENT[0:T, 0:T])
                    last.then_inc(a_filled, 1)

            def gat_front(layer):
                heads = H0 if layer < 2 else 1
                weight = WG0 if layer == 0 else W
                pe.wait_ge(wa_made, layer + 1)
                b = fill("V", ("sc", layer))
                for t in range(NT):
                    for k in range(KD):
                        last = mm(b[0:T, t * 2 * heads:(t + 1) * 2 * heads], XT[:, k, t * T:(t + 1) * T],
                                  WA[:, k, :, 0:heads], k == 0, k == KD - 1)
                last.then_inc(v_filled, 1)
                pe.wait_ge(h_ones, 1 + layer // 2)
                for what, i in front(layer):
                    if what == "asrow":
                        pe.wait_ge(as_made, layer + 1)
                        column_rows(("asrow", layer, i), ASC[:, i, :])
                    elif what == "h":
                        for half in range(2):
                            natural_product("A", ("h", layer, i, half), weight, HALF, XT, n0=half * HALF, tile=i)
                    elif what == "rows":
                        pe.wait_ge(p_made, layer + 1)
                        rows(layer, i)

            def gat4(layer):
                gat_front(layer)
                pe.wait_ge(a_drained, A_AT[("h", layer, NT - 1, 1)] + 1)
                for h in range(H0):
                    banks = [None] * 5
                    for j in range(NT):
                        n = (layer * H0 + h) * NT + j
                        pe.wait_ge(et_made, n + 1)
                        for t in range(NT):
                            if j == 0 and t % 2 == 0:
                                banks[t // 2] = fill("V", ("acc", layer, h, t // 2))
                            o = banks[t // 2][0:T, (t % 2) * (C0 + 1):(t % 2 + 1) * (C0 + 1)]
                            last = mm(o, ET4[n % 4][0:T, t * T:(t + 1) * T], HN4[0:T, j, h, :],
                                      j == 0 and t % 2 == 0, j == NT - 1, share=True)
                            if j == NT - 1 and t % 2 == 1:
                                last.then_inc(v_filled, 1)
                        if j < NT - 1:
                            last.then_inc(et_used, 1)
                        if j == 4 and h + 1 < H0:
                            rows(layer, h + 1)

            def rows(layer, h):
                column_rows(("p", layer, h, 0), P1C[:, h, :])
                column_rows(("p", layer, h, 1), P2C[:, h, :])

            def gat1(layer):
                gat_front(layer)
                pe.wait_ge(a_drained, A_AT[("h", layer, NT - 1, 1)] + 1)
                for g in range(5):
                    pe.wait_ge(et_made, 80 + (layer - 2) * 5 + g + 1)
                    for tt in range(2):
                        for p in range(2):
                            b = fill("V", ("acc", layer, g, 2 * tt + p))
                            n = HALF + p
                            for j in range(NT):
                                last = mm(b[0:T, 0:n], ET1[g % 2][0:T, j, tt * T:(tt + 1) * T],
                                          HN1[0:T, j, p * HALF:p * HALF + n], j == 0, j == NT - 1)
                            last.then_inc(v_filled, 1)

            gat4(0)
            pe.wait_ge(v_drained, V_AT[("acc", 0, H0 - 1, 4)] + 1)
            turn("gat0", Y, lambda t: None)
            turned("gat0")
            gat4(1)
            turn("lnf", Y, lambda t: pe.wait_ge(tile_normed, 10 + t + 1))

            pe.wait_ge(pooled, 1)
            pe.wait_ge(rw_loaded, 32)
            b = fill("V", ("logits",))
            for k in range(KD):
                last = mm(b[:, 0:4], POOLC[:, k:k + 1].to_broadcast([128, 128]), RW0[:, k, :], k == 0, k == KD - 1)
            last.then_inc(v_filled, 1)
            for u in range(11):
                if u < 10:
                    e, c = divmod(u, 5)
                    pe.wait_ge(f1_loaded[e], 16)
                    for i in range(6):
                        b = fill("A", ("f1", u, i))
                        for j in range(2):
                            m = 2 * i + j
                            for k in range(KD):
                                last = mm(b[:, j * 250:(j + 1) * 250], W1[:, k, m * 128:(m + 1) * 128],
                                          XT[:, k, c * 250:(c + 1) * 250], k == 0, k == KD - 1)
                        last.then_inc(a_filled, 1)
                if u > 0:
                    e, c = divmod(u - 1, 5)
                    pe.wait_ge(f2_loaded[e], 16)
                    pe.wait_ge(act_made, u)
                    for i in range(4):
                        tt, half = divmod(i, 2)
                        b = fill("V", ("f2", u - 1, i))
                        for m in range(HM):
                            last = mm(b[0:T, 0:HALF], HB[(u - 1) % 2][:, m, tt * T:(tt + 1) * T],
                                      W2[:, m, half * HALF:(half + 1) * HALF], m == 0, m == HM - 1)
                        last.then_inc(v_filled, 1)

            turn("ln1", Y, lambda t: pe.wait_ge(tile_normed, 20 + t + 1))
            turned("ln1")
            pe.wait_ge(m1w[0], 16)
            for m in range(KD):
                for c, (n0, n) in enumerate(CH):
                    b = fill("A", ("q1", m, c))
                    for k in range(KD):
                        last = mm(b[:, 0:n], WF[0][:, k, m * 128:(m + 1) * 128], XT[:, k, n0:n0 + n], k == 0, k == KD - 1)
                    last.then_inc(a_filled, 1)
            pe.wait_ge(m1w[1], 16)
            for t in range(NT):
                for half in range(2):
                    natural_product("V", ("k1", t, half), WF[1], HALF, XT, n0=half * HALF, tile=t)
            pe.wait_ge(m1w[2], 16)
            for t in range(NT):
                for half in range(2):
                    natural_product("V", ("v1", t, half), WF[0], HALF, XT, n0=half * HALF, tile=t)
            pe.wait_ge(te_used, 18 + 20)
            pe.wait_ge(kvb_zero, 2)
            pe.wait_ge(v_drained, V_AT[("v1", NT - 1, 1)] + 1)
            for i in range(2):
                b = fill("V", ("kv1", i))
                for j in range(3):
                    m = 3 * i + j
                    for t in range(NT):
                        last = mm(b[:, j * 129:(j + 1) * 129], K1[0:T, t, m * 128:(m + 1) * 128], V1[0:T, t, m, :],
                                  t == 0, t == NT - 1)
                last.then_inc(v_filled, 1)
            pe.wait_ge(v_drained, V_AT[("kv1", 1)] + 1)
            for t in range(NT):
                for i in range(2):
                    b = fill("V", ("n1", t, i))
                    for j in range(3):
                        m = 3 * i + j
                        last = mm(b[0:T, j * 130:(j + 1) * 130], QT1[:, m, t * T:(t + 1) * T], KVB[:, m, :], True, True)
                    last.then_inc(v_filled, 1)
            pe.wait_ge(v_drained, V_AT[("n1", NT - 1, 1)] + 1)
            turn("mix1", K1, lambda t: None)
            turned("mix1")
            pe.wait_ge(m1w[3], 16)
            for t in range(NT):
                for half in range(2):
                    natural_product("V", ("proj1", t, half), WF[1], HALF, AT, n0=half * HALF, tile=t)
            gat1(2)
            pe.wait_ge(v_drained, V_AT[("acc", 2, 4, 3)] + 1)
            turn("gat1", Y, lambda t: None)
            turned("gat1")
            gat1(3)
            turn("lng", Y, lambda t: pe.wait_ge(tile_normed, 30 + t + 1))
            turned("lng")
            pe.wait_ge(grw_loaded, 16)
            b = fill("V", ("router",))
            for t in range(NT):
                for k in range(KD):
                    last = mm(b[0:T, t * E1:(t + 1) * E1], XT[:, k, t * T:(t + 1) * T], RWT[:, k, :], k == 0, k == KD - 1)
            last.then_inc(v_filled, 1)

            def up1(c):
                pe.wait_ge(gw1_loaded, 16)
                for i in range(4):
                    b = fill("A", ("g1", c, i))
                    for j in range(2):
                        e = 2 * i + j
                        for k in range(KD):
                            last = mm(b[:, j * 250:(j + 1) * 250], GW1[:, k, e * I1:(e + 1) * I1],
                                      XT[:, k, c * 250:(c + 1) * 250], k == 0, k == KD - 1)
                    last.then_inc(a_filled, 1)

            up1(0)
            pe.wait_ge(rp_made, 1)
            b = fill("V", ("imp",))
            for t in range(NT):
                last = mm(b[:, 0:E1], ONES[0:T, 0:1].to_broadcast([T, 128]), PR[0:T, t, :], t == 0, t == NT - 1)
            last.then_inc(v_filled, 1)
            for c in range(6):
                if 0 < c < 5:
                    up1(c)
                if c < 5:
                    pe.wait_ge(gates_made, 1)
                    for i in range(4):
                        b = fill("V", ("gb", c, i))
                        for j in range(2):
                            e = 2 * i + j
                            for tt in range(2):
                                last = pe.transpose(b[:, j * 250 + tt * T:j * 250 + (tt + 1) * T],
                                                    GG[0:T, 2 * c + tt, e:e + 1].to_broadcast([T, 128]), IDENT[0:T, 0:T])
                        last.then_inc(v_filled, 1)
                if c > 0:
                    pe.wait_ge(v_drained, V_AT[("gb", c - 1, 3)] + 1)
                    pe.wait_ge(gw2_loaded, 16)
                    for i in range(4):
                        tt, half = divmod(i, 2)
                        b = fill("V", ("g2", c - 1, i))
                        for e in range(E1):
                            last = mm(b[0:T, 0:HALF], GA[(c - 1) % 2][:, e, tt * T:(tt + 1) * T],
                                      GW2[:, e, half * HALF:(half + 1) * HALF], e == 0, e == E1 - 1)
                        last.then_inc(v_filled, 1)
            assert count == {"V": len(V_LIST), "A": len(A_LIST)}

        @block.scalar
        def _(act):
            count = [0]
            own = [0]

            def bank(name):
                i = A_AT[name]
                assert i == count[0], (name, i, count[0])
                count[0] += 1
                return BANKS_A[i % ABANKS]

            def turn(stage, into, bias=None):
                for g, (t0, n) in enumerate(TG):
                    for k in range(KD):
                        act.wait_ge(a_filled, A_AT[("tr", stage, g, k)] + 1)
                        b = bank(("tr", stage, g, k))
                        o, i = into[:, k, t0 * T:(t0 + n) * T], b[:, 0:n * T]
                        if bias is None:
                            act.activation(o, i, ACT.Copy).then_inc(a_drained, 1)
                        else:
                            act.activation(o, i, ACT.Relu, bias=bias[:, k:k + 1]).then_inc(a_drained, 1)

            def deviation(stage):
                act.wait_ge(stats_made, stage + 1)
                act.activation(STD[0:T, :], VAR[0:T, :], ACT.Sqrt).then_inc(std_made, 1)

            deviation(0)
            turn("ln0", XT)

            def squares(h):
                for i, x in enumerate("qk"):
                    for c, (n0, n) in enumerate(CH):
                        act.wait_ge(v_drained, V_AT[(x, h, c)] + 1)
                        src, dst = ((QT, Q2), (KT, K2))[i]
                        act.activation(dst[0:MD, n0:n0 + n], src[0:MD, n0:n0 + n], ACT.Square).then_inc(squares_made, 1)

            squares(0)
            for h in range(MH):
                act.wait_ge(a_filled, A_AT[("kn", h)] + 1)
                b = bank(("kn", h))
                act.activation(KN[0:T, :], b[0:T, 0:NT], ACT.Copy).then_inc(a_drained, 1)
                act.wait_ge(a_drained, count[0])
                for i in range(5):
                    act.wait_ge(a_filled, A_AT[("pk", h, i)] + 1)
                    b = bank(("pk", h, i))
                    for j in range(2):
                        t = 2 * i + j
                        last = act.activation(PK[0:T, t, :], b[0:T, j * RF:(j + 1) * RF], ACT.Exp, bias=KN[0:T, t:t + 1])
                    last.then_inc(a_drained, 1)
                for m in range(2):
                    for c, (n0, n) in enumerate(CH):
                        act.wait_ge(a_filled, A_AT[("pq", h, m, c)] + 1)
                        b = bank(("pq", h, m, c))
                        act.activation(PQ[:, m, n0:n0 + n], b[:, 0:n], ACT.Exp).then_inc(a_drained, 1)
                if h + 1 < MH:
                    squares(h + 1)
            turn("mix0", AT)

            def rows(layer, h):
                for i in range(2):
                    for q, (t0, n) in enumerate(TG):
                        act.wait_ge(a_filled, A_AT[("p", layer, h, i, q)] + 1)
                        b = bank(("p", layer, h, i, q))
                        act.activation(PROW[h % 2][i][:, t0 * T:(t0 + n) * T], b[:, 0:n * T],
                                       ACT.Copy).then_inc(a_drained, 1)

            def weigh(et):
                act.activation(et, et, ACT.Relu, scale=-1.0).then_inc(act_step, 1)
                own[0] += 1
                act.wait_ge(act_step, own[0])
                act.activation(et, et, ACT.Exp, scale=-1.0).then_inc(exp_made, 1)

            def step4(layer, i):
                n = layer * H0 * NT + i
                if i < H0 * NT:
                    h, j = divmod(i, NT)
                    act.wait_ge(a_drained, A_AT[("p", layer, h, 1, 2)] + 1)
                    if n >= 2:
                        act.wait_ge(score_made, n - 1)
                    act.activation(E24[n % 2][0:T, :], PROW[h % 2][1][0:T, :], ACT.Identity,
                                   bias=AS2[0:T, h, j:j + 1]).then_inc(row_made, 1)
                if i > 0:
                    act.wait_ge(score_made, n)
                    weigh(ET4[(n - 1) % 4][0:T, :])
                if i < H0 * NT and j == 6 and h + 1 < H0:
                    rows(layer, h + 1)

            def step1(layer, i):
                n = 80 + (layer - 2) * 5 + i
                act.wait_ge(a_drained, A_AT[("p", layer, 0, 1, 2)] + 1)
                act.wait_ge(score_made, n)
                if i < 5:
                    for j in range(NT):
                        last = act.activation(E21[0:T, j, :], PROW[0][1][0:T, i * 250:(i + 1) * 250], ACT.Identity,
                                              bias=AS2[0:T, 0, j:j + 1])
                    last.then_inc(row_made, 1)
                if i > 0:
                    weigh(ET1[(i - 1) % 2][0:T])

            def gat(layer):
                heads = H0 if layer < 2 else 1
                step = step4 if layer < 2 else step1
                act.wait_ge(h_ones, 1 + layer // 2)
                if layer == 2:
                    for k in range(2):
                        act.wait_ge(slot_stored[k], 160)
                done = 0
                for what, i in front(layer):
                    if what == "h":
                        for half in range(2):
                            act.wait_ge(a_filled, A_AT[("h", layer, i, half)] + 1)
                            b = bank(("h", layer, i, half))
                            if heads > 1:
                                o = HN4[0:T, i, 2 * half:2 * half + 2, 0:C0]
                                v = b[0:T, 0:HALF].rearrange("p (a b) -> p a b", a=2)
                            else:
                                o, v = HN1[0:T, i, half * HALF:(half + 1) * HALF], b[0:T, 0:HALF]
                            act.activation(o, v, ACT.Copy).then_inc(a_drained, 1)
                    elif what == "asrow":
                        if i > 1:
                            act.wait_ge(max_done, layer * H0 + i - 1)
                        for q, (t0, n) in enumerate(TG):
                            act.wait_ge(a_filled, A_AT[("asrow", layer, i, q)] + 1)
                            b = bank(("asrow", layer, i, q))
                            act.activation(ASROW[i % 2][:, t0 * T:(t0 + n) * T], b[:, 0:n * T],
                                           ACT.Copy).then_inc(a_drained, 1)
                    elif what == "rows":
                        rows(layer, i)
                    else:
                        step(layer, i)
                        done = i + 1
                for i in range(done, H0 * NT + 1 if layer < 2 else 6):
                    step(layer, i)

            gat(0)
            act.wait_ge(grow_loaded[0], 48)
            turn("gat0", XT, BC[0])
            gat(1)
            deviation(1)
            turn("lnf", XT)
            act.wait_ge(routed, 1)
            act.activation(GATE[:, 1:2], LV[:, 1:2], ACT.Exp).then_inc(gate_exp, 1)

            for u in range(10):
                e = u // 5
                act.wait_ge(b1_loaded, 32)

                def expo(i):
                    act.wait_ge(clamped, 6 * u + i + 1)
                    act.activation(EB[:, 2 * i:2 * i + 2, :], TB[:, 2 * i:2 * i + 2, :], ACT.Exp).then_inc(expd, 1)

                for i in range(6):
                    act.wait_ge(a_filled, A_AT[("f1", u, i)] + 1)
                    b = bank(("f1", u, i))
                    for j in range(2):
                        m = 2 * i + j
                        last = act.activation(HB[u % 2][:, m, :], b[:, j * 250:(j + 1) * 250], ACT.Identity,
                                              bias=B1C[:, e, m:m + 1])
                    last.then_inc(a_drained, 1)
                    if i > 0:
                        expo(i - 1)
                expo(5)
                act.wait_ge(t_made, u + 1)
                act.activation(EB, HB[u % 2], ACT.Gelu).then_inc(gelu_made, 1)

            deviation(2)
            deviation(3)
            turn("ln1", XT)
            act.wait_ge(m1_small, 64)
            act.activation(NBQ1, BQ1, ACT.Copy, scale=-1.0).then_inc(act_step, 1)
            own[0] += 1
            act.wait_ge(act_step, own[0])
            n_te = 0
            for m in range(KD):
                for c, (n0, n) in enumerate(CH):
                    act.wait_ge(a_filled, A_AT[("q1", m, c)] + 1)
                    b = bank(("q1", m, c))
                    if n_te >= 2:
                        act.wait_ge(te_used, n_te - 1)
                    e = TE[n_te % 2][:, 0:n]
                    act.activation(e, b[:, 0:n], ACT.Relu, scale=-1.0, bias=NBQ1[:, m:m + 1]).then_inc(act_step, 1)
                    own[0] += 1
                    act.activation(TR[n_te % 2][:, 0:n], b[:, 0:n], ACT.Relu, bias=BQ1[:, m:m + 1]).then_inc(a_drained, 1)
                    act.wait_ge(act_step, own[0])
                    act.activation(e, e, ACT.Exp, scale=-1.0).then_inc(te_made, 1)
                    n_te += 1
            for t in range(NT):
                for half in range(2):
                    act.wait_ge(v_drained, V_AT[("k1", t, half)] + 1)
                    act.wait_ge(te_used, n_te - 1)
                    e = TE[n_te % 2][0:T, 0:HALF]
                    act.activation(e, K1[0:T, t, half * HALF:(half + 1) * HALF], ACT.Relu, scale=-1.0).then_inc(act_step, 1)
                    own[0] += 1
                    act.wait_ge(act_step, own[0])
                    act.activation(e, e, ACT.Exp, scale=-1.0).then_inc(te_made, 1)
                    n_te += 1
            turn("mix1", AT)
            gat(2)
            act.wait_ge(grow_loaded[2], 48)
            turn("gat1", XT, BC[1])
            gat(3)
            deviation(4)
            turn("lng", XT)

            def up1(c):
                for i in range(4):
                    act.wait_ge(a_filled, A_AT[("g1", c, i)] + 1)
                    b = bank(("g1", c, i))
                    act.activation(GA[c % 2][:, 2 * i:2 * i + 2, :], b[:, 0:500].rearrange("p (a b) -> p a b", a=2),
                                           ACT.Silu).then_inc(a_drained, 1)

            act.wait_ge(rl_made, 1)
            act.activation(PE_[0:T], PR[0:T], ACT.Exp).then_inc(re_made, 1)
            for c in range(5):
                up1(c)
            assert count[0] == len(A_LIST)


        @block.vector
        def _(dve):
            count = [0]
            own = [0]

            def bank(name):
                i = V_AT[name]
                assert i == count[0], (name, i, count[0])
                count[0] += 1
                return BANKS_V[i % VBANKS]

            def step(ins):
                ins.then_inc(dve_step, 1)
                own[0] += 1
                return own[0]

            def after(n):
                if n > 0:
                    dve.wait_ge(dve_step, n)

            def now(ins):
                after(step(ins))

            def stats(t, src):
                s = STATS[0:T, t % 2]
                for i in range(2):
                    n = step(dve.bn_stats(s[:, i, :], src[:, i * HALF:(i + 1) * HALF]))
                after(n)
                return step(dve.bn_aggr(MV[0:T, t, :], s.rearrange("p a b -> p (a b)")))

            def spread(stage):
                after(own[0])
                dve.tensor_scalar(VAR[0:T, :], MV[0:T, :, 1], LN_EPS, None, ALU.add).then_inc(stats_made, 1)
                dve.wait_ge(std_made, stage + 1)
                now(dve.reciprocal(RSTD[0:T, :], STD[0:T, :]))

            def normalise(o, src, t):
                return dve.tensor_scalar(o, src, MV[0:T, t, 0:1], RSTD[0:T, t:t + 1], ALU.subtract, ALU.mult)

            for t in range(NT):
                if t % 2 == 0:
                    dve.wait_ge(x_loaded[t // 2], 16)
                stats(t, Y[0:T, t, :])
            spread(0)
            for t in range(NT):
                normalise(Y[0:T, t, :], Y[0:T, t, :], t).then_inc(tile_normed, 1)

            dve.wait_ge(edges_loaded, 32)
            dve.wait_ge(consts_made, NCONST)
            step(dve.tensor_copy(SRCF[0:T], SRCI[0:T]))
            step(dve.tensor_copy(TRASH[0:T], TRASHI[0:T]))
            now(dve.tensor_copy(DSTF[0:T], DSTI[0:T]))
            dve.scalar_tensor_tensor(KEY[0:T], SRCF[0:T], float(N), DSTF[0:T], ALU.mult, ALU.add).then_inc(keys_made, 1)
            dve.wait_ge(keys_made, 1)

            scratch = [0, 0]
            keys = list(range(NKEY))
            batch = [0]

            def key_group():
                i = keys.pop(0)
                dve.wait_ge(v_filled, V_AT[("key", i)] + 1)
                b = bank(("key", i))
                for j in range(min(KEYG, EC - i * KEYG)):
                    c = i * KEYG + j
                    row = b[0:T, j * T:(j + 1) * T]
                    after(scratch[c % 2])
                    step(dve.tensor_scalar(EQ[c % 2][0:T], row, KEY[0:T, c:c + 1], 0.0, ALU.is_equal, ALU.add,
                                           accum_out=COUNT[0:T, c:c + 1]))
                    ins = dve.scalar_tensor_tensor(EQL[c % 2][0:T], row, KEY[0:T, c:c + 1], LOWER[0:T], ALU.is_equal,
                                                   ALU.mult, accum_out=SEEN[0:T, c:c + 1])
                    if j < KEYG - 1 and c < EC - 1:
                        scratch[c % 2] = step(ins)
                    else:
                        ins.then_inc(v_drained, 1)
                        dve.wait_ge(v_drained, V_AT[("key", i)] + 1)
                        scratch[c % 2] = own[0]
                if i % 5 == 4 or i == NKEY - 1:
                    c0, c1 = batch[0], min((i + 1) * KEYG, EC)
                    batch[0] = c1
                    s = lambda x: x[0:T, c0:c1]
                    step(dve.tensor_scalar(s(FIRSTF), s(SEEN), 1.0, None, ALU.min))
                    now(dve.tensor_scalar(s(IDXE), s(KEY), -1.0, TRASH[0:T, 0:1], ALU.mult, ALU.add))
                    now(dve.tensor_tensor(s(IDXE), s(IDXE), s(FIRSTF), ALU.mult))
                    now(dve.tensor_tensor(s(IDXE), s(IDXE), s(KEY), ALU.add))
                    dve.tensor_copy(s(IDX_I), s(IDXE)).then_inc(index_made, 1)

            dve.wait_ge(m0_small, 64)
            for t in range(NT):
                for half in range(2):
                    dve.wait_ge(v_filled, V_AT[("v", t, half)] + 1)
                    b = bank(("v", t, half))
                    dve.tensor_tensor(V0[0:T, t, 4 * half:4 * half + 4, 0:MD],
                                              b[0:T, 0:HALF].rearrange("p (a b) -> p a b", a=4),
                                              ROW[0][0:T, half * HALF:(half + 1) * HALF].rearrange("p (a b) -> p a b", a=4),
                                              ALU.add).then_inc(v_drained, 1)
                    for _ in range(2):
                        if keys:
                            key_group()
            while keys:
                key_group()

            def qk(h):
                for i, x in enumerate("qk"):
                    for c, (n0, n) in enumerate(CH):
                        dve.wait_ge(v_filled, V_AT[(x, h, c)] + 1)
                        b = bank((x, h, c))
                        dve.tensor_scalar((QT, KT)[i][0:MD, n0:n0 + n], b[0:MD, 0:n], QKB[0:MD, i, h:h + 1],
                                                  float(MD) ** -0.5, ALU.add, ALU.mult).then_inc(v_drained, 1)

            qk(0)
            for h in range(MH):
                dve.wait_ge(v_filled, V_AT[("kv", h)] + 1)
                b = bank(("kv", h))
                dve.tensor_copy(KV0, b[:, 0:194].rearrange("p (a b) -> p a b", a=2)).then_inc(v_drained, 1)
                if h + 1 < MH:
                    qk(h + 1)
                for i in range(2):
                    dve.wait_ge(v_filled, V_AT[("num", h, i)] + 1)
                    b = bank(("num", h, i))
                    v = b[0:T, 0:485].rearrange("p (a b) -> p a b", a=5)
                    r = RS[0:T, 5 * i:5 * i + 5]
                    now(dve.tensor_scalar(r, v[:, :, MD], 1e-6, None, ALU.max))
                    now(dve.reciprocal(r, r))
                    dve.tensor_tensor(Y[0:T, 5 * i:5 * i + 5, h * MD:(h + 1) * MD], v[:, :, 0:MD],
                                              r.unsqueeze(2).to_broadcast([T, 5, MD]), ALU.mult).then_inc(v_drained, 1)

            slots_used = [0]

            def slot(slots):
                n = slots_used[0]
                slots_used[0] += 1
                dve.wait_ge(slot_loaded[n % 2], 16 * (n // 2 + 1))
                return slots[n % 2][0:T]

            def score_weights(layer, blocks):
                heads = H0 if layer < 2 else 1
                a_s, a_d = (ROW[2], ROW[3], ROW[0], ROW[1], ROW[0], ROW[4], ROW[1], ROW[2])[2 * layer:2 * layer + 2]
                weight = WG0 if layer == 0 else W
                width = D // heads
                dve.wait_ge(grow_loaded[layer], 32 if layer == 1 else 48)
                dve.wait_ge(gw_loaded[layer], 16)
                for k in blocks:
                    for h in range(heads):
                        for i, row in enumerate((a_s, a_d)):
                            cols = slice(h * width, (h + 1) * width)
                            after(tok[i])
                            ins = dve.tensor_tensor_reduce(WA_PART[layer][i], weight[:, k, cols], row[:, cols], 1.0, 0.0,
                                                           ALU.mult, ALU.add, WA[:, k, i, h:h + 1])
                            if (k, h, i) == (KD - 1, heads - 1, 1):
                                ins.then_inc(wa_made, 1)
                            else:
                                tok[i] = step(ins)

            tok = [0, 0]

            def project(name, slots, bias, between):
                for t in range(NT):
                    s = slot(slots)
                    now(dve.tensor_tensor(s, s, bias[0:T], ALU.add))
                    for half in range(2):
                        dve.wait_ge(v_filled, V_AT[(name, t, half)] + 1)
                        b = bank((name, t, half))
                        o = s[:, half * HALF:(half + 1) * HALF]
                        dve.tensor_tensor(o, b[0:T, 0:HALF], o, ALU.add).then_inc(v_drained, 1)
                    dve.wait_ge(v_drained, count[0])
                    dve.engine_nop().then_inc(slot_done, 1)
                    between(t)

            def mask(j):
                dve.wait_ge(count_loaded[j % 2], 32 * (j // 2 + 1))
                c, c2 = CS[j % 2][0][0:T], CS[j % 2][1][0:T]
                now(dve.tensor_tensor(c, c, c2, ALU.add))
                own_block = c[:, j * T:(j + 1) * T]
                dve.tensor_tensor(own_block, own_block, IDENT[0:T, 0:T], ALU.add).then_inc(count_summed, 1)
                dve.wait_ge(count_summed, j + 1)
                step(dve.tensor_copy(CT[0:T, j, :], c))
                for g, (t0, n) in enumerate(TG):
                    dve.wait_ge(v_filled, V_AT[("mask", j, g)] + 1)
                    b = bank(("mask", j, g))
                    dve.tensor_scalar(NEG[0:T, t0:t0 + n, j * T:(j + 1) * T],
                                              b[0:T, 0:n * T].rearrange("p (a b) -> p a b", a=n),
                                              0.0, NEG_BIG, ALU.is_equal, ALU.mult).then_inc(v_drained, 1)
                if j == 3:
                    score_weights(0, range(KD))

            dve.wait_ge(gatb_loaded, 16)
            now(dve.tensor_tensor(ROW[1][0:T], ROW[1][0:T], ROW[5][0:T], ALU.add))
            project("proj", SLOT_M, ROW[1], mask)
            after(own[0])
            for k in range(2):
                dve.wait_ge(slot_stored[k], 80)

            def gat_front(layer):
                heads = H0 if layer < 2 else 1
                hs = slice(0, heads)
                dve.wait_ge(v_filled, V_AT[("sc", layer)] + 1)
                b = bank(("sc", layer))
                v = b[0:T, 0:2 * heads * NT].rearrange("p (t a h) -> p a h t", t=NT, a=2)
                step(dve.tensor_copy(ADC[0:T, hs], v[:, 1]))
                dve.tensor_copy(ASC[0:T, hs], v[:, 0]).then_inc(v_drained, 1)
                dve.wait_ge(v_drained, count[0])
                dve.tensor_scalar(AS2[0:T, hs], ASC[0:T, hs], SLOPE, None, ALU.mult).then_inc(as_made, 1)
                n = 0
                for h in range(heads):
                    dve.wait_ge(a_drained, A_AT[("asrow", layer, h, 2)] + 1)
                    for t in range(NT):
                        if layer > 0 and h == 0 and t % 2 == 0:
                            dve.wait_ge(neg_loaded[t // 2], 16 * layer)
                        after(tok[n % 2])
                        ins = dve.tensor_tensor_reduce(E24[n % 2][0:T, :], NEG[0:T, t, :], ASROW[h % 2][0:T, :], 1.0, -3e38,
                                                       ALU.add, ALU.max, MX[0:T, h, t:t + 1])
                        if t < NT - 1:
                            tok[n % 2] = step(ins)
                        else:
                            ins.then_inc(max_done, 1)
                            heads_done[0] += 1
                            dve.wait_ge(max_done, heads_done[0])
                            tok[n % 2] = own[0]
                        n += 1
                after(own[0])
                now(dve.tensor_tensor(EM[0:T, hs], ADC[0:T, hs], MX[0:T, hs], ALU.add))
                now(dve.scalar_tensor_tensor(EM[0:T, hs], EM[0:T, hs], SLOPE, EM[0:T, hs], ALU.mult, ALU.max))
                now(dve.tensor_tensor(P1C[0:T, hs], ADC[0:T, hs], EM[0:T, hs], ALU.subtract))
                dve.scalar_tensor_tensor(P2C[0:T, hs], ADC[0:T, hs], SLOPE, EM[0:T, hs], ALU.mult,
                                         ALU.subtract).then_inc(p_made, 1)

            heads_done = [0]

            def gat4(layer):
                gat_front(layer)
                dve.wait_ge(mask_saved, 32)

                def drain_head(h):
                    for k in range(5):
                        dve.wait_ge(v_filled, V_AT[("acc", layer, h, k)] + 1)
                        b = bank(("acc", layer, h, k))
                        v = b[0:T, 0:2 * (C0 + 1)].rearrange("p (a b) -> p a b", a=2)
                        r = RS[0:T, 2 * k:2 * k + 2]
                        now(dve.reciprocal(r, v[:, :, C0]))
                        dve.tensor_tensor(Y[0:T, 2 * k:2 * k + 2, h * C0:(h + 1) * C0], v[:, :, 0:C0],
                                          r.unsqueeze(2).to_broadcast([T, 2, C0]), ALU.mult).then_inc(v_drained, 1)

                for i in range(H0 * NT + 1):
                    n = layer * H0 * NT + i
                    if i < H0 * NT:
                        h, j = divmod(i, NT)
                        m = n - 4
                        if m >= 0:
                            ml, mh, mj = m // (H0 * NT), m // NT % H0, m % NT
                            if mj < NT - 1:
                                dve.wait_ge(et_used, (ml * H0 + mh) * (NT - 1) + mj + 1)
                            else:
                                dve.wait_ge(v_filled, V_AT[("acc", ml, mh, 4)] + 1)
                        dve.wait_ge(row_made, n + 1)
                        dve.scalar_tensor_tensor(ET4[n % 4][0:T], PROW[h % 2][0][0:T, :], ASC[0:T, h, j:j + 1],
                                                 E24[n % 2][0:T], ALU.add, ALU.max).then_inc(score_made, 1)
                    if i > 0:
                        et = ET4[(n - 1) % 4][0:T]
                        dve.wait_ge(exp_made, n)
                        dve.tensor_tensor(et, et, CT[0:T, (i - 1) % NT, :], ALU.mult).then_inc(et_made, 1)
                        if i > NT and i % NT == 1:
                            drain_head(i // NT - 1)
                        if layer == 0 and 12 <= i < 12 + KD:
                            score_weights(1, [i - 12])
                drain_head(H0 - 1)

            def gat1(layer):
                gat_front(layer)

                def scores(n, g):
                    dve.wait_ge(row_made, n + 1)
                    for j in range(NT):
                        last = dve.scalar_tensor_tensor(ET1[g % 2][0:T, j, :], PROW[0][0][0:T, g * 250:(g + 1) * 250],
                                                        ASC[0:T, 0, j:j + 1], E21[0:T, j, :], ALU.add, ALU.max)
                    last.then_inc(score_made, 1)

                def drain_group(g):
                    for tt in range(2):
                        t = 2 * g + tt
                        dve.wait_ge(v_filled, V_AT[("acc", layer, g, 2 * tt)] + 1)
                        b0 = bank(("acc", layer, g, 2 * tt))
                        dve.wait_ge(v_filled, V_AT[("acc", layer, g, 2 * tt + 1)] + 1)
                        b1 = bank(("acc", layer, g, 2 * tt + 1))
                        r = RS[0:T, 2 * tt:2 * tt + 1]
                        now(dve.reciprocal(r, b1[0:T, HALF:HALF + 1]))
                        for p, b in enumerate((b0, b1)):
                            dve.tensor_scalar(Y[0:T, t, p * HALF:(p + 1) * HALF], b[0:T, 0:HALF], r, None,
                                              ALU.mult).then_inc(v_drained, 1)

                if layer == 2:
                    dve.wait_ge(ct_loaded, 16)
                for g in range(6):
                    n = 80 + (layer - 2) * 5 + g
                    if g == 1:
                        scores(n, g)
                    if g > 0:
                        dve.wait_ge(exp_made, n)
                        et = ET1[(g - 1) % 2][0:T]
                        dve.tensor_tensor(et, et, CT[0:T, :, (g - 1) * 250:g * 250], ALU.mult).then_inc(et_made, 1)
                    if g > 1:
                        drain_group(g - 2)
                    if g != 1 and g < 5:
                        scores(n, g)
                    if layer == 2 and g == 2:
                        score_weights(3, range(KD))
                drain_group(4)

            def join(slots):
                dve.wait_ge(v_drained, count[0])
                for t in range(NT):
                    s = slot(slots)
                    dve.tensor_tensor(Y[0:T, t, :], Y[0:T, t, :], s, ALU.add).then_inc(slot_done, 1)
                    dve.wait_ge(slot_done, slots_used[0])
                    stats(t, Y[0:T, t, :])

            gat4(0)
            gat4(1)
            join(SLOT_G)
            spread(1)
            dve.wait_ge(y_stored, 160)
            for t in range(NT):
                normalise(Y[0:T, t, :], Y[0:T, t, :], t).then_inc(tile_normed, 1)

            dve.wait_ge(a_drained, A_AT[("tr", "lnf", 2, KD - 1)] + 1)
            now(dve.tensor_reduce(POOLC[:, :], XT, AX, ALU.add))
            dve.tensor_scalar(POOLC[:, :], POOLC[:, :], 1.0 / N, None, ALU.mult).then_inc(pooled, 1)
            dve.wait_ge(v_filled, V_AT[("logits",)] + 1)
            b = bank(("logits",))
            dve.wait_ge(rw_loaded, 32)
            dve.tensor_tensor(LG[:, :], b[:, 0:4], RB[:, :], ALU.add).then_inc(v_drained, 1)
            dve.wait_ge(v_drained, count[0])
            by_j = LG[:, :].unsqueeze(1).to_broadcast([128, 4, 4])
            by_i = LG[:, :].unsqueeze(2).to_broadcast([128, 4, 4])
            step(dve.tensor_tensor(CMP, by_j, by_i, ALU.is_gt))
            now(dve.tensor_tensor(CMP2, by_j, by_i, ALU.is_equal))
            now(dve.tensor_tensor(CMP2, CMP2, LT4, ALU.mult))
            now(dve.tensor_tensor(CMP, CMP, CMP2, ALU.add))
            now(dve.tensor_reduce(RANK[:, :], CMP, AX, ALU.add))
            for s in range(2):
                step(dve.tensor_scalar(SEL[:, s, :], RANK[:, :], float(s), None, ALU.is_equal))
            after(own[0])
            for s in range(2):
                step(dve.tensor_tensor(TMP4[:, s, :], SEL[:, s, :], IOTA4[:, :], ALU.mult))
                step(dve.tensor_tensor(IS[:, s, :], SEL[:, s, :], LG[:, :], ALU.mult))
            after(own[0])
            now(dve.tensor_reduce(IDXF[:, :], TMP4, AX, ALU.add))
            dve.tensor_copy(IDXI, IDXF).then_inc(idx_made, 1)
            now(dve.tensor_reduce(LV[:, :], IS, AX, ALU.add))
            dve.tensor_tensor(LV[:, 1:2], LV[:, 1:2], LV[:, 0:1], ALU.subtract).then_inc(routed, 1)
            KO, MISH, CC, NCK, KG = (CO[:, 2 * i:2 * i + 2] for i in range(5))
            step(dve.tensor_scalar(KO, IDXF, 1.0, None, ALU.is_equal))
            now(dve.tensor_scalar(MISH, IDXF, 2.0, None, ALU.is_equal))
            now(dve.tensor_tensor(KO, KO, MISH, ALU.add))
            step(dve.tensor_scalar(CC, MISH, 1.0, None, ALU.add))
            step(dve.tensor_scalar(KG, KO, -1.0, 1.0, ALU.mult, ALU.add))
            after(own[0])
            now(dve.scalar_tensor_tensor(NCK, CC, -1.0, KO, ALU.mult, ALU.mult))
            dve.wait_ge(gate_exp, 1)
            now(dve.tensor_scalar(GATE[:, 0:1], GATE[:, 1:2], 1.0, None, ALU.add))
            now(dve.reciprocal(GATE[:, 0:1], GATE[:, 0:1]))
            now(dve.tensor_tensor(GATE[:, 1:2], GATE[:, 1:2], GATE[:, 0:1], ALU.mult))
            dve.wait_ge(frow_loaded, 64)
            now(dve.tensor_scalar(ROW[5][0:T], ROW[2][0:T], GATE[0:T, 0:1], None, ALU.mult))
            now(dve.scalar_tensor_tensor(ROW[5][0:T], ROW[3][0:T], GATE[0:T, 1:2], ROW[5][0:T], ALU.mult, ALU.add))

            def clamp(u, i):
                dve.wait_ge(a_drained, A_AT[("f1", u, i)] + 1)
                s = slice(2 * i, 2 * i + 2)
                dve.tensor_scalar(TB[:, s, :], HB[u % 2][:, s, :], 30.0, None, ALU.min).then_inc(clamped, 1)

            def ratio(u, i):
                e = u // 5
                dve.wait_ge(expd, 6 * u + i + 1)
                s = slice(2 * i, 2 * i + 2)
                t_, x, h = TB[:, s, :], EB[:, s, :], HB[u % 2][:, s, :]
                c = lambda k: k[:, e:e + 1]
                now(dve.tensor_scalar(t_, x, c(MISH), c(CC), ALU.mult, ALU.add))
                ins = dve.tensor_tensor(t_, t_, x, ALU.mult)
                if i == 5:
                    ins.then_inc(t_made, 1)
                    dve.wait_ge(t_made, u + 1)
                else:
                    now(ins)
                now(dve.tensor_scalar(t_, t_, c(CC), None, ALU.add))
                now(dve.reciprocal(t_, t_))
                now(dve.scalar_tensor_tensor(t_, t_, c(NCK), h, ALU.mult, ALU.mult))
                now(dve.scalar_tensor_tensor(t_, h, c(KO), t_, ALU.mult, ALU.add))

            for u in range(11):
                if u < 10:
                    e = u // 5
                    for i in range(6):
                        clamp(u, i)
                        if i > 0:
                            ratio(u, i - 1)
                    ratio(u, 5)
                    dve.wait_ge(gelu_made, u + 1)
                    dve.scalar_tensor_tensor(HB[u % 2], EB, KG[:, e:e + 1], TB, ALU.mult, ALU.add).then_inc(act_made, 1)
                    dve.wait_ge(act_made, u + 1)
                if u > 0:
                    e, c = divmod(u - 1, 5)
                    for i in range(4):
                        tt, half = divmod(i, 2)
                        dve.wait_ge(v_filled, V_AT[("f2", u - 1, i)] + 1)
                        b = bank(("f2", u - 1, i))
                        o = Y[0:T, 2 * c + tt, half * HALF:(half + 1) * HALF]
                        dve.scalar_tensor_tensor(o, b[0:T, 0:HALF], GATE[0:T, e:e + 1], o, ALU.mult, ALU.add).then_inc(v_drained, 1)
            dve.wait_ge(v_drained, count[0])
            for t in range(NT):
                now(dve.tensor_tensor(Y[0:T, t, :], Y[0:T, t, :], ROW[5][0:T], ALU.add))
                stats(t, Y[0:T, t, :])
            spread(2)
            for t in range(NT):
                s = slot(SLOT_F)
                o = NORM_F[t % 2][0:T]
                now(normalise(o, Y[0:T, t, :], t))
                now(dve.tensor_tensor(o, o, ROW[4][0:T], ALU.mult))
                now(dve.tensor_tensor(o, o, ROW[0][0:T], ALU.add))
                dve.tensor_tensor(Y[0:T, t, :], o, s, ALU.add).then_inc(slot_done, 1)
                dve.wait_ge(slot_done, slots_used[0])
            for t in range(NT):
                stats(t, Y[0:T, t, :])
            spread(3)
            dve.wait_ge(y_stored, 320)
            for t in range(NT):
                normalise(Y[0:T, t, :], Y[0:T, t, :], t).then_inc(tile_normed, 1)

            dve.wait_ge(m1_small, 64)
            n_te = 0
            for m in range(KD):
                for c, (n0, n) in enumerate(CH):
                    dve.wait_ge(te_made, n_te + 1)
                    dve.tensor_tensor(QT1[:, m, n0:n0 + n], TE[n_te % 2][:, 0:n], TR[n_te % 2][:, 0:n],
                                      ALU.add).then_inc(te_used, 1)
                    n_te += 1
            for t in range(NT):
                for half in range(2):
                    cols = slice(half * HALF, (half + 1) * HALF)
                    dve.wait_ge(v_filled, V_AT[("k1", t, half)] + 1)
                    b = bank(("k1", t, half))
                    dve.tensor_tensor(K1[0:T, t, cols], b[0:T, 0:HALF], ROW[2][0:T, cols], ALU.add).then_inc(v_drained, 1)
                    dve.wait_ge(v_drained, count[0])
                    dve.wait_ge(te_made, n_te + 1)
                    e_ = TE[n_te % 2][0:T, 0:HALF]
                    k_ = K1[0:T, t, cols]
                    dve.scalar_tensor_tensor(k_, k_, 0.0, e_, ALU.max, ALU.add).then_inc(te_used, 1)
                    n_te += 1
            for t in range(NT):
                for half in range(2):
                    dve.wait_ge(v_filled, V_AT[("v1", t, half)] + 1)
                    b = bank(("v1", t, half))
                    dve.tensor_tensor(V1[0:T, t, 3 * half:3 * half + 3, 0:128],
                                              b[0:T, 0:HALF].rearrange("p (a b) -> p a b", a=3),
                                              ROW[3][0:T, half * HALF:(half + 1) * HALF].rearrange("p (a b) -> p a b", a=3),
                                              ALU.add).then_inc(v_drained, 1)
            dve.wait_ge(kvb_zero, 2)
            for i in range(2):
                dve.wait_ge(v_filled, V_AT[("kv1", i)] + 1)
                b = bank(("kv1", i))
                v = b[:, 0:387].rearrange("p (a b) -> p a b", a=3)
                for s in range(2):
                    p = slice(64 * s, 64 * s + 64)
                    step(dve.tensor_copy(KVB[p, 3 * i:3 * i + 3, 64 * s:64 * s + 64], v[p, :, 64 * s:64 * s + 64]))
                    last = dve.tensor_copy(KVB[p, 3 * i:3 * i + 3, 128 + s:129 + s], v[p, :, 128:129])
                    if s == 0:
                        step(last)
                last.then_inc(v_drained, 1)
            for t in range(NT):
                for i in range(2):
                    dve.wait_ge(v_filled, V_AT[("n1", t, i)] + 1)
                    b = bank(("n1", t, i))
                    v = b[0:T, 0:390].rearrange("p (a b) -> p a b", a=3)
                    RZ = RZ2[:, i]
                    now(dve.reciprocal(RZ[0:T], v[:, :, 128:130]))
                    for s in range(2):
                        last = dve.tensor_tensor(
                            K1[0:T, t, 384 * i:384 * (i + 1)].rearrange("p (a b) -> p a b", a=3)[:, :, 64 * s:64 * s + 64],
                            v[:, :, 64 * s:64 * s + 64], RZ[0:T, :, s:s + 1].to_broadcast([T, 3, 64]), ALU.mult)
                        if s == 0:
                            step(last)
                    last.then_inc(v_drained, 1)
            dve.wait_ge(grow_loaded[3], 16)
            now(dve.tensor_tensor(ROW[1][0:T], ROW[1][0:T], ROW[5][0:T], ALU.add))
            project("proj1", SLOT_1, ROW[1], lambda t: score_weights(2, range(KD)) if t == 4 else None)
            gat1(2)
            gat1(3)
            join(SLOT_G)
            spread(4)
            dve.wait_ge(y_stored, 480)
            for t in range(NT):
                normalise(Y[0:T, t, :], Y[0:T, t, :], t).then_inc(tile_normed, 1)

            dve.wait_ge(v_filled, V_AT[("router",)] + 1)
            b = bank(("router",))
            v = b[0:T, 0:NT * E1].rearrange("p (a b) -> p a b", a=NT)
            wide = lambda x: x[0:T].unsqueeze(2).to_broadcast([T, NT, E1])
            now(dve.tensor_reduce(RMX[0:T], v, AX, ALU.max))
            dve.tensor_tensor(PR[0:T], v, wide(RMX), ALU.subtract).then_inc(v_drained, 1)
            dve.wait_ge(v_drained, count[0])
            dve.engine_nop().then_inc(rl_made, 1)
            dve.wait_ge(re_made, 1)
            now(dve.tensor_reduce(RMX[0:T], PE_[0:T], AX, ALU.add))
            now(dve.reciprocal(RMX[0:T], RMX[0:T]))
            dve.tensor_tensor(PR[0:T], PE_[0:T], wide(RMX), ALU.mult).then_inc(rp_made, 1)
            dve.wait_ge(rp_made, 1)
            dve.wait_ge(lt8_made, 2)
            by_j = PR[0:T].unsqueeze(2).to_broadcast([T, NT, E1, E1])
            by_i = PR[0:T].unsqueeze(3).to_broadcast([T, NT, E1, E1])
            step(dve.tensor_tensor(CM8[0:T], by_j, by_i, ALU.is_gt))
            now(dve.tensor_tensor(CM8B[0:T], by_j, by_i, ALU.is_equal))
            now(dve.tensor_tensor(CM8B[0:T], CM8B[0:T], LT8[0:T].unsqueeze(1).to_broadcast([T, NT, E1, E1]), ALU.mult))
            now(dve.tensor_tensor(CM8[0:T], CM8[0:T], CM8B[0:T], ALU.add))
            now(dve.tensor_reduce(MASK1[0:T], CM8[0:T], AX, ALU.add))
            now(dve.tensor_scalar(MASK1[0:T], MASK1[0:T], 2.0, None, ALU.is_lt))
            now(dve.tensor_tensor(MASK1[0:T], MASK1[0:T], PR[0:T], ALU.mult))
            dve.wait_ge(v_filled, V_AT[("imp",)] + 1)
            b = bank(("imp",))
            dve.tensor_scalar(RUN, b[:, 0:E1], 0.1, 0.91, ALU.mult, ALU.add).then_inc(v_drained, 1)
            dve.wait_ge(v_drained, count[0])
            now(dve.reciprocal(RUN, RUN))
            now(dve.tensor_tensor(GG[0:T], MASK1[0:T], RUN[0:T].unsqueeze(1).to_broadcast([T, NT, E1]), ALU.mult))
            now(dve.tensor_reduce(RMX[0:T], GG[0:T], AX, ALU.add))
            now(dve.reciprocal(RMX[0:T], RMX[0:T]))
            dve.tensor_tensor(GG[0:T], GG[0:T], wide(RMX), ALU.mult).then_inc(gates_made, 1)

            for c in range(6):
                if c < 5:
                    for i in range(4):
                        dve.wait_ge(a_drained, A_AT[("g1", c, i)] + 1)
                        dve.wait_ge(v_filled, V_AT[("gb", c, i)] + 1)
                        b = bank(("gb", c, i))
                        o = GA[c % 2][:, 2 * i:2 * i + 2, :]
                        dve.tensor_tensor(o, o, b[:, 0:500].rearrange("p (a b) -> p a b", a=2), ALU.mult).then_inc(v_drained, 1)
                if c > 0:
                    for i in range(4):
                        tt, half = divmod(i, 2)
                        dve.wait_ge(v_filled, V_AT[("g2", c - 1, i)] + 1)
                        b = bank(("g2", c - 1, i))
                        if half == 0:
                            s = slot(SLOT_2)
                        o = s[:, half * HALF:(half + 1) * HALF]
                        dve.tensor_tensor(o, b[0:T, 0:HALF], o, ALU.add).then_inc(v_drained, 1)
                        if half == 1:
                            dve.wait_ge(v_drained, count[0])
                            dve.engine_nop().then_inc(slot_done, 1)
            assert count[0] == len(V_LIST)

        @block.gpsimd
        def _(pool):
            made = [0]

            def const(ins):
                ins.then_inc(consts_made, 1)
                made[0] += 1

            pool.memset(ZERO, 0.0).then_inc(zeros_made, 1)
            const(pool.memset(IDENT, 0.0))
            const(pool.memset(LOWER, 1.0))
            const(pool.memset(LT4, 1.0))
            const(pool.memset(ONES, 1.0))
            const(pool.memset(HALVES, -0.5))
            for i in range(4):
                const(pool.memset(IOTA4[:, i:i + 1], float(i)))
            const(pool.iota(TRASHI, pattern=[[0, 1]], base=N * N, channel_multiplier=1))
            pool.wait_ge(consts_made, 3)
            const(pool.affine_select(out=IDENT, in_=IDENT, compare_op=ALU.not_equal, fill=1.0, base=0,
                                     pattern=[[-1, 128]], channel_multiplier=1))
            const(pool.affine_select(out=LOWER, in_=LOWER, compare_op=ALU.is_gt, fill=0.0, base=0,
                                     pattern=[[-1, T]], channel_multiplier=1))
            const(pool.affine_select(out=LT4, in_=LT4, compare_op=ALU.is_gt, fill=0.0, base=0,
                                     pattern=[[1, 4], [-1, 4]], channel_multiplier=0))
            const(pool.memset(RS, 0.0))
            const(pool.memset(RS2, 0.0))
            assert made[0] == NCONST, made
            pool.memset(V0[0:T, :, :, MD:MD + 1], 1.0).then_inc(v_ones, 1)
            pool.wait_ge(zeros_written, 64)
            for c in range(EC):
                k = c % 2
                if c % (5 * KEYG) == 0:
                    pool.wait_ge(index_made, c // (5 * KEYG) + 1)
                if c >= 2:
                    pool.wait_ge(added[k], 16 * (c // 2))
                pool.indirect_dma_start(counts[k], bass.IndirectOffsetOnAxis(ap=IDX_I[0:T, c:c + 1].bitcast(U32), axis=0),
                                        COUNT[0:T, c:c + 1], None, compute_op=ALU.add).then_inc(added[k], 16)
            pool.wait_ge(v_filled, V_AT[("proj", NT - 1, 1)] + 1)
            pool.memset(HN4[0:T, :, :, C0:C0 + 1], 1.0).then_inc(h_ones, 1)
            pool.wait_ge(tile_normed, 30)
            pool.memset(V1[0:T, :, :, 128:129], 1.0).then_inc(kvb_zero, 1)
            pool.memset(KVB, 0.0).then_inc(kvb_zero, 1)
            pool.wait_ge(v_filled, V_AT[("proj1", NT - 1, 1)] + 1)
            pool.memset(HN1[0:T, :, D:D + 1], 1.0).then_inc(h_ones, 1)
            pool.wait_ge(et_made, 90)
            pool.memset(LT8, 1.0).then_inc(lt8_made, 1)
            pool.wait_ge(lt8_made, 1)
            pool.affine_select(out=LT8, in_=LT8, compare_op=ALU.is_gt, fill=0.0, base=0,
                               pattern=[[1, E1], [-1, E1]], channel_multiplier=0).then_inc(lt8_made, 1)

        @block.sync
        def _(sp):
            def load(o, i, s):
                sp.dma_start(o, i).then_inc(s, 16)

            def row_load(k, name, s):
                load(ROW[k], w[name].to_broadcast([128, D]), s)

            def vf(name):
                sp.wait_ge(v_filled, V_AT[name] + 1)

            def af(name):
                sp.wait_ge(a_filled, A_AT[name] + 1)

            x = w["x"]
            for i in range(5):
                load(Y[0:T, 2 * i:2 * i + 2, :], x[250 * i:250 * (i + 1), :].rearrange("(a p) d -> p a d", a=2), x_loaded[i])
            load(SRCI[0:T], w["src"], edges_loaded)
            load(DSTI[0:T], w["dst"], edges_loaded)
            load(W, w["mix0_wv"], wv_loaded)
            load(RFT[0:MD], w["mix0_rf"], m0_small)
            load(QKB[0:MD], w["mix0_qkb"], m0_small)
            row_load(0, "mix0_bv", m0_small)
            row_load(1, "mix0_bp", m0_small)
            for h in range(2):
                load(QKW[h], w["mix0_qk"][h], qkw_loaded[h])
            sp.wait_ge(zeros_made, 1)
            for k in range(2):
                load(counts[k][0:N * N, :].rearrange("(p c n) o -> p c (n o)", p=T, c=NT),
                     ZERO[0:T].unsqueeze(1).to_broadcast([T, NT, N]), zeros_written)
                load(counts[k][N * N:CNT, :], ZERO[0:T, 0:1], zeros_written)
            load(RW0, w["ffn0_rw"], rw_loaded)
            load(RB, w["ffn0_rb"].to_broadcast([128, 4]), rw_loaded)
            row_load(2, "gat0_as", grow_loaded[0])
            row_load(3, "gat0_ad", grow_loaded[0])
            load(BC[0], w["gat0_bc"], grow_loaded[0])
            row_load(5, "gat1_b", gatb_loaded)
            vf(("v", NT - 1, 1))
            load(W, w["mix0_wp"], wp_loaded)
            for h in range(2, MH):
                vf(("k", h - 2, 2))
                load(QKW[h % 2], w["mix0_qk"][h], qkw_loaded[h % 2])

            loads = [0, 0]
            stores = [0, 0]
            y_stores = [0]

            def residual(n_pass, src, slots, dst, in_slot, beside=lambda t: None):
                def get(t):
                    n = n_pass * NT + t
                    load(slots[n % 2][0:T], src[t * T:(t + 1) * T, :], slot_loaded[n % 2])

                get(0)
                get(1)
                beside(0)
                beside(1)
                for t in range(NT):
                    n = n_pass * NT + t
                    sp.wait_ge(slot_done, n + 1)
                    o = dst[t * T:(t + 1) * T, :]
                    if in_slot:
                        load(o, slots[n % 2][0:T], slot_stored[n % 2])
                        stores[n % 2] += 16
                        if t + 2 < NT:
                            sp.wait_ge(slot_stored[n % 2], stores[n % 2])
                    else:
                        load(o, Y[0:T, t, :], y_stored)
                    if t + 2 < NT:
                        get(t + 2)
                        beside(t + 2)
                if in_slot:
                    for k in range(2):
                        sp.wait_ge(slot_stored[k], stores[k])
                else:
                    y_stores[0] += 160
                    sp.wait_ge(y_stored, y_stores[0])

            vf(("num", MH - 1, 1))
            load(WG0, w["gat0_w"], gw_loaded[0])
            for k in range(2):
                sp.wait_ge(added[k], 16 * (EC // 2))

            def count_load(j):
                if j >= 2:
                    vf(("mask", j - 2, 2))
                    sp.wait_ge(v_drained, V_AT[("mask", j - 2, 0)] + 1)
                if j < NT:
                    for k in range(2):
                        load(CS[j % 2][k][0:T], counts[k][j * T * N:(j + 1) * T * N, :].rearrange("(p n) o -> p (n o)", p=T),
                             count_loaded[j % 2])

            residual(0, x, SLOT_M, res[XMID0], True, count_load)
            load(W, w["gat1_w"], gw_loaded[1])
            row_load(0, "gat1_as", grow_loaded[1])
            row_load(1, "gat1_ad", grow_loaded[1])
            sp.wait_ge(v_drained, V_AT[("mask", NT - 1, 2)] + 1)
            load(ct_dram, CT[0:T].rearrange("p a b -> p (a b)"), mask_saved)
            load(neg_dram, NEG[0:T].rearrange("p a b -> p (a b)"), mask_saved)
            sp.wait_ge(mask_saved, 32)

            def mask_load(stage):
                for i in range(5):
                    if i % 2 == 0:
                        af(("tr", stage, i // 2, KD - 1))
                    load(NEG[0:T, 2 * i:2 * i + 2, :].rearrange("p a b -> p (a b)"), neg_dram[:, 2 * i * N:(2 * i + 2) * N],
                         neg_loaded[i])

            mask_load("gat0")
            row_load(4, "ffn0_g", frow_loaded)
            sp.wait_ge(wa_made, 2)
            row_load(0, "ffn0_b", frow_loaded)
            sp.wait_ge(et_made, 80)
            residual(1, res[XMID0], SLOT_G, res[X1], False)

            sp.wait_ge(idx_made, 1)
            chosen = [sp.value_load(IDXI[0:1, s:s + 1], min_val=0, max_val=3) for s in range(2)]
            for s in range(2):
                load(B1C[:, s, :], w["ffn0_b1"][bass.DynSlice(chosen[s], 1)].rearrange("e p n -> (e p) n"), b1_loaded)
            load(W1.rearrange("p a b -> p (a b)"), w["ffn0_w1"][bass.DynSlice(chosen[0], 1)].rearrange("e p n -> (e p) n"), f1_loaded[0])
            for s in range(2):
                load(ROW[2 + s], w["ffn0_b2"][bass.DynSlice(chosen[s], 1), :].to_broadcast([128, D]), frow_loaded)
            load(W2.rearrange("p a b -> p (a b)"), w["ffn0_w2"][bass.DynSlice(chosen[0], 1)].rearrange("e p n -> (e p) n"), f2_loaded[0])
            af(("f1", 4, 5))
            load(W1.rearrange("p a b -> p (a b)"), w["ffn0_w1"][bass.DynSlice(chosen[1], 1)].rearrange("e p n -> (e p) n"), f1_loaded[1])
            vf(("f2", 4, 3))
            load(W2.rearrange("p a b -> p (a b)"), w["ffn0_w2"][bass.DynSlice(chosen[1], 1)].rearrange("e p n -> (e p) n"), f2_loaded[1])
            row_load(1, "mix1_bo", m1_small)
            row_load(2, "mix1_bk", m1_small)
            row_load(3, "mix1_bv", m1_small)
            vf(("f2", 9, 3))
            load(WF[0], w["mix1_wq"], m1w[0])
            load(WF[1], w["mix1_wk"], m1w[1])
            load(BQ1, w["mix1_bq"], m1_small)
            residual(2, res[X1], SLOT_F, res[X2], False)
            af(("q1", KD - 1, 2))
            load(WF[0], w["mix1_wv"], m1w[2])
            vf(("k1", NT - 1, 1))
            load(WF[1], w["mix1_wo"], m1w[3])
            vf(("n1", NT - 1, 1))
            load(CT[0:T].rearrange("p a b -> p (a b)"), ct_dram, ct_loaded)
            load(W, w["gat2_w"], gw_loaded[2])
            row_load(0, "gat2_as", grow_loaded[2])
            row_load(4, "gat2_ad", grow_loaded[2])
            load(BC[1], w["gat2_bc"], grow_loaded[2])
            row_load(5, "gat3_b", grow_loaded[3])
            mask_load("mix1")
            residual(3, res[X2], SLOT_1, res[XMID1], True)
            row_load(1, "gat3_as", grow_loaded[3])
            row_load(2, "gat3_ad", grow_loaded[3])
            af(("h", 2, NT - 1, 1))
            load(W, w["gat3_w"], gw_loaded[3])
            mask_load("gat1")
            sp.wait_ge(et_made, 90)
            vf(("acc", 3, 4, 3))
            load(GW1, w["ffn1_w1"], gw1_loaded)
            load(RWT, w["ffn1_rw"], grw_loaded)
            load(GW2, w["ffn1_w2"], gw2_loaded)
            residual(4, res[XMID1], SLOT_G, res[X3], False)
            residual(5, res[X3], SLOT_2, out, True)


def _inputs(inputs):
    import numpy as np

    g = {k: np.asarray(v) for k, v in inputs.items()}

    def by_rows(m):
        k, n = m.shape
        return m.reshape(k // 128, 128, n).transpose(1, 0, 2)

    def row(v):
        return v.reshape(1, -1)

    qkv, qkv_b = g["L0_mix_qkv_w"], g["L0_mix_qkv_b"]
    qk = qkv[:2 * D].reshape(2, MH, MD, KD, 128)
    out = {
        "x": g["x"],
        "src": g["src"].reshape(T, EC), "dst": g["dst"].reshape(T, EC),
        "mix0_wv": by_rows(qkv[2 * D:].T),
        "mix0_qk": qk.transpose(1, 4, 0, 3, 2),
        "mix0_qkb": qkv_b[:2 * D].reshape(2, MH, MD).transpose(2, 0, 1),
        "mix0_bv": row(qkv_b[2 * D:]), "mix0_bp": row(g["L0_mix_proj_b"]),
        "mix0_wp": by_rows(g["L0_mix_proj_w"].T), "mix0_rf": g["L0_mix_rf"].T,
        "ffn0_rw": by_rows(g["L0_ffn_router_w"].T), "ffn0_rb": row(g["L0_ffn_router_b"]),
        "ffn0_w1": g["L0_ffn_w1"].reshape(4, KD, 128, HID).transpose(0, 2, 1, 3).reshape(4, 128, KD * HID),
        "ffn0_b1": g["L0_ffn_b1"].reshape(4, HM, 128).transpose(0, 2, 1),
        "ffn0_w2": g["L0_ffn_w2"].reshape(4, HM, 128, D).transpose(0, 2, 1, 3).reshape(4, 128, HM * D),
        "ffn0_b2": g["L0_ffn_b2"], "ffn0_g": row(g["L0_ffn_ln_g"]), "ffn0_b": row(g["L0_ffn_ln_b"]),
        "mix1_wq": by_rows(g["L1_mix_Wq"]), "mix1_wk": by_rows(g["L1_mix_Wk"]), "mix1_wv": by_rows(g["L1_mix_Wv"]),
        "mix1_wo": by_rows(g["L1_mix_Wo"]), "mix1_bq": g["L1_mix_bq"].reshape(KD, 128).T,
        "mix1_bk": row(g["L1_mix_bk"]), "mix1_bv": row(g["L1_mix_bv"]), "mix1_bo": row(g["L1_mix_bo"]),
        "ffn1_rw": by_rows(g["L1_ffn_router_w"].T),
        "ffn1_w1": by_rows(g["L1_ffn_w1"].reshape(E1 * I1, D).T),
        "ffn1_w2": g["L1_ffn_w2"].transpose(2, 0, 1),
    }
    for i, (layer, n) in enumerate(((0, 1), (0, 2), (1, 1), (1, 2))):
        a = "a" if layer == 0 else "att"
        out[f"gat{i}_w"] = by_rows(g[f"L{layer}_gnn_W{n}"])
        out[f"gat{i}_as"] = row(g[f"L{layer}_gnn_{a}_src{n}"])
        out[f"gat{i}_ad"] = row(g[f"L{layer}_gnn_{a}_dst{n}"])
        out[f"gat{i}_b"] = row(g[f"L{layer}_gnn_b{n}"])
        out[f"gat{i}_bc"] = g[f"L{layer}_gnn_b{n}"].reshape(KD, 128).T
    for k in ("gat0_b", "gat2_b", "gat1_bc", "gat3_bc"):
        del out[k]
    return {k: np.ascontiguousarray(v) for k, v in out.items()}


def kernel(**inputs):
    import concourse.bacc as bacc
    from concourse.bass_utils import run_bass_kernel_spmd

    arrays = _inputs(inputs)
    nc = bacc.Bacc("TRN2", target_bir_lowering=False, num_devices=1)
    w = {k: nc.dram_tensor(f"in_{k}", a.shape, mybir.dt.from_np(a.dtype), kind="ExternalInput").ap()
         for k, a in arrays.items()}
    out = nc.dram_tensor("out_0", (N, D), F32, kind="ExternalOutput").ap()
    gps_kernel(nc, w, out)
    r = run_bass_kernel_spmd(nc, [{f"in_{k}": a for k, a in arrays.items()}], core_ids=[0])
    return r.results[0]["out_0"]
```

```python
import concourse.bass as bass
from concourse import mybir
from contextlib import ExitStack

F32 = mybir.dt.float32
BF16 = mybir.dt.bfloat16
U16 = mybir.dt.uint16
I32 = mybir.dt.int32
U32 = mybir.dt.uint32
ALU = mybir.AluOpType
ACT = mybir.ActivationFunctionType
AX = mybir.AxisListType.X

N, D = 1250, 768
T, NT = 125, 10
KD = D // 128
E = 21250
EC = E // T
KEYG = 4
NKEY = (EC + KEYG - 1) // KEYG
CH = [(0, 500), (500, 500), (1000, 250)]
TG = [(0, 4), (4, 4), (8, 2)]
HALF = D // 2
CNT = N * N + T
NEG_BIG = -1.0e30
LN_EPS = 1e-5
SLOPE = 0.2
H0, C0 = 4, 192
MH, MD, RF = 8, 96, 256
HID, HM = 1536, 12
E1, I1 = 8, 128
VBANKS, ABANKS = 5, 3


def front(layer):
    if layer > 1:
        seq = [("h", (t, 0)) for t in range(NT)] + [("asrow", 0)]
        for t in range(NT):
            seq.append(("h", (t, 1)))
            seq += {3: [("rows", 0), ("step", 0)], 7: [("step", 1)]}.get(t, [])
        return seq
    seq = [("asrow", 0), ("asrow", 1)]
    for t in range(NT):
        seq += [("h", (t, 0)), ("h", (t, 1))]
        seq += {2: [("asrow", 2)], 4: [("asrow", 3)]}.get(t, [])
        if layer == 1:
            seq += {7: [("rows", 0), ("step", 0)], 8: [("step", 1)], 9: [("step", 2)]}.get(t, [])
    if layer == 0:
        seq.append(("rows", 0))
    return seq


def plan():
    V, A = [], []

    def turned(stage, groups=range(3)):
        A.extend(("tr", stage, g, k) for g in groups for k in range(KD))

    def gat(layer):
        heads = H0 if layer < 2 else 1
        if layer < 2:
            V.append(("sc", layer))

        def rows(h):
            A.extend(("p", layer, h, i, q) for i in range(2) for q in range(3))

        for what, i in front(layer):
            if what == "h":
                A.append(("h", layer) + i)
            elif what == "asrow":
                A.extend(("asrow", layer, i, q) for q in range(3))
            elif what == "rows":
                rows(i)
        if heads > 1:
            for h in range(heads - 1):
                rows(h + 1)
            V.extend(("acc", layer, h, b) for h in range(heads) for b in range(5))
        else:
            V.extend(("acc", layer, g, i) for g in range(5) for i in range(4))

    turned("ln0")
    keys = [("key", i) for i in range(NKEY)]
    for t in range(NT):
        for half in range(2):
            V.append(("v", t, half))
            for _ in range(2):
                if keys:
                    V.append(keys.pop(0))
    V.extend(keys)

    def qk(h):
        V.extend((x, h, c) for x in "qk" for c in range(3))

    qk(0)
    for h in range(MH):
        A.append(("kn", h))
        A.extend(("qn", h, c) for c in range(3))
        A.extend(("pk", h, i) for i in range(5))
        A.extend(("pq", h, m, c) for m in range(2) for c in range(3))
        V.append(("kv", h))
        if h + 1 < MH:
            qk(h + 1)
        V.extend(("num", h, i) for i in range(2))
    turned("mix0")
    for t in range(NT):
        V.extend(("proj", t, half) for half in range(2))
        V.extend(("mask", t, g) for g in range(3))
    gat(0)
    turned("gat0")
    gat(1)
    turned("lnf")
    V.append(("logits",))
    for u in range(11):
        if u < 10:
            A.extend(("f1", u, i) for i in range(6))
        if u > 0:
            V.extend(("f2", u - 1, i) for i in range(4))
    turned("ln1", (0,))
    A.extend(("q1", m, 0) for m in range(KD))
    turned("ln1", (1, 2))
    A.extend(("q1", m, c) for c in (1, 2) for m in range(KD))
    V.extend(("k1", t, half) for t in range(NT) for half in range(2))
    V.extend(("v1", t, half) for t in range(NT) for half in range(2))
    V.extend(("kv1", i) for i in range(2))
    V.extend(("n1", t, i) for t in range(NT) for i in range(2))
    turned("mix1")
    V.extend(("proj1", t, half) for t in range(NT) for half in range(2))
    gat(2)
    turned("gat1")
    gat(3)
    turned("lng", (0, 1))
    A.extend(("g1", 0, i) for i in range(4))
    turned("lng", (2,))
    V.append(("router",))
    A.extend(("g1", 1, i) for i in range(4))
    V.append(("imp",))
    for c in range(6):
        if 1 < c < 5:
            A.extend(("g1", c, i) for i in range(4))
        if c < 5:
            V.extend(("gb", c, i) for i in range(4))
        if c > 0:
            V.extend(("g2", c - 1, i) for i in range(4))
    return V, A


def gps_kernel(nc, w, out):
    V_LIST, A_LIST = plan()
    V_AT = {name: i for i, name in enumerate(V_LIST)}
    A_AT = {name: i for i, name in enumerate(A_LIST)}

    counts = [nc.dram_tensor(f"count_matrix{i}", [CNT, 1], F32).ap() for i in range(2)]
    ct_dram = nc.dram_tensor("ct_saved", [T, NT * N], U16).ap()
    neg_dram = nc.dram_tensor("neg_saved", [T, NT * N], BF16).ap()
    res = [nc.dram_tensor(f"residual{i}", [N, D], F32).ap() for i in range(5)]
    XMID0, X1, X2, XMID1, X3 = range(5)

    ctx = ExitStack()
    with ctx:
        def sem(name):
            return ctx.enter_context(nc.semaphore(name))

        ARENA = 53200
        arena = ctx.enter_context(nc.sbuf_tensor("arena", [128, ARENA], F32))
        psum = ctx.enter_context(nc.psum_tensor("psum", [128, 8, 512], F32))
        BANKS_V = [psum[:, i, :] for i in range(VBANKS)]
        BANKS_A = [psum[:, VBANKS + i, :] for i in range(ABANKS)]

        def mem(at, *shape):
            n = 1
            for s in shape:
                n *= s
            assert at + n <= ARENA, (at, shape)
            v = arena[:, at:at + n]
            if len(shape) == 1:
                return v
            names = "abcd"[:len(shape)]
            return v.rearrange(f"p ({' '.join(names)}) -> p {' '.join(names)}",
                               **{k: s for k, s in zip(names[1:], shape[1:])})

        XT_AT, B_AT, C_AT, D_AT = 0, 7500, 15260, 22940
        W_AT = D_AT + 6250
        F_AT = W_AT + KD * (D + 2)
        ROW_AT = ARENA - 6 * D
        K_AT = ROW_AT - 838
        XT = mem(XT_AT, KD, N)
        Y = mem(C_AT, NT, D)
        NEG = arena[:, C_AT:C_AT + 6250].bitcast(BF16).rearrange("p (a b) -> p a b", a=NT)
        CT = arena[:, D_AT:D_AT + 6250].bitcast(U16).rearrange("p (a b) -> p a b", a=NT)
        W = mem(W_AT, KD, D)
        WS = mem(W_AT, KD, D + 2)
        ROW = [mem(ROW_AT + i * D, D) for i in range(6)]
        used = [K_AT]

        def small(*shape):
            n = 1
            for s in shape:
                n *= s
            at = used[0]
            used[0] += n
            assert used[0] <= ROW_AT
            return mem(at, *shape) if shape else None

        IDENT = small(128)
        ONES = small(1)
        STATS = small(2, 2, 6)
        MV = small(NT, 2)
        STD = small(NT)
        RSTD, NMR = small(NT), small(NT)
        VAR = small(NT)
        SC2 = small(2, H0, NT)
        ASC, ADC = SC2[:, 0], SC2[:, 1]
        AS2, MX, EM, P1C, P2C = (small(H0, NT) for _ in range(5))
        RS = small(12)
        RS2 = small(12)
        POOLC = small(KD)
        LG = small(4)
        RB = small(4)
        CMP, CMP2 = small(4, 4), small(4, 4)
        LT4 = small(4, 4)
        IOTA4 = small(4)
        RANK = small(4)
        SEL = small(2, 4)
        TMP4 = small(2, 4)
        IDXF = small(2)
        LV = small(2)
        IDXI = small(2).bitcast(I32)
        GATE = small(2)
        CO = small(16)
        IS = small(2, 4)
        B1C = small(2, HM)
        RW0 = small(KD, 4)
        RZ2 = small(2, 3, 2)
        WA = small(KD, 2, H0)
        BC = [small(KD) for _ in range(2)]
        POOL3 = small(KD, 3)
        STATS4 = ROW[5][:, 0:NT * H0 * 6].rearrange("p (a b c) -> p a b c", a=NT, b=H0)

        V0 = mem(B_AT, NT, MH, MD + 1)
        AT = mem(B_AT, KD, N)
        QK_AT = F_AT
        QKW = [mem(QK_AT + i * 1152, 2, KD, MD) for i in range(2)]
        QT, KT, Q2, K2 = (mem(QK_AT + 2304 + i * N, N) for i in range(4))
        PQ = mem(QK_AT + 7304, 2, N)
        PK = mem(QK_AT + 9804, NT, RF)
        assert QK_AT + 12364 <= K_AT
        d = [D_AT]

        def in_d(*shape):
            n = 1
            for s in shape:
                n *= s
            at = d[0]
            d[0] += n
            assert d[0] <= W_AT
            return mem(at, *shape)

        RFT = in_d(RF)
        KV0 = in_d(2, MD + 1)
        QKB = in_d(2, MH)
        KN = in_d(NT)
        HALVES = in_d(128)
        SRCI, DSTI = in_d(EC).bitcast(I32), in_d(EC).bitcast(I32)
        SRCF, DSTF, KEY, SEEN, COUNT, FIRSTF, IDXE = (in_d(EC) for _ in range(7))
        IDX_I = in_d(EC).bitcast(I32)
        TRASHI, TRASH = in_d(1).bitcast(I32), in_d(1)
        LOWER = in_d(T)
        EQ = [in_d(T) for _ in range(2)]
        EQL = [in_d(T) for _ in range(2)]
        SLOT_M = [mem(F_AT + 5000 + i * D, D) for i in range(2)]
        WG0 = mem(F_AT + 7500, KD, D)
        ZERO = in_d(N)

        HN4 = mem(B_AT, NT, H0, C0 + 1)
        HN1 = mem(B_AT, NT, D + 1)
        ET4 = [mem(F_AT + i * N, N) for i in range(4)]
        ET1 = [mem(F_AT + i * 2500, NT, 250) for i in range(2)]
        E2_AT = F_AT + 5000
        E24 = [mem(E2_AT + i * N, N) for i in range(2)]
        E21 = mem(E2_AT, NT, 250)
        PROW = [[mem(F_AT + 7500 + (2 * s + i) * N, N) for i in range(2)] for s in range(2)]
        ASROW = [mem(F_AT + 12500, N), mem(F_AT + 3750, N)]
        WA_PART = [[mem(F_AT + at + i * n, n) for i in range(2)]
                   for at, n in ((12500, C0), (12500, C0), (9216, D), (10000, D))]
        assert F_AT + 13750 <= K_AT
        CS = [[mem(F_AT + (2 * s + i) * N, N) for i in range(2)] for s in range(2)]

        W1 = mem(D_AT, KD, HID)
        W2 = mem(D_AT + KD * HID, HM, D)
        HB_AT = D_AT + KD * HID + HM * D
        HB = [mem(HB_AT + i * 3000, HM, 250) for i in range(2)]
        assert HB_AT + 6000 <= K_AT
        EB = mem(B_AT, HM, 250)
        TB = mem(B_AT + 3000, HM, 250)
        SLOT_F = [mem(B_AT + 6000 + i * D, D) for i in range(2)]

        QT1 = mem(D_AT, KD, N)
        K1 = mem(C_AT, NT, D)
        V1 = mem(B_AT, NT, KD, 129)
        WQ = mem(B_AT, KD, D)
        WF = [mem(F_AT + i * KD * D, KD, D) for i in range(2)]
        TE = [mem(F_AT + 9216 + i * 500, 500) for i in range(2)]
        TR = [mem(F_AT + 10216 + i * 500, 500) for i in range(2)]
        KVB = mem(F_AT + 11216, KD, 130)
        BQ1 = mem(F_AT + 12002, KD)
        NBQ1 = mem(F_AT + 12008, KD)
        SLOT_1 = [mem(F_AT + 12014 + i * D, D) for i in range(2)]
        assert F_AT + 12014 + 2 * D <= K_AT

        GW1 = mem(D_AT, KD, E1 * I1)
        GW2 = mem(D_AT + KD * E1 * I1, E1, D)
        G_AT = D_AT + KD * E1 * I1 + E1 * D
        GA = [mem(G_AT + i * 2000, E1, 250) for i in range(2)]
        SLOT_2 = [mem(G_AT + 4000 + i * D, D) for i in range(2)]
        RWT = mem(G_AT + 5600, KD, E1)
        PR = mem(G_AT + 5700, NT, E1)
        PE_ = mem(G_AT + 5800, NT, E1)
        MASK1 = mem(G_AT + 5900, NT, E1)
        GG = mem(G_AT + 6000, NT, E1)
        RUN = mem(G_AT + 6100, E1)
        RMX = mem(G_AT + 6110, NT)
        LT8 = mem(G_AT + 6130, E1, E1)
        CM8 = mem(G_AT + 6200, NT, E1, E1)
        CM8B = mem(G_AT + 6200 + 640, NT, E1, E1)
        assert G_AT + 7480 <= K_AT

        v_filled, a_filled = sem("v_filled"), sem("a_filled")
        v_drained, a_drained = sem("v_drained"), sem("a_drained")
        x_loaded, edges_loaded = [sem(f"x_loaded{i}") for i in range(5)], sem("edges_loaded")
        consts_made, zeros_made, zeros_written = sem("consts_made"), sem("zeros_made"), sem("zeros_written")
        stats_made, std_made, scale_made = sem("stats_made"), sem("std_made"), sem("scale_made")
        tile_normed, x_normed = sem("tile_normed"), sem("x_normed")
        pair_stats, pair_std, pair_normed = sem("pair_stats_made"), sem("pair_std_made"), sem("pair_normed")
        keys_made, index_made = sem("keys_made"), sem("index_made")
        added = [sem("edges_added0"), sem("edges_added1")]
        wv_loaded, qkw_loaded, wp_loaded = sem("wv_loaded"), [sem("qkw_loaded0"), sem("qkw_loaded1")], sem("wp_loaded")
        m0_small = sem("mix0_constants_loaded")
        squares_made, v_ones = sem("squares_made"), sem("v_ones_made")
        slot_loaded = [sem("residual_loaded0"), sem("residual_loaded1")]
        slot_stored = [sem("residual_stored0"), sem("residual_stored1")]
        slot_done = sem("residual_done")
        count_loaded = [sem("counts_loaded0"), sem("counts_loaded1")]
        count_summed = sem("counts_summed")
        mask_saved = sem("mask_saved")
        max_done = sem("maxima_made")
        b1_loaded, lt8_made = sem("b1_loaded"), sem("lt8_made")
        neg_loaded, ct_loaded = [sem(f"neg_loaded{i}") for i in range(5)], sem("ct_loaded")
        norm_row_made = sem("norm_row_made")
        wa_made = sem("score_weights_made")
        gw_loaded = [sem(f"gat_weight_loaded{i}") for i in range(4)]
        grow_loaded = [sem(f"gat_rows_loaded{i}") for i in range(4)]
        as_made, p_made, h_ones = sem("source_scores_made"), sem("target_scores_made"), sem("h_ones_made")
        gatb_loaded = sem("gat1_bias_loaded")
        slopes_made, larger_made = sem("slopes_made"), sem("larger_made")
        et_made, et_used = sem("weights_made"), sem("weights_used")
        y_loaded = [sem(f"tiles_loaded{i}") for i in range(5)]
        y_stored = [sem(f"tiles_stored{i}") for i in range(5)]
        pooled, routed, gate_exp = sem("pooled"), sem("experts_chosen"), sem("gate_exp")
        idx_made = sem("expert_index_made")
        rw_loaded = sem("router_loaded")
        f1_first = [sem(f"w1_columns_loaded{i}") for i in range(6)]
        f1_loaded, f2_loaded = [None, sem("w1_loaded1")], [sem("w2_loaded0"), sem("w2_loaded1")]
        frow_loaded = sem("ffn_rows_loaded")
        clamped, expd, t_made, gelu_made, act_made = (sem("hidden_clamped"), sem("hidden_exp"), sem("hidden_exp_used"),
                                                      sem("gelu_made"), sem("hidden_made"))
        m1w = [sem(f"mix1_weight_loaded{i}") for i in range(4)]
        m1_small = sem("mix1_constants_loaded")
        te_made, te_used, kvb_zero = sem("phi_parts_made"), sem("phi_made"), sem("kv1_cleared")
        gw1_loaded, gw2_loaded, grw_loaded = sem("gw1_loaded"), sem("gw2_loaded"), sem("grouter_loaded")
        rl_made, re_made, rp_made, gates_made, ga_made = (sem("router_centred"), sem("router_exp"), sem("router_probs"),
                                                          sem("gates_made"), sem("gated_hidden"))
        dve_step, act_step, pool_step = sem("dve_step"), sem("act_step"), sem("pool_step")

        block = ctx.enter_context(nc.Block())

        NCONST = 15

        @block.tensor
        def _(pe):
            count = {"V": 0, "A": 0}

            def fill(ring, name):
                at, banks, drained = (V_AT, BANKS_V, v_drained) if ring == "V" else (A_AT, BANKS_A, a_drained)
                i = at[name]
                assert i == count[ring], (name, i, count[ring])
                count[ring] += 1
                if i >= len(banks):
                    pe.wait_ge(drained, i - len(banks) + 1)
                return banks[i % len(banks)]

            def mm(o, lhsT, rhs, start, stop, share=False):
                return pe.matmul(o, lhsT, rhs, start=start, stop=stop, skip_group_check=share)

            def turn(stage, source, ready, groups=range(3)):
                for g in groups:
                    t0, n = TG[g]
                    for k in range(KD):
                        ready(t0 + n - 1)
                        b = fill("A", ("tr", stage, g, k))
                        for i in range(n):
                            last = pe.transpose(b[:, i * T:(i + 1) * T], source[0:T, t0 + i, k * 128:(k + 1) * 128],
                                                IDENT[0:T, 0:T])
                        last.then_inc(a_filled, 1)

            def turned(stage, g=2):
                pe.wait_ge(a_drained, A_AT[("tr", stage, g, KD - 1)] + 1)

            def natural_product(ring, name, weight, n, xt, blocks=KD, n0=0, tile=0):
                b = fill(ring, name)
                for k in range(blocks):
                    last = mm(b[0:T, 0:n], xt[:, k, tile * T:(tile + 1) * T], weight[:, k, n0:n0 + n],
                              k == 0, k == blocks - 1)
                last.then_inc(v_filled if ring == "V" else a_filled, 1)

            def turn_group_of(t, stage, source, ready=lambda t: None):
                for g, (t0, _) in enumerate(TG):
                    if t == t0:
                        turn(stage, source, ready, (g,))
                        turned(stage, g)

            pe.wait_ge(consts_made, NCONST)

            keys = list(range(NKEY))

            def key_rows():
                i = keys.pop(0)
                pe.wait_ge(keys_made, 1)
                b = fill("V", ("key", i))
                for j in range(min(KEYG, EC - i * KEYG)):
                    c = i * KEYG + j
                    last = pe.transpose(b[0:T, j * T:(j + 1) * T], KEY[0:T, c:c + 1].to_broadcast([T, T]),
                                        IDENT[0:T, 0:T])
                last.then_inc(v_filled, 1)

            for t in range(NT):
                turn_group_of(t, "ln0", Y, lambda t: pe.wait_ge(x_normed, t + 1))
                if t == 0:
                    pe.wait_ge(wv_loaded, 16)
                for half in range(2):
                    natural_product("V", ("v", t, half), W, HALF, XT, n0=half * HALF, tile=t)
                    for _ in range(2):
                        if keys:
                            key_rows()
            while keys:
                key_rows()

            def qk(h):
                pe.wait_ge(qkw_loaded[h % 2], 16 * (h // 2 + 1))
                for i, x in enumerate("qk"):
                    for c, (n0, n) in enumerate(CH):
                        b = fill("V", (x, h, c))
                        for k in range(KD):
                            last = mm(b[0:MD, 0:n], QKW[h % 2][:, i, k, :], XT[:, k, n0:n0 + n], k == 0, k == KD - 1)
                        last.then_inc(v_filled, 1)

            qk(0)
            pe.wait_ge(m0_small, 64)
            pe.wait_ge(norm_row_made, 1)
            for h in range(MH):
                pe.wait_ge(squares_made, 6 * h + 6)
                b = fill("A", ("kn", h))
                for t in range(NT):
                    last = mm(b[0:T, t:t + 1], K2[0:MD, t * T:(t + 1) * T], HALVES[0:MD, 0:1], True, True)
                last.then_inc(a_filled, 1)
                for c, (n0, n) in enumerate(CH):
                    b = fill("A", ("qn", h, c))
                    mm(b[0:MD + 1, 0:n], HALVES[0:MD, 0:MD + 1], Q2[0:MD, n0:n0 + n], True, True).then_inc(a_filled, 1)
                pe.wait_ge(v_drained, V_AT[("k", h, 2)] + 1)
                for i in range(5):
                    b = fill("A", ("pk", h, i))
                    for j in range(2):
                        t = 2 * i + j
                        last = mm(b[0:T, j * RF:(j + 1) * RF], KT[0:MD, t * T:(t + 1) * T], RFT[0:MD, :], True, True)
                    last.then_inc(a_filled, 1)
                pe.wait_ge(a_drained, A_AT[("qn", h, 2)] + 1)
                for m in range(2):
                    for c, (n0, n) in enumerate(CH):
                        b = fill("A", ("pq", h, m, c))
                        mm(b[:, 0:n], RFT[0:MD + 1, m * 128:(m + 1) * 128], QT[0:MD + 1, n0:n0 + n],
                           True, True).then_inc(a_filled, 1)
                pe.wait_ge(a_drained, A_AT[("pk", h, 4)] + 1)
                pe.wait_ge(v_ones, 1)
                pe.wait_ge(v_drained, V_AT[("v", NT - 1, 1)] + 1)
                b = fill("V", ("kv", h))
                for m in range(2):
                    for t in range(NT):
                        last = mm(b[:, m * 97:(m + 1) * 97], PK[0:T, t, m * 128:(m + 1) * 128], V0[0:T, t, h, :],
                                  t == 0, t == NT - 1)
                last.then_inc(v_filled, 1)
                if h + 1 < MH:
                    qk(h + 1)
                pe.wait_ge(a_drained, A_AT[("pq", h, 1, 2)] + 1)
                pe.wait_ge(v_drained, V_AT[("kv", h)] + 1)
                for i in range(2):
                    b = fill("V", ("num", h, i))
                    for j in range(5):
                        t = 5 * i + j
                        for m in range(2):
                            last = mm(b[0:T, j * 97:(j + 1) * 97], PQ[:, m, t * T:(t + 1) * T], KV0[:, m, :],
                                      m == 0, m == 1)
                    last.then_inc(v_filled, 1)
            pe.wait_ge(v_drained, V_AT[("num", MH - 1, 1)] + 1)
            turn("mix0", Y, lambda t: None)
            turned("mix0")
            pe.wait_ge(wp_loaded, 16)
            for j in range(NT):
                for half in range(2):
                    natural_product("V", ("proj", j, half), W, HALF, AT, n0=half * HALF, tile=j)
                pe.wait_ge(count_summed, j + 1)
                for g, (t0, n) in enumerate(TG):
                    b = fill("V", ("mask", j, g))
                    for i in range(n):
                        last = pe.transpose(b[0:T, i * T:(i + 1) * T], CS[j % 2][0][0:T, (t0 + i) * T:(t0 + i + 1) * T],
                                            IDENT[0:T, 0:T])
                    last.then_inc(v_filled, 1)

            def column_rows(name, col):
                for q, (t0, n) in enumerate(TG):
                    b = fill("A", name + (q,))
                    for i in range(n):
                        last = pe.transpose(b[:, i * T:(i + 1) * T], col[0:T, t0 + i:t0 + i + 1].to_broadcast([T, 128]),
                                            IDENT[0:T, 0:T])
                    last.then_inc(a_filled, 1)

            def gat_front(layer):
                heads = H0 if layer < 2 else 1
                weight = (WG0, W, WS, WS)[layer]
                pe.wait_ge(wa_made, layer + 1)
                if layer < 2:
                    b = fill("V", ("sc", layer))
                    for t in range(NT):
                        for k in range(KD):
                            last = mm(b[0:T, t * 2 * heads:(t + 1) * 2 * heads], XT[:, k, t * T:(t + 1) * T],
                                      WA[:, k, :, 0:heads], k == 0, k == KD - 1)
                    last.then_inc(v_filled, 1)
                pe.wait_ge(h_ones, 1 + layer // 2)
                for what, i in front(layer):
                    if what == "asrow":
                        pe.wait_ge(as_made, layer + 1)
                        column_rows(("asrow", layer, i), ASC[:, i, :])
                    elif what == "h":
                        t, half = i
                        if layer < 2:
                            natural_product("A", ("h", layer) + i, weight, HALF, XT, n0=half * HALF, tile=t)
                        else:
                            natural_product("A", ("h", layer) + i, weight, HALF + 2 - 2 * half, XT,
                                            n0=half * (HALF + 2), tile=t)
                    elif what == "rows":
                        pe.wait_ge(p_made, layer + 1)
                        rows(layer, i)

            def gat4(layer):
                gat_front(layer)
                pe.wait_ge(a_drained, A_AT[("h", layer, NT - 1, 1)] + 1)
                for h in range(H0):
                    banks = [None] * 5
                    for j in range(NT):
                        n = (layer * H0 + h) * NT + j
                        pe.wait_ge(et_made, n + 1)
                        for t in range(NT):
                            if j == 0 and t % 2 == 0:
                                banks[t // 2] = fill("V", ("acc", layer, h, t // 2))
                            o = banks[t // 2][0:T, (t % 2) * (C0 + 1):(t % 2 + 1) * (C0 + 1)]
                            last = mm(o, ET4[n % 4][0:T, t * T:(t + 1) * T], HN4[0:T, j, h, :],
                                      j == 0 and t % 2 == 0, j == NT - 1, share=True)
                            if j == NT - 1 and t % 2 == 1:
                                last.then_inc(v_filled, 1)
                        if j < NT - 1:
                            last.then_inc(et_used, 1)
                        if j in (3, 5) and h + 1 < H0:
                            rows(layer, h + 1, [j // 4])

            def rows(layer, h, parts=range(2)):
                for i in parts:
                    column_rows(("p", layer, h, i), (P1C, P2C)[i][:, h, :])

            def gat1(layer):
                gat_front(layer)
                pe.wait_ge(a_drained, A_AT[("h", layer, NT - 1, 1)] + 1)
                for g in range(5):
                    pe.wait_ge(et_made, 80 + (layer - 2) * 5 + g + 1)
                    for tt in range(2):
                        for p in range(2):
                            b = fill("V", ("acc", layer, g, 2 * tt + p))
                            n = HALF + p
                            for j in range(NT):
                                last = mm(b[0:T, 0:n], ET1[g % 2][0:T, j, tt * T:(tt + 1) * T],
                                          HN1[0:T, j, p * HALF:p * HALF + n], j == 0, j == NT - 1)
                            last.then_inc(v_filled, 1)

            gat4(0)
            pe.wait_ge(v_drained, V_AT[("acc", 0, H0 - 1, 4)] + 1)
            turn("gat0", Y, lambda t: None)
            turned("gat0")
            gat4(1)
            turn("lnf", Y, lambda t: pe.wait_ge(tile_normed, t + 1))

            pe.wait_ge(pooled, 1)
            pe.wait_ge(rw_loaded, 32)
            b = fill("V", ("logits",))
            for k in range(KD):
                last = mm(b[:, 0:4], POOLC[:, k:k + 1].to_broadcast([128, 128]), RW0[:, k, :], k == 0, k == KD - 1)
            last.then_inc(v_filled, 1)
            for u in range(11):
                if u < 10:
                    e, c = divmod(u, 5)
                    for i in range(6):
                        if c == 0:
                            pe.wait_ge(f1_first[i] if e == 0 else f1_loaded[e], 16)
                        b = fill("A", ("f1", u, i))
                        for j in range(2):
                            m = 2 * i + j
                            for k in range(KD):
                                last = mm(b[:, j * 250:(j + 1) * 250], W1[:, k, m * 128:(m + 1) * 128],
                                          XT[:, k, c * 250:(c + 1) * 250], k == 0, k == KD - 1)
                        last.then_inc(a_filled, 1)
                if u > 0:
                    e, c = divmod(u - 1, 5)
                    pe.wait_ge(f2_loaded[e], 16)
                    pe.wait_ge(act_made, u)
                    for i in range(4):
                        tt, half = divmod(i, 2)
                        b = fill("V", ("f2", u - 1, i))
                        for m in range(HM):
                            last = mm(b[0:T, 0:HALF], HB[(u - 1) % 2][:, m, tt * T:(tt + 1) * T],
                                      W2[:, m, half * HALF:(half + 1) * HALF], m == 0, m == HM - 1)
                        last.then_inc(v_filled, 1)

            def q1(c):
                n0, n = CH[c]
                for m in range(KD):
                    b = fill("A", ("q1", m, c))
                    for k in range(KD):
                        last = mm(b[:, 0:n], WQ[:, k, m * 128:(m + 1) * 128], XT[:, k, n0:n0 + n], k == 0, k == KD - 1)
                    last.then_inc(a_filled, 1)

            turn("ln1", Y, lambda t: pe.wait_ge(pair_normed, t + 1), (0,))
            turned("ln1", 0)
            pe.wait_ge(m1w[0], 16)
            q1(0)
            turn("ln1", Y, lambda t: pe.wait_ge(pair_normed, t + 1), (1, 2))
            turned("ln1")
            q1(1)
            q1(2)
            pe.wait_ge(m1w[1], 16)
            for t in range(NT):
                for half in range(2):
                    natural_product("V", ("k1", t, half), WF[1], HALF, XT, n0=half * HALF, tile=t)
            pe.wait_ge(m1w[2], 16)
            for t in range(NT):
                for half in range(2):
                    natural_product("V", ("v1", t, half), WF[0], HALF, XT, n0=half * HALF, tile=t)
            pe.wait_ge(te_used, 18 + 20)
            pe.wait_ge(kvb_zero, 2)
            pe.wait_ge(v_drained, V_AT[("v1", NT - 1, 1)] + 1)
            for i in range(2):
                b = fill("V", ("kv1", i))
                for j in range(3):
                    m = 3 * i + j
                    for t in range(NT):
                        last = mm(b[:, j * 129:(j + 1) * 129], K1[0:T, t, m * 128:(m + 1) * 128], V1[0:T, t, m, :],
                                  t == 0, t == NT - 1)
                last.then_inc(v_filled, 1)
            pe.wait_ge(v_drained, V_AT[("kv1", 1)] + 1)
            for t in range(NT):
                for i in range(2):
                    b = fill("V", ("n1", t, i))
                    for j in range(3):
                        m = 3 * i + j
                        last = mm(b[0:T, j * 130:(j + 1) * 130], QT1[:, m, t * T:(t + 1) * T], KVB[:, m, :], True, True)
                    last.then_inc(v_filled, 1)
            for t in range(NT):
                turn_group_of(t, "mix1", K1, lambda t: pe.wait_ge(v_drained, V_AT[("n1", t, 1)] + 1))
                if t == 0:
                    pe.wait_ge(m1w[3], 16)
                for half in range(2):
                    natural_product("V", ("proj1", t, half), WF[1], HALF, AT, n0=half * HALF, tile=t)
            gat1(2)
            pe.wait_ge(v_drained, V_AT[("acc", 2, 4, 3)] + 1)
            turn("gat1", Y, lambda t: None)
            turned("gat1")
            gat1(3)
            def up1(c):
                pe.wait_ge(gw1_loaded, 16)
                for i in range(4):
                    b = fill("A", ("g1", c, i))
                    for j in range(2):
                        e = 2 * i + j
                        for k in range(KD):
                            last = mm(b[:, j * 250:(j + 1) * 250], GW1[:, k, e * I1:(e + 1) * I1],
                                      XT[:, k, c * 250:(c + 1) * 250], k == 0, k == KD - 1)
                    last.then_inc(a_filled, 1)

            turn("lng", Y, lambda t: pe.wait_ge(tile_normed, 10 + t + 1), (0, 1))
            turned("lng", 0)
            up1(0)
            turn("lng", Y, lambda t: pe.wait_ge(tile_normed, 10 + t + 1), (2,))
            turned("lng")
            pe.wait_ge(grw_loaded, 16)
            b = fill("V", ("router",))
            for t in range(NT):
                for k in range(KD):
                    last = mm(b[0:T, t * E1:(t + 1) * E1], XT[:, k, t * T:(t + 1) * T], RWT[:, k, :], k == 0, k == KD - 1)
            last.then_inc(v_filled, 1)
            up1(1)
            pe.wait_ge(rp_made, 1)
            b = fill("V", ("imp",))
            for t in range(NT):
                last = mm(b[:, 0:E1], ONES[0:T, 0:1].to_broadcast([T, 128]), PR[0:T, t, :], t == 0, t == NT - 1)
            last.then_inc(v_filled, 1)
            for c in range(6):
                if 1 < c < 5:
                    up1(c)
                if c < 5:
                    pe.wait_ge(gates_made, 1)
                    for i in range(4):
                        b = fill("V", ("gb", c, i))
                        for j in range(2):
                            e = 2 * i + j
                            for tt in range(2):
                                last = pe.transpose(b[:, j * 250 + tt * T:j * 250 + (tt + 1) * T],
                                                    GG[0:T, 2 * c + tt, e:e + 1].to_broadcast([T, 128]), IDENT[0:T, 0:T])
                        last.then_inc(v_filled, 1)
                if c > 0:
                    pe.wait_ge(v_drained, V_AT[("gb", c - 1, 3)] + 1)
                    pe.wait_ge(gw2_loaded, 16)
                    for i in range(4):
                        tt, half = divmod(i, 2)
                        b = fill("V", ("g2", c - 1, i))
                        for e in range(E1):
                            last = mm(b[0:T, 0:HALF], GA[(c - 1) % 2][:, e, tt * T:(tt + 1) * T],
                                      GW2[:, e, half * HALF:(half + 1) * HALF], e == 0, e == E1 - 1)
                        last.then_inc(v_filled, 1)
            assert count == {"V": len(V_LIST), "A": len(A_LIST)}

        @block.scalar
        def _(act):
            count = [0]
            own = [0]

            def bank(name):
                i = A_AT[name]
                assert i == count[0], (name, i, count[0])
                count[0] += 1
                return BANKS_A[i % ABANKS]

            def turn(stage, into, bias=None, groups=range(3)):
                for g in groups:
                    t0, n = TG[g]
                    for k in range(KD):
                        act.wait_ge(a_filled, A_AT[("tr", stage, g, k)] + 1)
                        b = bank(("tr", stage, g, k))
                        o, i = into[:, k, t0 * T:(t0 + n) * T], b[:, 0:n * T]
                        if bias is None:
                            act.activation(o, i, ACT.Copy).then_inc(a_drained, 1)
                        else:
                            act.activation(o, i, ACT.Relu, bias=bias[:, k:k + 1]).then_inc(a_drained, 1)

            def deviation(stage, g):
                t0, n = TG[g]
                act.wait_ge(stats_made, 3 * stage + g + 1)
                act.activation(STD[0:T, t0:t0 + n], VAR[0:T, t0:t0 + n], ACT.Sqrt).then_inc(std_made, 1)

            def normalise(stage, g):
                t0, n = TG[g]
                act.wait_ge(scale_made, 3 * (stage - 1) + g + 1)
                for t in range(t0, t0 + n):
                    if t % 2 == 0:
                        act.wait_ge(y_stored[t // 2], 16 * stage)
                    act.activation(Y[0:T, t, :], Y[0:T, t, :], ACT.Identity, scale=RSTD[0:T, t:t + 1],
                                   bias=NMR[0:T, t:t + 1]).then_inc(tile_normed, 1)

            def pair_deviation(i):
                act.wait_ge(pair_stats, i + 1)
                s = slice(2 * (i // 2), 2 * (i // 2) + 2)
                act.activation(STD[0:T, s], VAR[0:T, s], ACT.Sqrt).then_inc(pair_std, 1)

            for g in range(3):
                deviation(0, g)
            turn("ln0", XT)

            def squares(h):
                for i, x in enumerate("qk"):
                    for c, (n0, n) in enumerate(CH):
                        act.wait_ge(v_drained, V_AT[(x, h, c)] + 1)
                        src, dst = ((QT, Q2), (KT, K2))[i]
                        act.activation(dst[0:MD, n0:n0 + n], src[0:MD, n0:n0 + n], ACT.Square).then_inc(squares_made, 1)

            squares(0)
            for h in range(MH):
                act.wait_ge(a_filled, A_AT[("kn", h)] + 1)
                b = bank(("kn", h))
                act.activation(KN[0:T, :], b[0:T, 0:NT], ACT.Copy).then_inc(a_drained, 1)
                for c, (n0, n) in enumerate(CH):
                    act.wait_ge(a_filled, A_AT[("qn", h, c)] + 1)
                    b = bank(("qn", h, c))
                    act.activation(QT[MD:MD + 1, n0:n0 + n], b[MD:MD + 1, 0:n], ACT.Copy).then_inc(a_drained, 1)
                act.wait_ge(a_drained, A_AT[("kn", h)] + 1)
                for i in range(5):
                    act.wait_ge(a_filled, A_AT[("pk", h, i)] + 1)
                    b = bank(("pk", h, i))
                    for j in range(2):
                        t = 2 * i + j
                        last = act.activation(PK[0:T, t, :], b[0:T, j * RF:(j + 1) * RF], ACT.Exp, bias=KN[0:T, t:t + 1])
                    last.then_inc(a_drained, 1)
                for m in range(2):
                    for c, (n0, n) in enumerate(CH):
                        act.wait_ge(a_filled, A_AT[("pq", h, m, c)] + 1)
                        b = bank(("pq", h, m, c))
                        act.activation(PQ[:, m, n0:n0 + n], b[:, 0:n], ACT.Exp).then_inc(a_drained, 1)
                if h + 1 < MH:
                    squares(h + 1)
            turn("mix0", AT)

            def rows(layer, h, parts=range(2)):
                for i in parts:
                    for q, (t0, n) in enumerate(TG):
                        act.wait_ge(a_filled, A_AT[("p", layer, h, i, q)] + 1)
                        b = bank(("p", layer, h, i, q))
                        act.activation(PROW[h % 2][i][:, t0 * T:(t0 + n) * T], b[:, 0:n * T],
                                       ACT.Copy).then_inc(a_drained, 1)

            def step4(layer, i):
                h, j = divmod(i, NT)
                n = layer * H0 * NT + i
                act.wait_ge(a_drained, A_AT[("p", layer, h, 1, 2)] + 1)
                m = n - 4
                if m >= 0:
                    ml, mh, mj = m // (H0 * NT), m // NT % H0, m % NT
                    if mj < NT - 1:
                        act.wait_ge(et_used, (ml * H0 + mh) * (NT - 1) + mj + 1)
                    else:
                        act.wait_ge(v_filled, V_AT[("acc", ml, mh, 4)] + 1)
                act.activation(ET4[n % 4][0:T, :], PROW[h % 2][0][0:T, :], ACT.Exp, bias=ASC[0:T, h, j:j + 1])
                if n >= 2:
                    act.wait_ge(larger_made, n - 1)
                act.activation(E24[n % 2][0:T, :], PROW[h % 2][1][0:T, :], ACT.Exp,
                               bias=AS2[0:T, h, j:j + 1]).then_inc(slopes_made, 1)
                if j in (7, 9) and h + 1 < H0:
                    rows(layer, h + 1, [j // 8])

            def step1(layer, i):
                n = 80 + (layer - 2) * 5 + i
                act.wait_ge(a_drained, A_AT[("p", layer, 0, 1, 2)] + 1)
                if i >= 2:
                    act.wait_ge(v_filled, V_AT[("acc", layer, i - 2, 3)] + 1)
                cols = slice(i * 250, (i + 1) * 250)
                for j in range(NT):
                    act.activation(ET1[i % 2][0:T, j, :], PROW[0][0][0:T, cols], ACT.Exp, bias=ASC[0:T, 0, j:j + 1])
                act.wait_ge(larger_made, n)
                for j in range(NT):
                    last = act.activation(E21[0:T, j, :], PROW[0][1][0:T, cols], ACT.Exp, bias=AS2[0:T, 0, j:j + 1])
                last.then_inc(slopes_made, 1)

            def gat(layer):
                heads = H0 if layer < 2 else 1
                step = step4 if layer < 2 else step1
                act.wait_ge(h_ones, 1 + layer // 2)
                if layer == 2:
                    for k in range(2):
                        act.wait_ge(slot_stored[k], 240)
                done = 0
                for what, i in front(layer):
                    if what == "h":
                        t, half = i
                        act.wait_ge(a_filled, A_AT[("h", layer, t, half)] + 1)
                        b = bank(("h", layer, t, half))
                        if heads > 1:
                            o = HN4[0:T, t, 2 * half:2 * half + 2, 0:C0]
                            v = b[0:T, 0:HALF].rearrange("p (a b) -> p a b", a=2)
                        else:
                            o = HN1[0:T, t, half * HALF:(half + 1) * HALF]
                            v = b[0:T, 0:HALF]
                            if half == 0:
                                act.activation(SC2[0:T, :, 0, t], b[0:T, 0:2], ACT.Copy)
                                v = b[0:T, 2:HALF + 2]
                        act.activation(o, v, ACT.Copy).then_inc(a_drained, 1)
                    elif what == "asrow":
                        if i > 1:
                            act.wait_ge(max_done, layer * H0 + i - 1)
                        for q, (t0, n) in enumerate(TG):
                            act.wait_ge(a_filled, A_AT[("asrow", layer, i, q)] + 1)
                            b = bank(("asrow", layer, i, q))
                            act.activation(ASROW[i % 2][:, t0 * T:(t0 + n) * T], b[:, 0:n * T],
                                           ACT.Copy).then_inc(a_drained, 1)
                    elif what == "rows":
                        rows(layer, i)
                    else:
                        step(layer, i)
                        done = i + 1
                for i in range(done, H0 * NT if layer < 2 else 5):
                    step(layer, i)
                    if layer == 3 and i == 4:
                        deviation(2, 0)
                if layer == 3:
                    normalise(2, 0)
                    deviation(2, 1)
                    normalise(2, 1)

            gat(0)
            act.wait_ge(grow_loaded[0], 48)
            turn("gat0", XT, BC[0])
            gat(1)
            for g in range(2):
                deviation(1, g)
                normalise(1, g)
            turn("lnf", XT, groups=(0,))
            deviation(1, 2)
            normalise(1, 2)
            turn("lnf", XT, groups=(1, 2))
            act.wait_ge(routed, 1)
            act.activation(GATE[:, 1:2], LV[:, 1:2], ACT.Exp).then_inc(gate_exp, 1)

            for u in range(10):
                e = u // 5
                act.wait_ge(b1_loaded, 32)

                def expo(i):
                    act.wait_ge(clamped, 6 * u + i + 1)
                    act.activation(EB[:, 2 * i:2 * i + 2, :], TB[:, 2 * i:2 * i + 2, :], ACT.Exp).then_inc(expd, 1)

                for i in range(6):
                    act.wait_ge(a_filled, A_AT[("f1", u, i)] + 1)
                    b = bank(("f1", u, i))
                    for j in range(2):
                        m = 2 * i + j
                        last = act.activation(HB[u % 2][:, m, :], b[:, j * 250:(j + 1) * 250], ACT.Identity,
                                              bias=B1C[:, e, m:m + 1])
                    last.then_inc(a_drained, 1)
                    if i > 0:
                        expo(i - 1)
                expo(5)
                act.wait_ge(t_made, u + 1)
                act.activation(EB, HB[u % 2], ACT.Gelu).then_inc(gelu_made, 1)
                if u >= 7:
                    pair_deviation(2 * (u - 7) + 1)
                if u >= 6:
                    pair_deviation(2 * (u - 6))
            pair_deviation(7)
            turn("ln1", XT, groups=(0,))
            pair_deviation(8)
            act.wait_ge(m1_small, 64)
            act.activation(NBQ1, BQ1, ACT.Copy, scale=-1.0).then_inc(act_step, 1)
            own[0] += 1
            act.wait_ge(act_step, own[0])
            n_te = 0
            for c, (n0, n) in enumerate(CH):
                if c == 1:
                    turn("ln1", XT, groups=(1, 2))
                for m in range(KD):
                    if (c, m) == (0, 2):
                        pair_deviation(9)
                    act.wait_ge(a_filled, A_AT[("q1", m, c)] + 1)
                    b = bank(("q1", m, c))
                    if n_te >= 2:
                        act.wait_ge(te_used, n_te - 1)
                    e = TE[n_te % 2][:, 0:n]
                    act.activation(e, b[:, 0:n], ACT.Relu, scale=-1.0, bias=NBQ1[:, m:m + 1]).then_inc(act_step, 1)
                    own[0] += 1
                    act.activation(TR[n_te % 2][:, 0:n], b[:, 0:n], ACT.Relu, bias=BQ1[:, m:m + 1]).then_inc(a_drained, 1)
                    act.wait_ge(act_step, own[0])
                    act.activation(e, e, ACT.Exp, scale=-1.0).then_inc(te_made, 1)
                    n_te += 1
            for t in range(NT):
                for half in range(2):
                    act.wait_ge(v_drained, V_AT[("k1", t, half)] + 1)
                    act.wait_ge(te_used, n_te - 1)
                    e = TE[n_te % 2][0:T, 0:HALF]
                    act.activation(e, K1[0:T, t, half * HALF:(half + 1) * HALF], ACT.Relu, scale=-1.0).then_inc(act_step, 1)
                    own[0] += 1
                    act.wait_ge(act_step, own[0])
                    act.activation(e, e, ACT.Exp, scale=-1.0).then_inc(te_made, 1)
                    n_te += 1
            turn("mix1", AT)
            gat(2)
            act.wait_ge(grow_loaded[2], 48)
            turn("gat1", XT, BC[1])
            gat(3)
            turn("lng", XT, groups=(0,))
            deviation(2, 2)
            normalise(2, 2)
            turn("lng", XT, groups=(1,))

            def up1(c):
                for i in range(4):
                    act.wait_ge(a_filled, A_AT[("g1", c, i)] + 1)
                    b = bank(("g1", c, i))
                    act.activation(GA[c % 2][:, 2 * i:2 * i + 2, :], b[:, 0:500].rearrange("p (a b) -> p a b", a=2),
                                           ACT.Silu).then_inc(a_drained, 1)

            up1(0)
            turn("lng", XT, groups=(2,))
            act.wait_ge(rl_made, 1)
            act.activation(PE_[0:T], PR[0:T], ACT.Exp).then_inc(re_made, 1)
            for c in range(1, 5):
                up1(c)
            assert count[0] == len(A_LIST)


        @block.vector
        def _(dve):
            count = [0]
            own = [0]

            def bank(name):
                i = V_AT[name]
                assert i == count[0], (name, i, count[0])
                count[0] += 1
                return BANKS_V[i % VBANKS]

            def step(ins):
                ins.then_inc(dve_step, 1)
                own[0] += 1
                return own[0]

            def after(n):
                if n > 0:
                    dve.wait_ge(dve_step, n)

            def now(ins):
                after(step(ins))

            def stats(t, src):
                s = STATS[0:T, t % 2]
                for i in range(2):
                    n = step(dve.bn_stats(s[:, i, :], src[:, i * HALF:(i + 1) * HALF]))
                after(n)
                return step(dve.bn_aggr(MV[0:T, t, :], s.rearrange("p a b -> p (a b)")))

            def variance(made, t0, n):
                after(own[0])
                dve.tensor_scalar(VAR[0:T, t0:t0 + n], MV[0:T, t0:t0 + n, 1], LN_EPS, None, ALU.add).then_inc(made, 1)

            def scale(stage, g):
                t0, n = TG[g]
                dve.wait_ge(std_made, 3 * stage + g + 1)
                s = slice(t0, t0 + n)
                now(dve.reciprocal(RSTD[0:T, s], STD[0:T, s]))
                dve.scalar_tensor_tensor(NMR[0:T, s], MV[0:T, s, 0], -1.0, RSTD[0:T, s], ALU.mult,
                                         ALU.mult).then_inc(scale_made, 1)

            def normalise(o, src, t):
                return dve.tensor_scalar(o, src, MV[0:T, t, 0:1], RSTD[0:T, t:t + 1], ALU.subtract, ALU.mult)

            dve.memset(RFT[MD:MD + 1, :], 1.0).then_inc(norm_row_made, 1)

            def normalise_x(g):
                t0, n = TG[g]
                dve.wait_ge(std_made, g + 1)
                now(dve.reciprocal(RSTD[0:T, t0:t0 + n], STD[0:T, t0:t0 + n]))
                for t in range(t0, t0 + n):
                    normalise(Y[0:T, t, :], Y[0:T, t, :], t).then_inc(x_normed, 1)

            for t in range(NT):
                if t % 2 == 0:
                    dve.wait_ge(x_loaded[t // 2], 16)
                stats(t, Y[0:T, t, :])
                if t in (3, 7, 9):
                    variance(stats_made, *TG[t // 4])
                if t in (5, 9):
                    normalise_x(t // 8)
            normalise_x(2)

            dve.wait_ge(edges_loaded, 32)
            dve.wait_ge(consts_made, NCONST)
            step(dve.tensor_copy(SRCF[0:T], SRCI[0:T]))
            step(dve.tensor_copy(TRASH[0:T], TRASHI[0:T]))
            now(dve.tensor_copy(DSTF[0:T], DSTI[0:T]))
            dve.scalar_tensor_tensor(KEY[0:T], SRCF[0:T], float(N), DSTF[0:T], ALU.mult, ALU.add).then_inc(keys_made, 1)
            dve.wait_ge(keys_made, 1)

            scratch = [0, 0]
            keys = list(range(NKEY))
            batch = [0]

            def key_group():
                i = keys.pop(0)
                dve.wait_ge(v_filled, V_AT[("key", i)] + 1)
                b = bank(("key", i))
                for j in range(min(KEYG, EC - i * KEYG)):
                    c = i * KEYG + j
                    row = b[0:T, j * T:(j + 1) * T]
                    after(scratch[c % 2])
                    step(dve.tensor_scalar(EQ[c % 2][0:T], row, KEY[0:T, c:c + 1], 0.0, ALU.is_equal, ALU.add,
                                           accum_out=COUNT[0:T, c:c + 1]))
                    ins = dve.scalar_tensor_tensor(EQL[c % 2][0:T], row, KEY[0:T, c:c + 1], LOWER[0:T], ALU.is_equal,
                                                   ALU.mult, accum_out=SEEN[0:T, c:c + 1])
                    if j < KEYG - 1 and c < EC - 1:
                        scratch[c % 2] = step(ins)
                    else:
                        ins.then_inc(v_drained, 1)
                        dve.wait_ge(v_drained, V_AT[("key", i)] + 1)
                        scratch[c % 2] = own[0]
                if i % 5 == 4 or i == NKEY - 1:
                    c0, c1 = batch[0], min((i + 1) * KEYG, EC)
                    batch[0] = c1
                    s = lambda x: x[0:T, c0:c1]
                    step(dve.tensor_scalar(s(FIRSTF), s(SEEN), 1.0, None, ALU.min))
                    now(dve.tensor_scalar(s(IDXE), s(KEY), -1.0, TRASH[0:T, 0:1], ALU.mult, ALU.add))
                    now(dve.tensor_tensor(s(IDXE), s(IDXE), s(FIRSTF), ALU.mult))
                    now(dve.tensor_tensor(s(IDXE), s(IDXE), s(KEY), ALU.add))
                    dve.tensor_copy(s(IDX_I), s(IDXE)).then_inc(index_made, 1)

            dve.wait_ge(m0_small, 64)
            for t in range(NT):
                for half in range(2):
                    dve.wait_ge(v_filled, V_AT[("v", t, half)] + 1)
                    b = bank(("v", t, half))
                    dve.tensor_tensor(V0[0:T, t, 4 * half:4 * half + 4, 0:MD],
                                              b[0:T, 0:HALF].rearrange("p (a b) -> p a b", a=4),
                                              ROW[0][0:T, half * HALF:(half + 1) * HALF].rearrange("p (a b) -> p a b", a=4),
                                              ALU.add).then_inc(v_drained, 1)
                    for _ in range(2):
                        if keys:
                            key_group()
            while keys:
                key_group()

            def qk(h):
                for i, x in enumerate("qk"):
                    for c, (n0, n) in enumerate(CH):
                        dve.wait_ge(v_filled, V_AT[(x, h, c)] + 1)
                        b = bank((x, h, c))
                        dve.tensor_scalar((QT, KT)[i][0:MD, n0:n0 + n], b[0:MD, 0:n], QKB[0:MD, i, h:h + 1],
                                                  float(MD) ** -0.5, ALU.add, ALU.mult).then_inc(v_drained, 1)

            qk(0)
            for h in range(MH):
                dve.wait_ge(v_filled, V_AT[("kv", h)] + 1)
                b = bank(("kv", h))
                dve.tensor_copy(KV0, b[:, 0:194].rearrange("p (a b) -> p a b", a=2)).then_inc(v_drained, 1)
                if h + 1 < MH:
                    qk(h + 1)
                for i in range(2):
                    dve.wait_ge(v_filled, V_AT[("num", h, i)] + 1)
                    b = bank(("num", h, i))
                    v = b[0:T, 0:485].rearrange("p (a b) -> p a b", a=5)
                    r = RS[0:T, 5 * i:5 * i + 5]
                    now(dve.tensor_scalar(r, v[:, :, MD], 1e-6, None, ALU.max))
                    now(dve.reciprocal(r, r))
                    dve.tensor_tensor(Y[0:T, 5 * i:5 * i + 5, h * MD:(h + 1) * MD], v[:, :, 0:MD],
                                              r.unsqueeze(2).to_broadcast([T, 5, MD]), ALU.mult).then_inc(v_drained, 1)

            slots_used = [0]

            def slot(slots):
                n = slots_used[0]
                slots_used[0] += 1
                dve.wait_ge(slot_loaded[n % 2], 16 * (n // 2 + 1))
                return slots[n % 2][0:T]

            def score_weights(layer, blocks):
                heads = H0 if layer < 2 else 1
                a_s, a_d = (ROW[2], ROW[3], ROW[0], ROW[1], ROW[0], ROW[4], ROW[1], ROW[2])[2 * layer:2 * layer + 2]
                weight = (WG0, W, WS[:, :, 2:], WS[:, :, 2:])[layer]
                width = D // heads
                dve.wait_ge(grow_loaded[layer], 32 if layer == 1 else 48)
                dve.wait_ge(gw_loaded[layer], 16)
                for k in blocks:
                    for h in range(heads):
                        for i, row in enumerate((a_s, a_d)):
                            cols = slice(h * width, (h + 1) * width)
                            after(tok[i])
                            ins = dve.tensor_tensor_reduce(WA_PART[layer][i], weight[:, k, cols], row[:, cols], 1.0, 0.0,
                                                           ALU.mult, ALU.add,
                                                           WA[:, k, i, h:h + 1] if layer < 2 else WS[:, k, i:i + 1])
                            if (k, h, i) == (KD - 1, heads - 1, 1):
                                ins.then_inc(wa_made, 1)
                            else:
                                tok[i] = step(ins)

            tok = [0, 0]

            def project(name, slots, bias, between, before=lambda t: None):
                for t in range(NT):
                    before(t)
                    s = slot(slots)
                    now(dve.tensor_tensor(s, s, bias[0:T], ALU.add))
                    for half in range(2):
                        dve.wait_ge(v_filled, V_AT[(name, t, half)] + 1)
                        b = bank((name, t, half))
                        o = s[:, half * HALF:(half + 1) * HALF]
                        dve.tensor_tensor(o, b[0:T, 0:HALF], o, ALU.add).then_inc(v_drained, 1)
                    dve.wait_ge(v_drained, count[0])
                    dve.engine_nop().then_inc(slot_done, 1)
                    between(t)

            def count_sum(j):
                dve.wait_ge(count_loaded[j % 2], 32 * (j // 2 + 1))
                c, c2 = CS[j % 2][0][0:T], CS[j % 2][1][0:T]
                now(dve.tensor_tensor(c, c, c2, ALU.add))
                own_block = c[:, j * T:(j + 1) * T]
                dve.tensor_tensor(own_block, own_block, IDENT[0:T, 0:T], ALU.add).then_inc(count_summed, 1)

            def mask(j):
                dve.wait_ge(count_summed, j + 1)
                step(dve.tensor_copy(CT[0:T, j, :], CS[j % 2][0][0:T]))
                for g, (t0, n) in enumerate(TG):
                    dve.wait_ge(v_filled, V_AT[("mask", j, g)] + 1)
                    b = bank(("mask", j, g))
                    dve.tensor_scalar(NEG[0:T, t0:t0 + n, j * T:(j + 1) * T],
                                              b[0:T, 0:n * T].rearrange("p (a b) -> p a b", a=n),
                                              0.0, NEG_BIG, ALU.is_equal, ALU.mult).then_inc(v_drained, 1)
                if 3 <= j < 3 + KD:
                    score_weights(0, [j - 3])

            dve.wait_ge(gatb_loaded, 16)
            now(dve.tensor_tensor(ROW[1][0:T], ROW[1][0:T], ROW[5][0:T], ALU.add))
            project("proj", SLOT_M, ROW[1], mask, count_sum)
            after(own[0])
            for k in range(2):
                dve.wait_ge(slot_stored[k], 80)

            def gat_front(layer):
                heads = H0 if layer < 2 else 1
                hs = slice(0, heads)
                if layer < 2:
                    dve.wait_ge(v_filled, V_AT[("sc", layer)] + 1)
                    b = bank(("sc", layer))
                    v = b[0:T, 0:2 * heads * NT].rearrange("p (t a h) -> p a h t", t=NT, a=2)
                    step(dve.tensor_copy(ADC[0:T, hs], v[:, 1]))
                    dve.tensor_copy(ASC[0:T, hs], v[:, 0]).then_inc(v_drained, 1)
                    dve.wait_ge(v_drained, count[0])
                else:
                    dve.wait_ge(a_drained, A_AT[("h", layer, NT - 1, 0)] + 1)
                dve.tensor_scalar(AS2[0:T, hs], ASC[0:T, hs], SLOPE, None, ALU.mult).then_inc(as_made, 1)
                n = 0
                for h in range(heads):
                    dve.wait_ge(a_drained, A_AT[("asrow", layer, h, 2)] + 1)
                    for t in range(NT):
                        if layer > 0 and h == 0 and t % 2 == 0:
                            dve.wait_ge(neg_loaded[t // 2], 16 * layer)
                        after(tok[n % 2])
                        ins = dve.tensor_tensor_reduce(E24[n % 2][0:T, :], NEG[0:T, t, :], ASROW[h % 2][0:T, :], 1.0, -3e38,
                                                       ALU.add, ALU.max, MX[0:T, h, t:t + 1])
                        if t < NT - 1:
                            tok[n % 2] = step(ins)
                        else:
                            ins.then_inc(max_done, 1)
                            heads_done[0] += 1
                            dve.wait_ge(max_done, heads_done[0])
                            tok[n % 2] = own[0]
                        n += 1
                after(own[0])
                now(dve.tensor_tensor(EM[0:T, hs], ADC[0:T, hs], MX[0:T, hs], ALU.add))
                now(dve.scalar_tensor_tensor(EM[0:T, hs], EM[0:T, hs], SLOPE, EM[0:T, hs], ALU.mult, ALU.max))
                now(dve.tensor_tensor(P1C[0:T, hs], ADC[0:T, hs], EM[0:T, hs], ALU.subtract))
                dve.scalar_tensor_tensor(P2C[0:T, hs], ADC[0:T, hs], SLOPE, EM[0:T, hs], ALU.mult,
                                         ALU.subtract).then_inc(p_made, 1)

            heads_done = [0]

            def gat4(layer):
                gat_front(layer)
                dve.wait_ge(mask_saved, 32)

                def drain_head(h):
                    for k in range(5):
                        dve.wait_ge(v_filled, V_AT[("acc", layer, h, k)] + 1)
                        b = bank(("acc", layer, h, k))
                        v = b[0:T, 0:2 * (C0 + 1)].rearrange("p (a b) -> p a b", a=2)
                        r = RS[0:T, 2 * k:2 * k + 2]
                        now(dve.reciprocal(r, v[:, :, C0]))
                        cols = slice(h * C0, (h + 1) * C0)
                        if layer == 0:
                            dve.tensor_tensor(Y[0:T, 2 * k:2 * k + 2, cols], v[:, :, 0:C0],
                                              r.unsqueeze(2).to_broadcast([T, 2, C0]), ALU.mult).then_inc(v_drained, 1)
                            continue
                        if h == 0:
                            dve.wait_ge(y_loaded[k], 16)
                        for i in range(2):
                            t = 2 * k + i
                            last = dve.scalar_tensor_tensor(Y[0:T, t, cols], v[:, i, 0:C0], r[:, i:i + 1], Y[0:T, t, cols],
                                                            ALU.mult, ALU.add)
                            if i == 0:
                                step(last)
                        last.then_inc(v_drained, 1)
                        if h < H0 - 1:
                            continue
                        dve.wait_ge(v_drained, count[0])
                        after(own[0])
                        if h == H0 - 1:
                            for i in range(2):
                                step(dve.bn_stats(STATS4[0:T, 2 * k + i, h, :], Y[0:T, 2 * k + i, cols]))
                            after(own[0])
                            for i in range(2):
                                t = 2 * k + i
                                step(dve.bn_aggr(MV[0:T, t, :], STATS4[0:T, t].rearrange("p a b -> p (a b)")))
                            if k in (1, 3, 4):
                                variance(stats_made, *TG[k // 2])
                            if k in (2, 4):
                                scale(1, k // 2 - 1)
                    if layer == 1 and h == H0 - 1:
                        scale(1, 2)

                for i in range(H0 * NT):
                    n = layer * H0 * NT + i
                    h, j = divmod(i, NT)
                    et = ET4[n % 4][0:T]
                    dve.wait_ge(slopes_made, n + 1)
                    dve.tensor_tensor(et, et, E24[n % 2][0:T], ALU.max).then_inc(larger_made, 1)
                    dve.wait_ge(larger_made, n + 1)
                    dve.scalar_tensor_tensor(et, et, 1.0, CT[0:T, j, :], ALU.min, ALU.mult).then_inc(et_made, 1)
                    if h > 0 and j == 1:
                        drain_head(h - 1)
                    if layer == 1 and h > 0 and 3 <= j < 8:
                        dve.wait_ge(v_drained, V_AT[("acc", layer, h - 1, 4)] + 1)
                        after(own[0])
                        for t in (2 * j - 6, 2 * j - 5):
                            step(dve.bn_stats(STATS4[0:T, t, h - 1, :], Y[0:T, t, (h - 1) * C0:h * C0]))
                    if layer == 0 and 13 <= i < 13 + KD:
                        score_weights(1, [i - 13])
                drain_head(H0 - 1)

            def gat1(layer):
                gat_front(layer)

                def larger(n, g):
                    dve.wait_ge(slopes_made, n + 1)
                    dve.tensor_tensor(ET1[g % 2][0:T], ET1[g % 2][0:T], E21[0:T], ALU.max).then_inc(larger_made, 1)

                def drain_group(g):
                    for tt in range(2):
                        t = 2 * g + tt
                        dve.wait_ge(v_filled, V_AT[("acc", layer, g, 2 * tt)] + 1)
                        b0 = bank(("acc", layer, g, 2 * tt))
                        dve.wait_ge(v_filled, V_AT[("acc", layer, g, 2 * tt + 1)] + 1)
                        b1 = bank(("acc", layer, g, 2 * tt + 1))
                        r = RS[0:T, 2 * tt:2 * tt + 1]
                        now(dve.reciprocal(r, b1[0:T, HALF:HALF + 1]))
                        for p, b in enumerate((b0, b1)):
                            o = Y[0:T, t, p * HALF:(p + 1) * HALF]
                            if layer == 2:
                                dve.tensor_scalar(o, b[0:T, 0:HALF], r, None, ALU.mult).then_inc(v_drained, 1)
                                continue
                            dve.wait_ge(y_loaded[g], 32)
                            dve.scalar_tensor_tensor(o, b[0:T, 0:HALF], r, o, ALU.mult, ALU.add).then_inc(v_drained, 1)
                        if layer == 3:
                            dve.wait_ge(v_drained, count[0])
                            stats(t, Y[0:T, t, :])
                            if t in (3, 7, 9):
                                variance(stats_made, *TG[t // 4])
                            if t in (5, 7):
                                scale(2, t // 6)
                    if layer == 3 and g == 4:
                        scale(2, 2)

                if layer == 2:
                    dve.wait_ge(ct_loaded, 16)
                for g in range(6):
                    n = 80 + (layer - 2) * 5 + g
                    if g > 0:
                        dve.wait_ge(larger_made, n)
                        et = ET1[(g - 1) % 2][0:T]
                        dve.scalar_tensor_tensor(et, et, 1.0, CT[0:T, :, (g - 1) * 250:g * 250], ALU.min,
                                                 ALU.mult).then_inc(et_made, 1)
                    if g > 1:
                        drain_group(g - 2)
                    if g < 5:
                        larger(n, g)
                    if layer == 2 and g == 2:
                        score_weights(3, range(KD))
                drain_group(4)

            gat4(0)
            gat4(1)

            for g, (n0, n) in enumerate(CH):
                dve.wait_ge(a_drained, A_AT[("tr", "lnf", g, KD - 1)] + 1)
                step(dve.tensor_reduce(POOL3[:, :, g], XT[:, :, n0:n0 + n], AX, ALU.add))
            after(own[0])
            now(dve.tensor_reduce(POOLC[:, :], POOL3, AX, ALU.add))
            dve.tensor_scalar(POOLC[:, :], POOLC[:, :], 1.0 / N, None, ALU.mult).then_inc(pooled, 1)
            dve.wait_ge(v_filled, V_AT[("logits",)] + 1)
            b = bank(("logits",))
            dve.wait_ge(rw_loaded, 32)
            dve.tensor_tensor(LG[:, :], b[:, 0:4], RB[:, :], ALU.add).then_inc(v_drained, 1)
            dve.wait_ge(v_drained, count[0])
            by_j = LG[:, :].unsqueeze(1).to_broadcast([128, 4, 4])
            by_i = LG[:, :].unsqueeze(2).to_broadcast([128, 4, 4])
            step(dve.tensor_tensor(CMP, by_j, by_i, ALU.is_gt))
            now(dve.tensor_tensor(CMP2, by_j, by_i, ALU.is_equal))
            now(dve.tensor_tensor(CMP2, CMP2, LT4, ALU.mult))
            now(dve.tensor_tensor(CMP, CMP, CMP2, ALU.add))
            now(dve.tensor_reduce(RANK[:, :], CMP, AX, ALU.add))
            for s in range(2):
                step(dve.tensor_scalar(SEL[:, s, :], RANK[:, :], float(s), None, ALU.is_equal))
            after(own[0])
            for s in range(2):
                step(dve.tensor_tensor(TMP4[:, s, :], SEL[:, s, :], IOTA4[:, :], ALU.mult))
                step(dve.tensor_tensor(IS[:, s, :], SEL[:, s, :], LG[:, :], ALU.mult))
            after(own[0])
            now(dve.tensor_reduce(IDXF[:, :], TMP4, AX, ALU.add))
            dve.tensor_copy(IDXI, IDXF).then_inc(idx_made, 1)
            now(dve.tensor_reduce(LV[:, :], IS, AX, ALU.add))
            dve.tensor_tensor(LV[:, 1:2], LV[:, 1:2], LV[:, 0:1], ALU.subtract).then_inc(routed, 1)
            KO, MISH, CC, NCK, KG = (CO[:, 2 * i:2 * i + 2] for i in range(5))
            step(dve.tensor_scalar(KO, IDXF, 1.0, None, ALU.is_equal))
            now(dve.tensor_scalar(MISH, IDXF, 2.0, None, ALU.is_equal))
            now(dve.tensor_tensor(KO, KO, MISH, ALU.add))
            step(dve.tensor_scalar(CC, MISH, 1.0, None, ALU.add))
            step(dve.tensor_scalar(KG, KO, -1.0, 1.0, ALU.mult, ALU.add))
            after(own[0])
            now(dve.scalar_tensor_tensor(NCK, CC, -1.0, KO, ALU.mult, ALU.mult))
            dve.wait_ge(gate_exp, 1)
            now(dve.tensor_scalar(GATE[:, 0:1], GATE[:, 1:2], 1.0, None, ALU.add))
            now(dve.reciprocal(GATE[:, 0:1], GATE[:, 0:1]))
            now(dve.tensor_tensor(GATE[:, 1:2], GATE[:, 1:2], GATE[:, 0:1], ALU.mult))

            def clamp(u, i):
                dve.wait_ge(a_drained, A_AT[("f1", u, i)] + 1)
                s = slice(2 * i, 2 * i + 2)
                dve.tensor_scalar(TB[:, s, :], HB[u % 2][:, s, :], 30.0, None, ALU.min).then_inc(clamped, 1)

            def ratio(u, i):
                e = u // 5
                dve.wait_ge(expd, 6 * u + i + 1)
                s = slice(2 * i, 2 * i + 2)
                t_, x, h = TB[:, s, :], EB[:, s, :], HB[u % 2][:, s, :]
                c = lambda k: k[:, e:e + 1]
                now(dve.tensor_scalar(t_, x, c(MISH), c(CC), ALU.mult, ALU.add))
                ins = dve.tensor_tensor(t_, t_, x, ALU.mult)
                if i == 5:
                    ins.then_inc(t_made, 1)
                    dve.wait_ge(t_made, u + 1)
                else:
                    now(ins)
                now(dve.tensor_scalar(t_, t_, c(CC), None, ALU.add))
                now(dve.reciprocal(t_, t_))
                now(dve.scalar_tensor_tensor(t_, t_, c(NCK), h, ALU.mult, ALU.mult))
                now(dve.scalar_tensor_tensor(t_, h, c(KO), t_, ALU.mult, ALU.add))

            def pair_output(c):
                dve.wait_ge(v_drained, count[0])
                for t in (2 * c, 2 * c + 1):
                    stats(t, Y[0:T, t, :])
                variance(pair_stats, 2 * c, 2)

            pair_slots = [None, None]

            def pair_residual(c):
                s = slice(2 * c, 2 * c + 2)
                dve.wait_ge(pair_std, 2 * c + 1)
                now(dve.reciprocal(RSTD[0:T, s], STD[0:T, s]))
                y = [Y[0:T, t, :] for t in (2 * c, 2 * c + 1)]
                for i in range(2):
                    step(normalise(y[i], y[i], 2 * c + i))
                at = own[0]
                for row, op in ((ROW[4], ALU.mult), (ROW[0], ALU.add)):
                    for i in range(2):
                        after(at - 1 + i)
                        step(dve.tensor_tensor(y[i], y[i], row[0:T], op))
                    at = own[0]
                for i in range(2):
                    pair_slots[i] = slot(SLOT_F)
                    after(at - 1 + i)
                    dve.tensor_tensor(pair_slots[i], y[i], pair_slots[i], ALU.add).then_inc(slot_done, 1)
                dve.wait_ge(slot_done, slots_used[0])
                for i in range(2):
                    stats(2 * c + i, pair_slots[i])
                variance(pair_stats, 2 * c, 2)

            def pair_next(c):
                s = slice(2 * c, 2 * c + 2)
                dve.wait_ge(pair_std, 2 * c + 2)
                now(dve.reciprocal(RSTD[0:T, s], STD[0:T, s]))
                for i in range(2):
                    t = 2 * c + i
                    normalise(Y[0:T, t, :], pair_slots[i], t).then_inc(pair_normed, 1)

            def last_bias():
                dve.wait_ge(frow_loaded, 64)
                now(dve.tensor_scalar(ROW[5][0:T], ROW[2][0:T], GATE[0:T, 0:1], None, ALU.mult))
                now(dve.scalar_tensor_tensor(ROW[5][0:T], ROW[3][0:T], GATE[0:T, 1:2], ROW[5][0:T], ALU.mult, ALU.add))
                for t in range(NT):
                    step(dve.tensor_tensor(Y[0:T, t, :], Y[0:T, t, :], ROW[5][0:T], ALU.add))

            for u in range(11):
                if u < 10:
                    e = u // 5
                    for i in range(6):
                        clamp(u, i)
                        if i > 0:
                            ratio(u, i - 1)
                    ratio(u, 5)
                    dve.wait_ge(gelu_made, u + 1)
                    dve.scalar_tensor_tensor(HB[u % 2], EB, KG[:, e:e + 1], TB, ALU.mult, ALU.add).then_inc(act_made, 1)
                    dve.wait_ge(act_made, u + 1)
                if u == 0:
                    last_bias()
                if u >= 7:
                    pair_residual(u - 7)
                if u == 10:
                    pair_next(3)
                if u > 0:
                    e, c = divmod(u - 1, 5)
                    for i in range(4):
                        tt, half = divmod(i, 2)
                        dve.wait_ge(v_filled, V_AT[("f2", u - 1, i)] + 1)
                        b = bank(("f2", u - 1, i))
                        o = Y[0:T, 2 * c + tt, half * HALF:(half + 1) * HALF]
                        dve.scalar_tensor_tensor(o, b[0:T, 0:HALF], GATE[0:T, e:e + 1], o, ALU.mult, ALU.add).then_inc(v_drained, 1)
                if u >= 6:
                    pair_output(u - 6)
                if 7 <= u < 10:
                    pair_next(u - 7)
            pair_residual(4)
            pair_next(4)

            dve.wait_ge(m1_small, 64)
            n_te = 0
            for c, (n0, n) in enumerate(CH):
                for m in range(KD):
                    dve.wait_ge(te_made, n_te + 1)
                    dve.tensor_tensor(QT1[:, m, n0:n0 + n], TE[n_te % 2][:, 0:n], TR[n_te % 2][:, 0:n],
                                      ALU.add).then_inc(te_used, 1)
                    n_te += 1
            for t in range(NT):
                for half in range(2):
                    cols = slice(half * HALF, (half + 1) * HALF)
                    dve.wait_ge(v_filled, V_AT[("k1", t, half)] + 1)
                    b = bank(("k1", t, half))
                    dve.tensor_tensor(K1[0:T, t, cols], b[0:T, 0:HALF], ROW[2][0:T, cols], ALU.add).then_inc(v_drained, 1)
                    dve.wait_ge(v_drained, count[0])
                    dve.wait_ge(te_made, n_te + 1)
                    e_ = TE[n_te % 2][0:T, 0:HALF]
                    k_ = K1[0:T, t, cols]
                    dve.scalar_tensor_tensor(k_, k_, 0.0, e_, ALU.max, ALU.add).then_inc(te_used, 1)
                    n_te += 1
            for k in range(2):
                dve.wait_ge(slot_stored[k], 160)
            for t in range(NT):
                for half in range(2):
                    dve.wait_ge(v_filled, V_AT[("v1", t, half)] + 1)
                    b = bank(("v1", t, half))
                    dve.tensor_tensor(V1[0:T, t, 3 * half:3 * half + 3, 0:128],
                                              b[0:T, 0:HALF].rearrange("p (a b) -> p a b", a=3),
                                              ROW[3][0:T, half * HALF:(half + 1) * HALF].rearrange("p (a b) -> p a b", a=3),
                                              ALU.add).then_inc(v_drained, 1)
            dve.wait_ge(kvb_zero, 2)
            for i in range(2):
                dve.wait_ge(v_filled, V_AT[("kv1", i)] + 1)
                b = bank(("kv1", i))
                v = b[:, 0:387].rearrange("p (a b) -> p a b", a=3)
                for s in range(2):
                    p = slice(64 * s, 64 * s + 64)
                    step(dve.tensor_copy(KVB[p, 3 * i:3 * i + 3, 64 * s:64 * s + 64], v[p, :, 64 * s:64 * s + 64]))
                    last = dve.tensor_copy(KVB[p, 3 * i:3 * i + 3, 128 + s:129 + s], v[p, :, 128:129])
                    if s == 0:
                        step(last)
                last.then_inc(v_drained, 1)
            for t in range(NT):
                for i in range(2):
                    dve.wait_ge(v_filled, V_AT[("n1", t, i)] + 1)
                    b = bank(("n1", t, i))
                    v = b[0:T, 0:390].rearrange("p (a b) -> p a b", a=3)
                    RZ = RZ2[:, i]
                    now(dve.reciprocal(RZ[0:T], v[:, :, 128:130]))
                    for s in range(2):
                        last = dve.tensor_tensor(
                            K1[0:T, t, 384 * i:384 * (i + 1)].rearrange("p (a b) -> p a b", a=3)[:, :, 64 * s:64 * s + 64],
                            v[:, :, 64 * s:64 * s + 64], RZ[0:T, :, s:s + 1].to_broadcast([T, 3, 64]), ALU.mult)
                        if s == 0:
                            step(last)
                    last.then_inc(v_drained, 1)
            dve.wait_ge(grow_loaded[3], 16)
            now(dve.tensor_tensor(ROW[1][0:T], ROW[1][0:T], ROW[5][0:T], ALU.add))
            project("proj1", SLOT_1, ROW[1], lambda t: score_weights(2, range(KD)) if t == 4 else None)
            gat1(2)
            gat1(3)

            dve.wait_ge(v_filled, V_AT[("router",)] + 1)
            b = bank(("router",))
            v = b[0:T, 0:NT * E1].rearrange("p (a b) -> p a b", a=NT)
            wide = lambda x: x[0:T].unsqueeze(2).to_broadcast([T, NT, E1])
            now(dve.tensor_reduce(RMX[0:T], v, AX, ALU.max))
            dve.tensor_tensor(PR[0:T], v, wide(RMX), ALU.subtract).then_inc(v_drained, 1)
            dve.wait_ge(v_drained, count[0])
            dve.engine_nop().then_inc(rl_made, 1)
            dve.wait_ge(re_made, 1)
            now(dve.tensor_reduce(RMX[0:T], PE_[0:T], AX, ALU.add))
            now(dve.reciprocal(RMX[0:T], RMX[0:T]))
            dve.tensor_tensor(PR[0:T], PE_[0:T], wide(RMX), ALU.mult).then_inc(rp_made, 1)
            dve.wait_ge(rp_made, 1)
            dve.wait_ge(lt8_made, 2)
            by_j = PR[0:T].unsqueeze(2).to_broadcast([T, NT, E1, E1])
            by_i = PR[0:T].unsqueeze(3).to_broadcast([T, NT, E1, E1])
            step(dve.tensor_tensor(CM8[0:T], by_j, by_i, ALU.is_gt))
            now(dve.tensor_tensor(CM8B[0:T], by_j, by_i, ALU.is_equal))
            now(dve.tensor_tensor(CM8B[0:T], CM8B[0:T], LT8[0:T].unsqueeze(1).to_broadcast([T, NT, E1, E1]), ALU.mult))
            now(dve.tensor_tensor(CM8[0:T], CM8[0:T], CM8B[0:T], ALU.add))
            now(dve.tensor_reduce(MASK1[0:T], CM8[0:T], AX, ALU.add))
            now(dve.tensor_scalar(MASK1[0:T], MASK1[0:T], 2.0, None, ALU.is_lt))
            now(dve.tensor_tensor(MASK1[0:T], MASK1[0:T], PR[0:T], ALU.mult))
            dve.wait_ge(v_filled, V_AT[("imp",)] + 1)
            b = bank(("imp",))
            dve.tensor_scalar(RUN, b[:, 0:E1], 0.1, 0.91, ALU.mult, ALU.add).then_inc(v_drained, 1)
            dve.wait_ge(v_drained, count[0])
            now(dve.reciprocal(RUN, RUN))
            now(dve.tensor_tensor(GG[0:T], MASK1[0:T], RUN[0:T].unsqueeze(1).to_broadcast([T, NT, E1]), ALU.mult))
            now(dve.tensor_reduce(RMX[0:T], GG[0:T], AX, ALU.add))
            now(dve.reciprocal(RMX[0:T], RMX[0:T]))
            dve.tensor_tensor(GG[0:T], GG[0:T], wide(RMX), ALU.mult).then_inc(gates_made, 1)

            for c in range(6):
                if c < 5:
                    for i in range(4):
                        dve.wait_ge(a_drained, A_AT[("g1", c, i)] + 1)
                        dve.wait_ge(v_filled, V_AT[("gb", c, i)] + 1)
                        b = bank(("gb", c, i))
                        o = GA[c % 2][:, 2 * i:2 * i + 2, :]
                        dve.tensor_tensor(o, o, b[:, 0:500].rearrange("p (a b) -> p a b", a=2), ALU.mult).then_inc(v_drained, 1)
                if c > 0:
                    for i in range(4):
                        tt, half = divmod(i, 2)
                        dve.wait_ge(v_filled, V_AT[("g2", c - 1, i)] + 1)
                        b = bank(("g2", c - 1, i))
                        if half == 0:
                            s = slot(SLOT_2)
                        o = s[:, half * HALF:(half + 1) * HALF]
                        dve.tensor_tensor(o, b[0:T, 0:HALF], o, ALU.add).then_inc(v_drained, 1)
                        if half == 1:
                            dve.wait_ge(v_drained, count[0])
                            dve.engine_nop().then_inc(slot_done, 1)
            assert count[0] == len(V_LIST)

        @block.gpsimd
        def _(pool):
            made = [0]

            def const(ins):
                ins.then_inc(consts_made, 1)
                made[0] += 1

            pool.memset(ZERO, 0.0).then_inc(zeros_made, 1)
            const(pool.memset(IDENT, 0.0))
            const(pool.memset(LOWER, 1.0))
            const(pool.memset(LT4, 1.0))
            const(pool.memset(ONES, 1.0))
            const(pool.memset(HALVES, -0.5))
            for i in range(4):
                const(pool.memset(IOTA4[:, i:i + 1], float(i)))
            const(pool.iota(TRASHI, pattern=[[0, 1]], base=N * N, channel_multiplier=1))
            pool.wait_ge(consts_made, 3)
            const(pool.affine_select(out=IDENT, in_=IDENT, compare_op=ALU.not_equal, fill=1.0, base=0,
                                     pattern=[[-1, 128]], channel_multiplier=1))
            const(pool.affine_select(out=LOWER, in_=LOWER, compare_op=ALU.is_gt, fill=0.0, base=0,
                                     pattern=[[-1, T]], channel_multiplier=1))
            const(pool.affine_select(out=LT4, in_=LT4, compare_op=ALU.is_gt, fill=0.0, base=0,
                                     pattern=[[1, 4], [-1, 4]], channel_multiplier=0))
            const(pool.memset(RS, 0.0))
            const(pool.memset(RS2, 0.0))
            assert made[0] == NCONST, made
            pool.memset(V0[0:T, :, :, MD:MD + 1], 1.0).then_inc(v_ones, 1)
            pool.wait_ge(zeros_written, 64)
            for c in range(EC):
                k = c % 2
                if c % (5 * KEYG) == 0:
                    pool.wait_ge(index_made, c // (5 * KEYG) + 1)
                if c >= 2:
                    pool.wait_ge(added[k], 16 * (c // 2))
                pool.indirect_dma_start(counts[k], bass.IndirectOffsetOnAxis(ap=IDX_I[0:T, c:c + 1].bitcast(U32), axis=0),
                                        COUNT[0:T, c:c + 1], None, compute_op=ALU.add).then_inc(added[k], 16)
            pool.wait_ge(v_filled, V_AT[("proj", NT - 1, 1)] + 1)
            pool.memset(HN4[0:T, :, :, C0:C0 + 1], 1.0).then_inc(h_ones, 1)
            pool.wait_ge(a_filled, A_AT[("q1", KD - 1, 2)] + 1)
            for k in range(2):
                pool.wait_ge(slot_stored[k], 160)
            pool.memset(V1[0:T, :, :, 128:129], 1.0).then_inc(kvb_zero, 1)
            pool.memset(KVB, 0.0).then_inc(kvb_zero, 1)
            pool.wait_ge(v_filled, V_AT[("proj1", NT - 1, 1)] + 1)
            pool.memset(HN1[0:T, :, D:D + 1], 1.0).then_inc(h_ones, 1)
            pool.wait_ge(et_made, 90)
            pool.memset(LT8, 1.0).then_inc(lt8_made, 1)
            pool.wait_ge(lt8_made, 1)
            pool.affine_select(out=LT8, in_=LT8, compare_op=ALU.is_gt, fill=0.0, base=0,
                               pattern=[[1, E1], [-1, E1]], channel_multiplier=0).then_inc(lt8_made, 1)

        @block.sync
        def _(sp):
            def load(o, i, s):
                sp.dma_start(o, i).then_inc(s, 16)

            def row_load(k, name, s):
                load(ROW[k], w[name].to_broadcast([128, D]), s)

            def vf(name):
                sp.wait_ge(v_filled, V_AT[name] + 1)

            def af(name):
                sp.wait_ge(a_filled, A_AT[name] + 1)

            x = w["x"]
            for i in range(5):
                load(Y[0:T, 2 * i:2 * i + 2, :], x[250 * i:250 * (i + 1), :].rearrange("(a p) d -> p a d", a=2), x_loaded[i])
            load(SRCI[0:T], w["src"], edges_loaded)
            load(DSTI[0:T], w["dst"], edges_loaded)
            load(W, w["mix0_wv"], wv_loaded)
            load(RFT[0:MD], w["mix0_rf"], m0_small)
            load(QKB[0:MD], w["mix0_qkb"], m0_small)
            row_load(0, "mix0_bv", m0_small)
            row_load(1, "mix0_bp", m0_small)
            for h in range(2):
                load(QKW[h], w["mix0_qk"][h], qkw_loaded[h])
            sp.wait_ge(zeros_made, 1)
            for k in range(2):
                load(counts[k][0:N * N, :].rearrange("(p c n) o -> p c (n o)", p=T, c=NT),
                     ZERO[0:T].unsqueeze(1).to_broadcast([T, NT, N]), zeros_written)
                load(counts[k][N * N:CNT, :], ZERO[0:T, 0:1], zeros_written)
            load(RW0, w["ffn0_rw"], rw_loaded)
            load(RB, w["ffn0_rb"].to_broadcast([128, 4]), rw_loaded)
            row_load(2, "gat0_as", grow_loaded[0])
            row_load(3, "gat0_ad", grow_loaded[0])
            load(BC[0], w["gat0_bc"], grow_loaded[0])
            row_load(5, "gat1_b", gatb_loaded)
            vf(("v", NT - 1, 1))
            load(W, w["mix0_wp"], wp_loaded)
            for h in range(2, MH):
                vf(("k", h - 2, 2))
                load(QKW[h % 2], w["mix0_qk"][h], qkw_loaded[h % 2])

            loads = [0, 0]
            stores = [0, 0]

            def residual(n_pass, src, slots, dst, beside=lambda t: None, reused=lambda t: None):
                def get(t):
                    n = n_pass * NT + t
                    load(slots[n % 2][0:T], src[t * T:(t + 1) * T, :], slot_loaded[n % 2])

                get(0)
                get(1)
                beside(0)
                beside(1)
                for t in range(NT):
                    n = n_pass * NT + t
                    sp.wait_ge(slot_done, n + 1)
                    o = dst[t * T:(t + 1) * T, :]
                    load(o, slots[n % 2][0:T], slot_stored[n % 2])
                    stores[n % 2] += 16
                    if t + 2 < NT:
                        sp.wait_ge(slot_stored[n % 2], stores[n % 2])
                        reused(t)
                        get(t + 2)
                        beside(t + 2)
                for k in range(2):
                    sp.wait_ge(slot_stored[k], stores[k])

            def tiles_load(src):
                for i in range(5):
                    load(Y[0:T, 2 * i:2 * i + 2, :], src[250 * i:250 * (i + 1), :].rearrange("(a p) d -> p a d", a=2),
                         y_loaded[i])

            def tiles_store(dst, i):
                load(dst[250 * i:250 * (i + 1), :].rearrange("(a p) d -> p a d", a=2), Y[0:T, 2 * i:2 * i + 2, :],
                     y_stored[i])

            vf(("num", MH - 1, 1))
            load(WG0, w["gat0_w"], gw_loaded[0])
            for k in range(2):
                sp.wait_ge(added[k], 16 * (EC // 2))

            def count_load(j):
                if j >= 2:
                    vf(("mask", j - 2, 2))
                    sp.wait_ge(v_drained, V_AT[("mask", j - 2, 0)] + 1)
                if j < NT:
                    for k in range(2):
                        load(CS[j % 2][k][0:T], counts[k][j * T * N:(j + 1) * T * N, :].rearrange("(p n) o -> p (n o)", p=T),
                             count_loaded[j % 2])

            residual(0, x, SLOT_M, res[XMID0], count_load)
            load(W, w["gat1_w"], gw_loaded[1])
            row_load(0, "gat1_as", grow_loaded[1])
            row_load(1, "gat1_ad", grow_loaded[1])
            sp.wait_ge(v_drained, V_AT[("mask", NT - 1, 2)] + 1)
            load(ct_dram, CT[0:T].rearrange("p a b -> p (a b)"), mask_saved)
            load(neg_dram, NEG[0:T].rearrange("p a b -> p (a b)"), mask_saved)
            sp.wait_ge(mask_saved, 32)

            def mask_load(stage, pieces=range(5)):
                for i in pieces:
                    if i % 2 == 0:
                        af(("tr", stage, i // 2, KD - 1))
                    load(NEG[0:T, 2 * i:2 * i + 2, :].rearrange("p a b -> p (a b)"), neg_dram[:, 2 * i * N:(2 * i + 2) * N],
                         neg_loaded[i])

            mask_load("gat0")
            row_load(4, "ffn0_g", frow_loaded)
            sp.wait_ge(wa_made, 2)
            row_load(0, "ffn0_b", frow_loaded)
            sp.wait_ge(max_done, 2 * H0)
            tiles_load(res[XMID0])
            for i in range(5):
                sp.wait_ge(v_drained, V_AT[("acc", 1, H0 - 1, i)] + 1)
                tiles_store(res[X1], i)
            for i in range(5):
                sp.wait_ge(y_stored[i], 16)

            sp.wait_ge(idx_made, 1)
            chosen = [sp.value_load(IDXI[0:1, s:s + 1], min_val=0, max_val=3) for s in range(2)]
            for s in range(2):
                load(B1C[:, s, :], w["ffn0_b1"][bass.DynSlice(chosen[s], 1)].rearrange("e p n -> (e p) n"), b1_loaded)
            for s in range(2):
                load(ROW[2 + s], w["ffn0_b2"][bass.DynSlice(chosen[s], 1), :].to_broadcast([128, D]), frow_loaded)
            for i in range(6):
                m = slice(256 * i, 256 * (i + 1))
                load(W1[:, :, m], w["ffn0_w1"][bass.DynSlice(chosen[0], 1)].rearrange(
                    "e p (k n) -> (e p) k n", k=KD)[:, :, m], f1_first[i])
            load(W2.rearrange("p a b -> p (a b)"), w["ffn0_w2"][bass.DynSlice(chosen[0], 1)].rearrange("e p n -> (e p) n"), f2_loaded[0])
            af(("f1", 4, 5))
            load(W1.rearrange("p a b -> p (a b)"), w["ffn0_w1"][bass.DynSlice(chosen[1], 1)].rearrange("e p n -> (e p) n"), f1_loaded[1])
            vf(("f2", 4, 3))
            load(W2.rearrange("p a b -> p (a b)"), w["ffn0_w2"][bass.DynSlice(chosen[1], 1)].rearrange("e p n -> (e p) n"), f2_loaded[1])
            row_load(1, "mix1_bo", m1_small)
            row_load(2, "mix1_bk", m1_small)
            row_load(3, "mix1_bv", m1_small)

            def mixer_load(t):
                if t == 7:
                    sp.wait_ge(act_made, 10)
                    load(WQ, w["mix1_wq"], m1w[0])
                if t == 9:
                    vf(("f2", 9, 3))
                    load(WF[1], w["mix1_wk"], m1w[1])
                    load(BQ1, w["mix1_bq"], m1_small)
                    load(WF[0], w["mix1_wv"], m1w[2])

            residual(1, res[X1], SLOT_F, res[X2], mixer_load, lambda t: sp.wait_ge(pair_normed, t + 1))
            vf(("k1", NT - 1, 1))
            load(WF[1], w["mix1_wo"], m1w[3])
            vf(("n1", NT - 1, 1))
            load(CT[0:T].rearrange("p a b -> p (a b)"), ct_dram, ct_loaded)
            load(WS[:, :, 2:], w["gat2_w"], gw_loaded[2])
            row_load(0, "gat2_as", grow_loaded[2])
            row_load(4, "gat2_ad", grow_loaded[2])
            load(BC[1], w["gat2_bc"], grow_loaded[2])
            row_load(5, "gat3_b", grow_loaded[3])
            residual(2, res[X2], SLOT_1, res[XMID1],
                     lambda t: mask_load("mix1", {0: (0, 1), 7: (2, 3), 9: (4,)}.get(t, ())))
            row_load(1, "gat3_as", grow_loaded[3])
            row_load(2, "gat3_ad", grow_loaded[3])
            af(("h", 2, NT - 1, 1))
            load(WS[:, :, 2:], w["gat3_w"], gw_loaded[3])
            mask_load("gat1")
            sp.wait_ge(max_done, 2 * H0 + 2)
            tiles_load(res[XMID1])
            for i in range(5):
                if i == 3:
                    sp.wait_ge(et_made, 90)
                    load(GW1, w["ffn1_w1"], gw1_loaded)
                    load(RWT, w["ffn1_rw"], grw_loaded)
                sp.wait_ge(v_drained, V_AT[("acc", 3, i, 3)] + 1)
                tiles_store(res[X3], i)
            load(GW2, w["ffn1_w2"], gw2_loaded)
            for i in range(5):
                sp.wait_ge(y_stored[i], 32)
            residual(3, res[X3], SLOT_2, out)


def _inputs(inputs):
    import numpy as np

    g = {k: np.asarray(v) for k, v in inputs.items()}

    def by_rows(m):
        k, n = m.shape
        return m.reshape(k // 128, 128, n).transpose(1, 0, 2)

    def row(v):
        return v.reshape(1, -1)

    qkv, qkv_b = g["L0_mix_qkv_w"], g["L0_mix_qkv_b"]
    qk = qkv[:2 * D].reshape(2, MH, MD, KD, 128)
    out = {
        "x": g["x"],
        "src": g["src"].reshape(T, EC), "dst": g["dst"].reshape(T, EC),
        "mix0_wv": by_rows(qkv[2 * D:].T),
        "mix0_qk": qk.transpose(1, 4, 0, 3, 2),
        "mix0_qkb": qkv_b[:2 * D].reshape(2, MH, MD).transpose(2, 0, 1),
        "mix0_bv": row(qkv_b[2 * D:]), "mix0_bp": row(g["L0_mix_proj_b"]),
        "mix0_wp": by_rows(g["L0_mix_proj_w"].T), "mix0_rf": g["L0_mix_rf"].T,
        "ffn0_rw": by_rows(g["L0_ffn_router_w"].T), "ffn0_rb": row(g["L0_ffn_router_b"]),
        "ffn0_w1": g["L0_ffn_w1"].reshape(4, KD, 128, HID).transpose(0, 2, 1, 3).reshape(4, 128, KD * HID),
        "ffn0_b1": g["L0_ffn_b1"].reshape(4, HM, 128).transpose(0, 2, 1),
        "ffn0_w2": g["L0_ffn_w2"].reshape(4, HM, 128, D).transpose(0, 2, 1, 3).reshape(4, 128, HM * D),
        "ffn0_b2": g["L0_ffn_b2"], "ffn0_g": row(g["L0_ffn_ln_g"]), "ffn0_b": row(g["L0_ffn_ln_b"]),
        "mix1_wq": by_rows(g["L1_mix_Wq"]), "mix1_wk": by_rows(g["L1_mix_Wk"]), "mix1_wv": by_rows(g["L1_mix_Wv"]),
        "mix1_wo": by_rows(g["L1_mix_Wo"]), "mix1_bq": g["L1_mix_bq"].reshape(KD, 128).T,
        "mix1_bk": row(g["L1_mix_bk"]), "mix1_bv": row(g["L1_mix_bv"]), "mix1_bo": row(g["L1_mix_bo"]),
        "ffn1_rw": by_rows(g["L1_ffn_router_w"].T),
        "ffn1_w1": by_rows(g["L1_ffn_w1"].reshape(E1 * I1, D).T),
        "ffn1_w2": g["L1_ffn_w2"].transpose(2, 0, 1),
    }
    for i, (layer, n) in enumerate(((0, 1), (0, 2), (1, 1), (1, 2))):
        a = "a" if layer == 0 else "att"
        out[f"gat{i}_w"] = by_rows(g[f"L{layer}_gnn_W{n}"])
        out[f"gat{i}_as"] = row(g[f"L{layer}_gnn_{a}_src{n}"])
        out[f"gat{i}_ad"] = row(g[f"L{layer}_gnn_{a}_dst{n}"])
        out[f"gat{i}_b"] = row(g[f"L{layer}_gnn_b{n}"])
        out[f"gat{i}_bc"] = g[f"L{layer}_gnn_b{n}"].reshape(KD, 128).T
    for k in ("gat0_b", "gat2_b", "gat1_bc", "gat3_bc"):
        del out[k]
    return {k: np.ascontiguousarray(v) for k, v in out.items()}


def kernel(**inputs):
    import concourse.bacc as bacc
    from concourse.bass_utils import run_bass_kernel_spmd

    arrays = _inputs(inputs)
    nc = bacc.Bacc("TRN2", target_bir_lowering=False, num_devices=1)
    w = {k: nc.dram_tensor(f"in_{k}", a.shape, mybir.dt.from_np(a.dtype), kind="ExternalInput").ap()
         for k, a in arrays.items()}
    out = nc.dram_tensor("out_0", (N, D), F32, kind="ExternalOutput").ap()
    gps_kernel(nc, w, out)
    r = run_bass_kernel_spmd(nc, [{f"in_{k}": a for k, a in arrays.items()}], core_ids=[0])
    return r.results[0]["out_0"]
```
